# Optimizing a Trainium2 kernel written in Bass

```python
import numpy as np
import jax
import jax.numpy as jnp

def _softmax(x, axis=-1):
    return jax.nn.softmax(x, axis=axis)

def _gelu(x):
    return jax.nn.gelu(x, approximate=True)

def _silu(x):
    return jax.nn.silu(x)

def _sigmoid(x):
    return jax.nn.sigmoid(x)

def _layernorm(x, axis=-1, eps=1e-05):
    m = jnp.mean(x, axis=axis, keepdims=True)
    v = jnp.var(x, axis=axis, keepdims=True)
    return (x - m) / jnp.sqrt(v + eps)

def _scatter_add(tgt, idx, src, axis=0):
    return tgt.at[idx].add(src)

def _segment_sum(src, seg, n):
    return jax.ops.segment_sum(src, seg, n)
kernel_name = 'mk_perceiver_d1_seqx_r8_4e846d'

def setup_inputs(seed: int=0):
    np.random.seed(seed)
    _w = jnp.asarray

    def _rec_inputs():
        import jax
        import jax.numpy as jnp
        _rk = jax.random.key(seed)
        x = -0.0002928 + 1 * jax.random.normal(jax.random.fold_in(_rk, 1), (4, 128, 128), jnp.float32)
        _lenS = 128 - jax.random.randint(jax.random.fold_in(_rk, 7), (4,), 0, max(1, 128 // 4) + 1, jnp.int32)
        _lenS2 = 2048 - jax.random.randint(jax.random.fold_in(_rk, 8), (4,), 0, max(1, 2048 // 4) + 1, jnp.int32)
        _ctx_1024P = jax.random.normal(jax.random.fold_in(_rk, 11), (4, 16, 128), jnp.float32)
        _ctx_1024c = jax.random.dirichlet(jax.random.fold_in(_rk, 511), 0.3 * jnp.ones((16,), jnp.float32), (4, 2048))
        _ctx_1024t = jnp.einsum('bsk,bkd->bsd', _ctx_1024c, _ctx_1024P)
        _ctx_1024t = _ctx_1024t * jax.lax.rsqrt(jnp.mean(jnp.square(_ctx_1024t)) + 1e-12) * 0.953939
        ctx_1024 = -1.39393e-06 + 0.999914 * (_ctx_1024t + 0.3 * jax.random.normal(jax.random.fold_in(_rk, 611), (4, 2048, 128), jnp.float32))
        fside_BxSxS2_0 = jax.random.uniform(jax.random.fold_in(_rk, 12), (4, 128, 2048), jnp.float32, 0.0, 1)
        _validS = jnp.arange(128)[None, :] < _lenS[:, None]
        _validS2 = jnp.arange(2048)[None, :] < _lenS2[:, None]
        _causal = jnp.tril(jnp.ones((128, 128), dtype=bool))
        mask_BxSxS2_ik1 = jnp.where(jnp.broadcast_to(_validS2[:, None, :], (4, 128, 2048)), 1, 0).astype(jnp.int32)
        return (x, ctx_1024, fside_BxSxS2_0, mask_BxSxS2_ik1)
    x, ctx_1024, fside_BxSxS2_0, mask_BxSxS2_ik1 = _rec_inputs()

    def _L0_xattn_setup():
        import jax, jax.numpy as jnp
        import numpy as np
        NUM_HEADS = 16
        HIDDEN = 128
        B, S = (2, 256)

        def _split_heads(x, H):
            b, s, d = x.shape
            return x.reshape(b, s, H, d // H).transpose(0, 2, 1, 3)
        key = jax.random.key(seed)
        ks = jax.random.split(key, 14)
        D = HIDDEN
        scale = 1.0 / np.sqrt(D)
        inp = {'query': jax.random.normal(ks[0], (B, S, D), jnp.float32), 'key_in': jax.random.normal(ks[1], (B, S, D), jnp.float32), 'value': jax.random.normal(ks[2], (B, S, D), jnp.float32), 'group_prob': jax.random.uniform(ks[3], (B, S, S), jnp.float32), 'mask': jax.random.randint(ks[4], (B, S, S), 0, 2, jnp.int32), 'wq_k': jax.random.normal(ks[5], (D, D), jnp.float32) * scale, 'wq_b': jnp.zeros((D,), jnp.float32), 'wk_k': jax.random.normal(ks[6], (D, D), jnp.float32) * scale, 'wk_b': jnp.zeros((D,), jnp.float32), 'wv_k': jax.random.normal(ks[7], (D, D), jnp.float32) * scale, 'wv_b': jnp.zeros((D,), jnp.float32), 'wo_k': jax.random.normal(ks[8], (D, D), jnp.float32) * scale, 'wo_b': jnp.zeros((D,), jnp.float32)}
        return inp
    _L0_xattn_all = _L0_xattn_setup()
    _L0_xattn_in = {k: v for k, v in _L0_xattn_all.items() if k in ('wq_k', 'wq_b', 'wk_k', 'wk_b', 'wv_k', 'wv_b', 'wo_k', 'wo_b')}
    del _L0_xattn_all

    def _L0_attn_setup():
        import jax, jax.numpy as jnp
        import numpy as np
        B, T, D, H = (2, 256, 128, 4)
        DK, DV = (128, 256)
        HK, HV = (DK // H, DV // H)
        LR = 16
        EPS = 1e-05
        GATE_NORM = 16.0

        def _xavier(k, shape, gain):
            fan_in, fan_out = shape
            lim = gain * np.sqrt(6.0 / (fan_in + fan_out))
            return jax.random.uniform(k, shape, jnp.float32, -lim, lim)

        def _gla_scan(q, k, v, g):
            S0 = jnp.zeros((q.shape[-1], v.shape[-1]), q.dtype)

            def step(S, inp):
                qt, kt, vt, gt = inp
                S = jnp.exp(gt)[:, None] * S + kt[:, None] * vt[None, :]
                return (S, qt @ S)
            return jax.lax.scan(step, S0, (q, k, v, g))[1]

        def _forward(x, Wq, Wk, Wv, Wg, gk_w1, gk_w2, gk_b, Wo, rms_w):
            b, t = (x.shape[0], x.shape[1])
            scale = HK ** (-0.5)
            q = (x @ Wq).reshape(b, t, H, HK).transpose(0, 2, 1, 3) * scale
            k = (x @ Wk).reshape(b, t, H, HK).transpose(0, 2, 1, 3)
            v = (x @ Wv).reshape(b, t, H, HV).transpose(0, 2, 1, 3)
            gl = x @ gk_w1 @ gk_w2 + gk_b
            g = jax.nn.log_sigmoid(gl.astype(jnp.float32)) / GATE_NORM
            g = g.reshape(b, t, H, HK).transpose(0, 2, 1, 3)
            o = jax.vmap(jax.vmap(_gla_scan))(q, k, v, g)
            o = o.transpose(0, 2, 1, 3)
            o = o * jax.lax.rsqrt(jnp.mean(o * o, axis=-1, keepdims=True) + EPS) * rms_w
            o = o.reshape(b, t, DV) * jax.nn.silu(x @ Wg)
            return o @ Wo
        key = jax.random.key(seed)
        ks = jax.random.split(key, 10)
        g_qkv = 2 ** (-2.5)
        return {'x': jax.random.normal(ks[0], (B, T, D), jnp.float32), 'Wq': _xavier(ks[1], (D, DK), g_qkv), 'Wk': _xavier(ks[2], (D, DK), g_qkv), 'Wv': _xavier(ks[3], (D, DV), g_qkv), 'Wg': _xavier(ks[4], (D, DV), g_qkv), 'gk_w1': _xavier(ks[5], (D, LR), g_qkv), 'gk_w2': _xavier(ks[6], (LR, DK), g_qkv), 'gk_b': jnp.zeros((DK,), jnp.float32), 'Wo': _xavier(ks[7], (DV, D), 2 ** (-1)), 'rms_w': jnp.ones((HV,), jnp.float32)}
    _L0_attn_all = _L0_attn_setup()
    _L0_attn_in = {k: v for k, v in _L0_attn_all.items() if k in ('Wq', 'Wk', 'Wv', 'Wg', 'gk_w1', 'gk_w2', 'gk_b', 'Wo', 'rms_w')}
    del _L0_attn_all

    def _L0_ffn_setup():
        import jax, jax.numpy as jnp
        import numpy as np
        B, T = (2, 256)
        D_MODEL, D_HIDDEN = (128, 256)
        N_EXPERTS, TOP_K = (8, 2)
        N_TOKENS = B * T
        CAPACITY = 2 * N_TOKENS * TOP_K // N_EXPERTS
        key = jax.random.key(seed)
        k_x, k_rw, k_w, k_v, k_o = jax.random.split(key, 5)
        x = jax.random.normal(k_x, (B, T, D_MODEL), jnp.float32)
        router_w = jax.random.normal(k_rw, (N_EXPERTS, D_MODEL), jnp.float32) * D_MODEL ** (-0.5)
        router_b = jnp.zeros((N_EXPERTS,), jnp.float32)
        W = jax.random.normal(k_w, (N_EXPERTS, D_MODEL, D_HIDDEN), jnp.float32) * D_MODEL ** (-0.5)
        V = jax.random.normal(k_v, (N_EXPERTS, D_MODEL, D_HIDDEN), jnp.float32) * D_MODEL ** (-0.5)
        W_out = jax.random.normal(k_o, (N_EXPERTS, D_HIDDEN, D_MODEL), jnp.float32) * D_HIDDEN ** (-0.5)
        return {'x': x, 'router_w': router_w, 'router_b': router_b, 'W': W, 'V': V, 'W_out': W_out}
    _L0_ffn_all = _L0_ffn_setup()
    _L0_ffn_in = {k: v for k, v in _L0_ffn_all.items() if k in ('router_w', 'router_b', 'W', 'V', 'W_out')}
    del _L0_ffn_all
    return {'x': x, 'ctx_1024': ctx_1024, 'fside_BxSxS2_0': fside_BxSxS2_0, 'mask_BxSxS2_ik1': mask_BxSxS2_ik1, 'L0_xattn_wq_k': _L0_xattn_in['wq_k'], 'L0_xattn_wq_b': _L0_xattn_in['wq_b'], 'L0_xattn_wk_k': _L0_xattn_in['wk_k'], 'L0_xattn_wk_b': _L0_xattn_in['wk_b'], 'L0_xattn_wv_k': _L0_xattn_in['wv_k'], 'L0_xattn_wv_b': _L0_xattn_in['wv_b'], 'L0_xattn_wo_k': _L0_xattn_in['wo_k'], 'L0_xattn_wo_b': _L0_xattn_in['wo_b'], 'L0_attn_Wq': _L0_attn_in['Wq'], 'L0_attn_Wk': _L0_attn_in['Wk'], 'L0_attn_Wv': _L0_attn_in['Wv'], 'L0_attn_Wg': _L0_attn_in['Wg'], 'L0_attn_gk_w1': _L0_attn_in['gk_w1'], 'L0_attn_gk_w2': _L0_attn_in['gk_w2'], 'L0_attn_gk_b': _L0_attn_in['gk_b'], 'L0_attn_Wo': _L0_attn_in['Wo'], 'L0_attn_rms_w': _L0_attn_in['rms_w'], 'L0_ffn_router_w': _L0_ffn_in['router_w'], 'L0_ffn_router_b': _L0_ffn_in['router_b'], 'L0_ffn_W': _L0_ffn_in['W'], 'L0_ffn_V': _L0_ffn_in['V'], 'L0_ffn_W_out': _L0_ffn_in['W_out']}

def reference(x, ctx_1024, fside_BxSxS2_0, mask_BxSxS2_ik1, L0_xattn_wq_k, L0_xattn_wq_b, L0_xattn_wk_k, L0_xattn_wk_b, L0_xattn_wv_k, L0_xattn_wv_b, L0_xattn_wo_k, L0_xattn_wo_b, L0_attn_Wq, L0_attn_Wk, L0_attn_Wv, L0_attn_Wg, L0_attn_gk_w1, L0_attn_gk_w2, L0_attn_gk_b, L0_attn_Wo, L0_attn_rms_w, L0_ffn_router_w, L0_ffn_router_b, L0_ffn_W, L0_ffn_V, L0_ffn_W_out):
    import jax
    import jax.numpy as jnp

    def _L0_xattn_ref(query, key_in, value, group_prob, mask, wq_k, wq_b, wk_k, wk_b, wv_k, wv_b, wo_k, wo_b):
        import jax, jax.numpy as jnp
        import numpy as np
        NUM_HEADS = 16
        HIDDEN = 128
        B, S = (2, 256)

        def _split_heads(x, H):
            b, s, d = x.shape
            return x.reshape(b, s, H, d // H).transpose(0, 2, 1, 3)
        H = NUM_HEADS
        dh = query.shape[-1] // H
        q = _split_heads(query @ wq_k + wq_b, H)
        k = _split_heads(key_in @ wk_k + wk_b, H)
        v = _split_heads(value @ wv_k + wv_b, H)
        logits = jnp.einsum('bhqd,bhkd->bhqk', q, k) / jnp.sqrt(jnp.asarray(dh, q.dtype))
        neg = (1.0 - mask.astype(q.dtype)) * -1000000000.0
        logits = logits + neg[:, None, :, :]
        attn = jax.nn.softmax(logits, axis=-1)
        attn = attn * group_prob[:, None, :, :]
        out = jnp.einsum('bhqk,bhkd->bhqd', attn, v)
        out = out.transpose(0, 2, 1, 3).reshape(query.shape[0], -1, H * dh)
        return out @ wo_k + wo_b

    def _L0_attn_ref(x, Wq, Wk, Wv, Wg, gk_w1, gk_w2, gk_b, Wo, rms_w):
        import jax, jax.numpy as jnp
        import numpy as np
        B, T, D, H = (2, 256, 128, 4)
        DK, DV = (128, 256)
        HK, HV = (DK // H, DV // H)
        LR = 16
        EPS = 1e-05
        GATE_NORM = 16.0

        def _xavier(k, shape, gain):
            fan_in, fan_out = shape
            lim = gain * np.sqrt(6.0 / (fan_in + fan_out))
            return jax.random.uniform(k, shape, jnp.float32, -lim, lim)

        def _gla_scan(q, k, v, g):
            S0 = jnp.zeros((q.shape[-1], v.shape[-1]), q.dtype)

            def step(S, inp):
                qt, kt, vt, gt = inp
                S = jnp.exp(gt)[:, None] * S + kt[:, None] * vt[None, :]
                return (S, qt @ S)
            return jax.lax.scan(step, S0, (q, k, v, g))[1]

        def _forward(x, Wq, Wk, Wv, Wg, gk_w1, gk_w2, gk_b, Wo, rms_w):
            b, t = (x.shape[0], x.shape[1])
            scale = HK ** (-0.5)
            q = (x @ Wq).reshape(b, t, H, HK).transpose(0, 2, 1, 3) * scale
            k = (x @ Wk).reshape(b, t, H, HK).transpose(0, 2, 1, 3)
            v = (x @ Wv).reshape(b, t, H, HV).transpose(0, 2, 1, 3)
            gl = x @ gk_w1 @ gk_w2 + gk_b
            g = jax.nn.log_sigmoid(gl.astype(jnp.float32)) / GATE_NORM
            g = g.reshape(b, t, H, HK).transpose(0, 2, 1, 3)
            o = jax.vmap(jax.vmap(_gla_scan))(q, k, v, g)
            o = o.transpose(0, 2, 1, 3)
            o = o * jax.lax.rsqrt(jnp.mean(o * o, axis=-1, keepdims=True) + EPS) * rms_w
            o = o.reshape(b, t, DV) * jax.nn.silu(x @ Wg)
            return o @ Wo
        return _forward(x, Wq, Wk, Wv, Wg, gk_w1, gk_w2, gk_b, Wo, rms_w)

    def _L0_ffn_ref(x, router_w, router_b, W, V, W_out):
        import jax, jax.numpy as jnp
        import numpy as np
        B, T = (2, 256)
        D_MODEL, D_HIDDEN = (128, 256)
        N_EXPERTS, TOP_K = (8, 2)
        N_TOKENS = B * T
        CAPACITY = 2 * N_TOKENS * TOP_K // N_EXPERTS
        Bq, Tq, D = x.shape
        N = Bq * Tq
        x_flat = x.reshape(N, D)
        router_logits = x_flat @ router_w.T + router_b
        top_vals, top_ids = jax.lax.top_k(router_logits, TOP_K)
        top_probs = jax.nn.softmax(top_vals, axis=-1)
        x_pad = jnp.concatenate([x_flat, jnp.zeros((1, D), x_flat.dtype)], axis=0)
        probs_pad = jnp.concatenate([top_probs, jnp.zeros((1, TOP_K), top_probs.dtype)], axis=0)
        out = jnp.zeros((N + 1, D), x_flat.dtype)
        for e in range(N_EXPERTS):
            tok, slot = jnp.nonzero(top_ids == e, size=CAPACITY, fill_value=(N, 0))
            w = probs_pad[tok, slot][:, None]
            xin = x_pad[tok]
            a = xin @ W[e]
            b = xin @ V[e]
            y = a * (b * jax.nn.sigmoid(b)) @ W_out[e]
            out = out.at[tok].add(y * w)
        return out[:N].reshape(Bq, Tq, D)
    x = x + _L0_xattn_ref(_layernorm(x, axis=-1), ctx_1024, ctx_1024, fside_BxSxS2_0, mask_BxSxS2_ik1, L0_xattn_wq_k, L0_xattn_wq_b, L0_xattn_wk_k, L0_xattn_wk_b, L0_xattn_wv_k, L0_xattn_wv_b, L0_xattn_wo_k, L0_xattn_wo_b)
    x = x + _L0_attn_ref(_layernorm(x, axis=-1), L0_attn_Wq, L0_attn_Wk, L0_attn_Wv, L0_attn_Wg, L0_attn_gk_w1, L0_attn_gk_w2, L0_attn_gk_b, L0_attn_Wo, L0_attn_rms_w)
    x = x + _L0_ffn_ref(_layernorm(x, axis=-1), L0_ffn_router_w, L0_ffn_router_b, L0_ffn_W, L0_ffn_V, L0_ffn_W_out)
    return x

_drawn_inputs = setup_inputs


def setup_inputs(seed=0):
    import zlib

    import numpy as np

    out = dict(_drawn_inputs(seed))
    spreads = {'L0_xattn_wq_b': (0.0, 0.1),
     'L0_xattn_wk_b': (0.0, 0.8),
     'L0_xattn_wv_b': (0.0, 0.1),
     'L0_xattn_wo_b': (0.0, 0.1),
     'L0_attn_gk_b': (0.0, 0.8),
     'L0_attn_rms_w': (1.0, 0.2),
     'L0_ffn_router_b': (0.0, 0.1)}
    factors = {'L0_attn_gk_w1': 8.0, 'L0_attn_gk_w2': 8.0}
    for name, (base, spread) in spreads.items():
        noise = np.random.default_rng([zlib.crc32(name.encode()), seed]).standard_normal(out[name].shape)
        drawn = base * np.exp(spread * noise) if base else spread * noise
        out[name] = jnp.asarray(drawn.astype(out[name].dtype))
    for name, factor in factors.items():
        out[name] = (out[name] * factor).astype(out[name].dtype)
    return out
```

```python
from contextlib import ExitStack

import concourse.bass as bass
from concourse import mybir

F32 = mybir.dt.float32
BF16 = mybir.dt.bfloat16
I32 = mybir.dt.int32
U32 = mybir.dt.uint32
ALU = mybir.AluOpType
ACT = mybir.ActivationFunctionType
AX_X = mybir.AxisListType.X

P = 128
EPS = 1e-5
NEG = -998244352.0
LOWEST = -3.0e38

ONES_BF = 0x3F803F80
POOL_SETS = (3, 23, 24)

LEVELS = (64, 32, 16, 8, 4, 2, 1)
NLEVEL = len(LEVELS)
NDIAG = 6
CONSTS = NDIAG * 32 + 2 * P + 8

HEADS = 16
GH = 4
GROUPS = HEADS // GH
KT_TICK = 4
LEAD = GH + 1
PAIRS = [(0, 0), (0, 1), (1, 0), (1, 1), (0, 2), (2, 0)]
ZROW = 64
AUG = 68


def perceiver_kernel(nc, x, ctx, fside, mask, wq, bq, wk, bk, wv, bv, wo, bo,
                     gWq, gWk, gWv, gWg, gw1, gw2, gb, gWo, grms,
                     rw, rb, eW, eV, eWo, shape_consts, out):
    B, S, D = x.shape
    S2 = ctx.shape[1]
    DH = D // HEADS
    NK = S2 // P
    NC = S2 // 512
    UNITS = B * GROUPS
    STEPS = NK // KT_TICK
    TICKS = UNITS * STEPS
    HEAD_SEQ = UNITS * GH
    SCALE = float(DH) ** -0.5

    es = ExitStack()
    with es:
        def sb(name, shape, dt=F32):
            return es.enter_context(nc.sbuf_tensor(name, shape, dt))

        def pb(name, shape, dt=F32):
            return es.enter_context(nc.psum_tensor(name, shape, dt))

        def sem(name):
            return es.enter_context(nc.semaphore(name))

        identf = sb("identf", [P, P])
        negident = sb("negident", [P, GH, P], BF16)
        identb = negident[:, 0, :]
        ones32 = sb("ones32", [P, 32])
        headsel = sb("headsel", [P, GH])
        quadsel = sb("quadsel", [P, 1])
        halfneg = sb("halfneg", [P, B])

        x1 = sb("x1", [P, B, D])
        xh = sb("xh", [P, B, D])
        xhT = sb("xhT", [P, B * P])
        bnst = sb("bnst", [P, B, 6])
        mv = sb("mv", [P, B, 2])
        rstd = sb("rstd", [P, B])

        wq_s, wk_s, wv_s = sb("wq_s", [P, D]), sb("wk_s", [P, D]), sb("wv_s", [P, D])
        wo_s = sb("wo_s", [P, GROUPS, D])
        bv_s, bo_s = sb("bv_s", [P, D]), sb("bo_s", [P, D])
        bq_s, bk_s, bqs = sb("bq_s", [P, 1]), sb("bk_s", [P, 1]), sb("bqs", [P, 1])

        qf = sb("qf", [P, B * P])
        qparts = sb("qparts", [P, 3, B * P], BF16)
        qpart = [qparts[:, i, :] for i in range(3)]
        kparts = sb("kparts", [P, 3, S2], BF16)
        kpart = [kparts[:, i, :] for i in range(3)]
        qaug = sb("qaug", [AUG, HEADS, B, P], BF16)
        kaug = [sb(f"kaug{i}", [AUG, GH, S2], BF16) for i in range(3)]

        ctx_s = sb("ctx_s", [P, NK, D])
        ctxT = sb("ctxT", [P, S2])
        v_s = [sb(f"v_s{i}", [P, NK, D]) for i in range(2)]
        f_s = sb("f_s", [P, S2])
        gT = [sb(f"gT{i}", [P, NK, P]) for i in range(2)]
        mask_s = sb("mask_s", [P, S2], I32)
        neg = [sb(f"neg{i}", [P, S2], BF16) for i in range(2)]
        junk = sb("junk", [P, 2, 512], BF16)

        prob = [sb(f"prob{i}", [P, KT_TICK, GH * P]) for i in range(2)]
        probg = [sb(f"probg{i}", [P, KT_TICK, GH * P]) for i in range(2)]
        def kf(b, cols):
            return (prob[0][:, :, :].rearrange("p t q -> p (t q)") if b == 0 else f_s)[:, cols]
        mx = sb("mx", [P, GH, NC])
        mtop = sb("mtop", [P, GH])
        mres = sb("mres", [P, GH])
        mpart = sb("mpart", [P, GH, 4], BF16)
        numer = sb("numer", [P, GH, P])
        denom = sb("denom", [P, GH, P])
        rden = sb("rden", [P, GH])

        banks = pb("banks", [P, 8, 512])
        score = [banks[:, 0:2, :], banks[:, 2:4, :]]
        work = [banks[:, 4, :], banks[:, 5, :]]
        num_ps, den_ps = banks[:, 6, :], banks[:, 7, :]

        LH, HK = 4, gWq.shape[1] // 4
        HV = gWv.shape[1] // LH
        DV, LR, E, HID = gWv.shape[1], gw1.shape[1], eW.shape[0], eW.shape[2]
        CAPACITY = 2 * B * S * 2 // E
        N = B * P
        cst = sb("cst", [P, CONSTS])
        levelsel = cst[:, 0:NDIAG * 32].rearrange("p (l t) -> p l t", t=32)
        blocksel = cst[:, NDIAG * 32:NDIAG * 32 + P].rearrange("p (m t) -> p m t", t=32)
        upto = cst[:, NDIAG * 32 + P:NDIAG * 32 + 2 * P]
        expert_no = cst[:, NDIAG * 32 + 2 * P:CONSTS]
        ones_sq = sb("ones_sq", [P, P])

        def flat(t):
            return t[:, :, :].rearrange("p a b -> p (a b)")

        small = flat(v_s[0])
        free = [0]

        def carve(n):
            free[0] += n
            return small[:, free[0] - n:free[0]]

        wqk_l, wvg_l, wo_l = carve(2 * P), carve(2 * DV), carve(2 * D).rearrange("p (a n) -> p a n", a=2)
        w1_l, w2_l, b_l, rms_l = carve(LR), carve(P)[0:LR, :], carve(1), carve(HV)
        rw_s, rb_s = carve(E), carve(E)
        logit = carve(B * E).rearrange("p (b e) -> p b e", e=E)
        top = carve(B * E).rearrange("p (b e) -> p b e", e=E)
        topno = carve(B * E).rearrange("p (b e) -> p b e", e=E)
        topnof = carve(B * E).rearrange("p (b e) -> p b e", e=E)
        pick = [carve(B * E).rearrange("p (b e) -> p b e", e=E) for _ in range(2)]
        chosen = carve(B * E).rearrange("p (b e) -> p b e", e=E)
        weight = carve(B * E).rearrange("p (b e) -> p b e", e=E)
        ratio, top_p = carve(B), [carve(B) for _ in range(2)]
        rms_sum, rms_inv, rms_half = carve(B * LH), carve(B * LH), carve(B * LH)
        qT, kT = flat(prob[0])[:, 0:N], flat(prob[0])[:, N:2 * N]
        decay, cum = flat(prob[0])[:, 2 * N:3 * N], flat(prob[0])[:, 3 * N:4 * N]
        val = flat(prob[1])[:, 0:B * DV].rearrange("p (b v) -> p b v", v=DV)
        zgate = flat(prob[1])[:, B * DV:2 * B * DV].rearrange("p (b v) -> p b v", v=DV)
        expo = [flat(probg[0])[:, N * i:N * i + N] for i in range(2)]
        lowT = flat(probg[0])[0:LR, 2 * N:3 * N]
        lnexp = flat(probg[0])[:, 3 * N:4 * N]
        scaled = [flat(gT[i // 4])[:, N * (i % 4):N * (i % 4) + N] for i in range(NLEVEL)]
        attT = flat(probg[1]).rearrange("p (c t) -> p c t", t=P)
        picked = kparts[:, :, :].rearrange("p a b -> p (a b)").bitcast(F32).rearrange(
            "p (c l t) -> p c l t", l=NDIAG, t=32)
        diag = flat(gT[1])[:, 3 * N:4 * N].rearrange("p (c t) -> p c t", t=32)
        mixed = flat(v_s[1])[:, 0:B * DV].rearrange("p (b v) -> p b v", v=DV)
        squares = flat(v_s[1])[:, B * DV:2 * B * DV].rearrange("p (b v) -> p b v", v=DV)
        mixedT = flat(probg[0])[:, 0:2 * N].rearrange("p (a n) -> p a n", a=2)
        eW_s = flat(ctx_s).rearrange("p (e f) -> p e f", e=E)
        eV_s = f_s[:, :].rearrange("p (e f) -> p e f", e=E)
        eWo_s = mask_s[:, :].bitcast(F32).rearrange("p (e a d) -> p e a d", e=E, a=2)
        tanhs = [flat(prob[0])[:, N * i:N * i + N] for i in range(2)]
        gated = [flat(prob[0])[:, N * (2 + i):N * (2 + i) + N] for i in range(2)]
        hidT = [flat(prob[1])[:, N * i:N * i + N] for i in range(4)]

        q_dram = nc.dram_tensor("q_dram", [3, P, B * P], BF16, kind="Internal").ap()
        k_dram = nc.dram_tensor("k_dram", [B, 3, P, S2], BF16, kind="Internal").ap()

        x_in, w_in, wo_in = sem("x_in"), sem("w_in"), sem("wo_in")
        ctx_in, f_in, mask_in = sem("ctx_in"), sem("f_in"), sem("mask_in")
        qaug_in = sem("qaug_in")
        q_stored, k_stored = sem("q_stored"), sem("k_stored")
        kaug_in = [sem(f"kaug_in{i}") for i in range(3)]
        const_made = sem("const_made")
        kaug_set = sem("kaug_set")
        pool_chain, dve_chain, act_chain = sem("pool_chain"), sem("dve_chain"), sem("act_chain")
        stats_made, rstd_made, xh_made = sem("stats_made"), sem("rstd_made"), sem("xh_made")
        work_filled, work_read_dve, work_read_act = sem("work_filled"), sem("work_read_dve"), sem("work_read_act")
        q_parts_made = sem("q_parts_made")
        k_half_made = sem("k_half_made")
        k_parts_made = sem("k_parts_made")
        neg_made = sem("neg_made")
        score_made, exp_made = sem("score_made"), sem("exp_made")
        gated_pool, gated_dve = sem("gated_pool"), sem("gated_dve")
        pv_done = sem("pv_done")
        mpart_made = sem("mpart_made")
        numer_made, denom_made = sem("numer_made"), sem("denom_made")
        cst_in, l_in, e_in = sem("cst_in"), sem("l_in"), sem("e_in")
        attention_done = sem("attention_done")
        l_proj, l_read_act, l_read_dve = sem("l_proj"), sem("l_read_act"), sem("l_read_dve")
        abs_made, expo_made, decayed, scaled_made = sem("abs_made"), sem("expo_made"), sem("decayed"), sem("scaled_made")
        pairs_made, picked_read, off_read, att_made = sem("pairs_made"), sem("picked_read"), sem("off_read"), sem("att_made")
        mixed_made, squared, sums_made, rms_made = sem("mixed_made"), sem("squared"), sem("sums_made"), sem("rms_made")
        gated_made, mixT_made, mixT_read, l_out = sem("gated_made"), sem("mixT_made"), sem("mixT_read"), sem("l_out")
        x_added = sem("x_added")
        logits_made, ratio_in, ratio_made, chosen_made, rank_made = (sem("logits_made"), sem("ratio_in"), sem("ratio_made"),
                                                                    sem("chosen_made"), sem("rank_made"))
        up_made, tanh_made, hid_made, down_made, expert_added = (sem("up_made"), sem("tanh_made"), sem("hid_made"),
                                                                 sem("down_made"), sem("expert_added"))
        out_done = sem("out_done")

        def prep(b, kind, c):
            return (kind, b, c)

        def tick_work(t):
            u, s = divmod(t, STEPS)
            b, i = divmod(t, GROUPS * STEPS)
            items = []
            n = t + LEAD
            if n < HEAD_SEQ:
                items += [("max", n, c) for c in range(NC)]
            if b + 1 < B:
                if 1 <= i <= 4:
                    items.append(("ctxT", b + 1, i - 1))
                if i in (5, 6):
                    items += [("k", b + 1, 2 * (i - 5)), ("k", b + 1, 2 * (i - 5) + 1)]
                if 7 <= i <= 10:
                    items.append(("v", b + 1, i - 7))
                if 11 <= i <= 14:
                    items.append(("gT", b + 1, i - 11))
            if s == STEPS - 1 and u + 1 < UNITS:
                items.append(("mrow", u + 1, 0))
            if u >= 1 and s == 1:
                items.append(("den", u - 1, 0))
            if u >= 1 and s == 2:
                items.append(("wo", u - 1, 0))
            return items

        start_work = [("xhT", 0, 0)] + [("ctxT", 0, c) for c in range(NC)] + [("q", 0, 0)]
        start_work += [("k", 0, c) for c in range(NC)] + [("v", 0, c) for c in range(NC)]
        start_work += [("gT", 0, c) for c in range(NC)]
        start_work += [("max", n, c) for n in range(GH) for c in range(NC)] + [("mrow", 0, 0)]
        start_work += [("max", n, c) for n in range(GH, LEAD) for c in range(NC)]
        end_work = [("den", UNITS - 1, 0), ("wo", UNITS - 1, 0)]
        all_work = start_work + [w for t in range(TICKS) for w in tick_work(t)] + end_work
        slot = {w: n for n, w in enumerate(all_work)}
        BY_ACT = ("ctxT", "q", "k", "gT", "mrow", "xhT")
        reads_before = {}
        counts = {"act": 0, "dve": 0}
        for w in all_work:
            who = "act" if w[0] in BY_ACT else "dve"
            counts[who] += 1
            reads_before[w] = (who, counts[who])

        def bank_of(w):
            return work[slot[w] % 2]

        def await_bank(pe, w):
            if slot[w] >= 2:
                who, n = reads_before[all_work[slot[w] - 2]]
                pe.wait_ge(work_read_act if who == "act" else work_read_dve, n)

        def await_filled(eng, w):
            eng.wait_ge(work_filled, slot[w] + 1)

        block = es.enter_context(nc.Block())

        @block.sync
        def _(sp):
            sp.dma_start(x1[:, :, :], x.rearrange("b s d -> s b d")).then_inc(x_in, 16)
            for h in range(2):
                sp.dma_start(ctx_s[:, 8 * h:8 * h + 8, :],
                             ctx[0, 1024 * h:1024 * h + 1024, :].rearrange("(t p) d -> p t d", p=P)).then_inc(ctx_in, 16)
            sp.dma_start(wk_s[:, :], wk).then_inc(w_in, 16)
            sp.dma_start(wq_s[:, :], wq).then_inc(w_in, 16)
            sp.dma_start(bk_s[:, :], bk.rearrange("(d a) -> d a", a=1)).then_inc(w_in, 16)
            sp.dma_start(bq_s[:, :], bq.rearrange("(d a) -> d a", a=1)).then_inc(w_in, 16)
            sp.dma_start(wv_s[:, :], wv).then_inc(w_in, 16)
            sp.dma_start(bv_s[:, :], bv.partition_broadcast(P)).then_inc(w_in, 16)
            sp.dma_start(bo_s[:, :], bo.partition_broadcast(P)).then_inc(w_in, 16)
            sp.dma_start(mask_s[:, :], mask[0]).then_inc(mask_in, 16)
            sp.dma_start(f_s[:, :], fside[0]).then_inc(f_in, 16)

            def stack_q():
                sp.dma_start(q_dram.rearrange("i p n -> p i n"), qparts[:, :, :]).then_inc(q_stored, 16)
                sp.wait_ge(q_stored, 16)
                for c, (qi, _) in enumerate(PAIRS):
                    sp.dma_start(qaug[8 * c:8 * c + 8, :, :, :].rearrange("d h b q -> d h (b q)"),
                                 q_dram[qi].rearrange("(h d) n -> d h n", d=DH)).then_inc(qaug_in, 16)

            def store_k(b):
                sp.wait_ge(k_parts_made, b + 1)
                sp.dma_start(k_dram[b].rearrange("i p n -> p i n"), kparts[:, :, :]).then_inc(k_stored, 16)
                sp.wait_ge(k_stored, 16 * (b + 1))

            def stack_k(u):
                b, g = divmod(u, GROUPS)
                if g == 0:
                    store_k(b)
                if u < 3:
                    sp.wait_ge(kaug_set, 3 + u)
                    sp.wait_ge(pool_chain, POOL_SETS[u])
                if u >= 3:
                    sp.wait_ge(score_made, 2 * STEPS * (u - 2))
                for c, (_, ki) in enumerate(PAIRS):
                    sp.dma_start(kaug[u % 3][8 * c:8 * c + 8, :, :],
                                 k_dram[b, ki, 32 * g:32 * g + 32, :].rearrange("(h d) n -> d h n", d=DH)).then_inc(
                        kaug_in[u % 3], 16)

            sp.wait_ge(q_parts_made, 1)
            sp.wait_ge(kaug_set, 2)
            stack_q()
            stack_k(0)
            sp.dma_start(cst[:, :], shape_consts).then_inc(cst_in, 16)
            for g in range(GROUPS):
                sp.dma_start(wo_s[32 * g:32 * g + 32, :, :], wo.rearrange("(g r) n -> r g n", r=32)).then_inc(wo_in, 16)
            for u in range(1, UNITS):
                b, g = divmod(u, GROUPS)
                if g == 1 and b + 1 < B:
                    sp.wait_ge(work_filled, slot[("ctxT", b, NC - 1)] + 1)
                    for h in range(2):
                        sp.dma_start(ctx_s[:, 8 * h:8 * h + 8, :],
                                     ctx[b + 1, 1024 * h:1024 * h + 1024, :].rearrange("(t p) d -> p t d", p=P)).then_inc(ctx_in, 16)
                    sp.wait_ge(neg_made, b + 1)
                    sp.dma_start(mask_s[:, :], mask[b + 1]).then_inc(mask_in, 16)
                if g == 0:
                    sp.wait_ge(k_parts_made, b + 1)
                    sp.dma_start(f_s[:, :], fside[b]).then_inc(f_in, 16)
                stack_k(u)
            sp.wait_ge(pv_done, (B - 1) * GROUPS * STEPS)
            for dst, src in ((wqk_l[:, 0:P], gWq), (wqk_l[:, P:2 * P], gWk), (wvg_l[:, 0:DV], gWv), (wvg_l[:, DV:], gWg),
                             (wo_l, gWo.rearrange("(a p) n -> p a n", p=P)), (w1_l, gw1), (w2_l, gw2),
                             (b_l, gb.rearrange("(d a) -> d a", a=1)), (rms_l, grms.partition_broadcast(P)),
                             (rw_s, rw), (rb_s, rb.partition_broadcast(P))):
                sp.dma_start(dst, src).then_inc(l_in, 16)
            sp.wait_ge(neg_made, B)
            sp.dma_start(eWo_s, eWo.rearrange("e (a p) d -> p e a d", p=P)).then_inc(e_in, 16)
            sp.wait_ge(work_filled, slot[("gT", B - 1, NC - 1)] + 1)
            sp.dma_start(eW_s, eW.rearrange("e d f -> d e f")).then_inc(e_in, 16)
            sp.dma_start(eV_s, eV.rearrange("e d f -> d e f")).then_inc(e_in, 16)
            sp.wait_ge(expert_added, E)
            sp.dma_start(out.rearrange("b s d -> s b d"), x1[:, :, :]).then_inc(out_done, 16)
            sp.wait_ge(out_done, 16)

        @block.tensor
        def _(pe):
            T = nc.tensor

            def transposes(w, src):
                await_bank(pe, w)
                for j in range(4):
                    last = T.transpose(bank_of(w)[:, P * j:P * j + P], src(j), identf[:, :])
                last.then_inc(work_filled, 1)

            def do_work(w):
                kind, a, c = w
                bank = bank_of(w)
                if kind == "xhT":
                    pe.wait_ge(pool_chain, 2)
                    pe.wait_ge(xh_made, 1)
                    transposes(w, lambda j: xh[:, j, :])
                elif kind == "ctxT":
                    pe.wait_ge(ctx_in, 32 * (a + 1))
                    transposes(w, lambda j: ctx_s[:, 4 * c + j, :])
                elif kind == "gT":
                    pe.wait_ge(f_in, 16 * (a + 1))
                    transposes(w, lambda j: f_s[:, 512 * c + P * j:512 * c + P * j + P])
                elif kind == "q":
                    pe.wait_ge(w_in, 112)
                    await_bank(pe, w)
                    pe.wait_ge(work_read_act, reads_before[("xhT", 0, 0)][1])
                    T.matmul(bank[:, :], wq_s[:, :], xhT[:, :], start=True, stop=True).then_inc(work_filled, 1)
                elif kind == "k":
                    await_bank(pe, w)
                    pe.wait_ge(work_read_act, reads_before[("ctxT", a, c)][1])
                    T.matmul(bank[:, :], wk_s[:, :], ctxT[:, 512 * c:512 * c + 512], start=True, stop=True).then_inc(work_filled, 1)
                elif kind == "v":
                    await_bank(pe, w)
                    for j in range(4):
                        o = 512 * c + P * j
                        last = T.matmul(bank[:, P * j:P * j + P], ctxT[:, o:o + P], wv_s[:, :], start=True, stop=True)
                    last.then_inc(work_filled, 1)
                elif kind == "max":
                    u, h = divmod(a, GH)
                    b, g = divmod(u, GROUPS)
                    if c == 0:
                        pe.wait_ge(qaug_in, 16 * len(PAIRS))
                        pe.wait_ge(kaug_in[u % 3], 16 * len(PAIRS) * (u // 3 + 1))
                    await_bank(pe, w)
                    T.matmul(bank[:, :], qaug[0:ZROW + 1, GH * g + h, b, :],
                             kaug[u % 3][0:ZROW + 1, h, 512 * c:512 * c + 512], start=True, stop=True).then_inc(work_filled, 1)
                elif kind == "mrow":
                    await_bank(pe, w)
                    pe.wait_ge(mpart_made, a + 1)
                    for h in range(GH):
                        last = T.matmul(bank[ZROW:AUG, P * h:P * h + P], mpart[:, h, :], identb, start=True, stop=True,
                                        tile_position=(0, ZROW))
                    last.then_inc(work_filled, 1)
                elif kind == "den":
                    await_bank(pe, w)
                    pe.wait_ge(denom_made, a + 1)
                    for h in range(GH):
                        last = T.matmul(bank[:, h:h + 1], denom[:, h, :], quadsel[:, :], start=True, stop=True)
                    last.then_inc(work_filled, 1)
                elif kind == "wo":
                    g = a % GROUPS
                    if a == 0:
                        pe.wait_ge(wo_in, 64)
                    await_bank(pe, w)
                    pe.wait_ge(numer_made, a + 1)
                    for h in range(GH):
                        last = T.matmul(bank[:, P * h:P * h + P], numer[:, h, :], wo_s[:, g, :], start=True, stop=True)
                    last.then_inc(work_filled, 1)

            def scores(t, half):
                u, s = divmod(t, STEPS)
                b, g = divmod(u, GROUPS)
                e = 2 * t + half
                if e >= 2:
                    pe.wait_ge(exp_made, e - 1)
                if s == 0 and half == 0:
                    pe.wait_ge(work_read_act, reads_before[("mrow", u, 0)][1])
                    pe.wait_ge(neg_made, b + 1)
                for j in range(2):
                    kt = KT_TICK * s + 2 * half + j
                    T.matmul(score[half][:, j, :], neg[b % 2][:, P * kt:P * kt + P],
                             negident[:, :, :].rearrange("p h q -> p (h q)"), start=True, stop=False)
                    for h in range(GH):
                        last = T.matmul(score[half][:, j, P * h:P * h + P], kaug[u % 3][:, h, P * kt:P * kt + P],
                                        qaug[:, GH * g + h, b, :], start=False, stop=(h == GH - 1))
                last.then_inc(score_made, 1)

            def values(t):
                u, s = divmod(t, STEPS)
                b, g = divmod(u, GROUPS)
                pe.wait_ge(exp_made, 2 * t + 2)
                if s == 0 and u >= 1:
                    pe.wait_ge(denom_made, u)
                for j in range(KT_TICK):
                    T.matmul(den_ps[32 * j:32 * j + 32, :], ones32[:, :], prob[t % 2][:, j, :],
                             start=(s == 0), stop=(s == STEPS - 1), tile_position=(0, 32 * j))
                pe.wait_ge(gated_pool, 2 * t + 2)
                pe.wait_ge(gated_dve, 2 * t + 2)
                if s == 0:
                    pe.wait_ge(work_read_dve, reads_before[("v", b, NC - 1)][1])
                    if u >= 1:
                        pe.wait_ge(numer_made, u)
                for j in range(KT_TICK):
                    last = T.matmul(num_ps[32 * j:32 * j + 32, :], v_s[b % 2][:, KT_TICK * s + j, 32 * g:32 * g + 32],
                                    probg[t % 2][:, j, :], start=(s == 0), stop=(s == STEPS - 1), tile_position=(0, 32 * j))
                last.then_inc(pv_done, 1)

            for w in start_work:
                do_work(w)
            for t in range(TICKS):
                items = tick_work(t)
                scores(t, 0)
                for w in items[:2]:
                    do_work(w)
                scores(t, 1)
                for w in items[2:4]:
                    do_work(w)
                if t >= 1:
                    values(t - 1)
                for w in items[4:]:
                    do_work(w)
            values(TICKS - 1)
            for w in end_work:
                do_work(w)

            def to_features(n):
                pe.wait_ge(xh_made, n + 1)
                for b in range(B):
                    last = T.transpose(banks[:, 0, P * b:P * b + P], xh[:, b, :], identf[:, :])
                last.then_inc(l_proj, 1)

            to_features(1)
            pe.wait_ge(l_in, 16 * 11)
            pe.wait_ge(l_read_act, 1)
            T.matmul(banks[0:LR, 1, :], w1_l, xhT[:, :], start=True, stop=True).then_inc(l_proj, 1)
            T.matmul(banks[:, 2, :], wqk_l[:, 0:P], xhT[:, :], start=True, stop=True)
            T.matmul(banks[:, 3, :], wqk_l[:, P:2 * P], xhT[:, :], start=True, stop=True).then_inc(l_proj, 1)
            pe.wait_ge(l_read_act, 2)
            T.matmul(banks[:, 0, :], w2_l, lowT, start=True, stop=True).then_inc(l_proj, 1)
            for b in range(B):
                last = T.matmul(banks[:, 4 + b, :], xhT[:, P * b:P * b + P], wvg_l, start=True, stop=True)
            last.then_inc(l_proj, 1)
            pe.wait_ge(l_read_act, 5)
            pe.wait_ge(l_read_dve, 2)
            for r in range(B // 2):
                if r == 1:
                    pe.wait_ge(picked_read, 1)
                    pe.wait_ge(off_read, 1)
                for b in (2 * r, 2 * r + 1):
                    for l in range(NDIAG):
                        if r == 0 and b == 0:
                            pe.wait_ge(scaled_made, NLEVEL if l == NDIAG - 1 else l + 3)
                        for m in range(4):
                            for h in range(LH):
                                kd = slice(HK * h, HK * h + HK)
                                o = P * b + 32 * m
                                left, right = (kT, qT) if l == NDIAG - 1 else (scaled[l + 2], scaled[l + 2])
                                T.matmul(banks[32 * m:32 * m + 32, LH * (b % 2) + h, 32 * l:32 * l + 32],
                                         left[kd, o:o + 32], right[kd, o:o + 32], start=True, stop=True,
                                         tile_position=(HK * h, 32 * m))
                    for h in range(LH):
                        kd = slice(HK * h, HK * h + HK)
                        bank = banks[:, LH * (b % 2) + h, :]
                        for m in (0, 64):
                            T.matmul(bank[m:m + 32, 256:288], scaled[1][kd, P * b + m:P * b + m + 32],
                                     scaled[1][kd, P * b + m + 32:P * b + m + 64], start=True, stop=True,
                                     tile_position=(HK * h, m))
                    for h in range(LH):
                        kd = slice(HK * h, HK * h + HK)
                        last = T.matmul(banks[0:64, LH * (b % 2) + h, 192:256], scaled[0][kd, P * b:P * b + 64],
                                        scaled[0][kd, P * b + 64:P * b + P], start=True, stop=True,
                                        tile_position=(HK * h, 0))
                last.then_inc(pairs_made, 1)
            pe.wait_ge(off_read, 2)
            for b in range(B):
                for h in range(LH):
                    o = DV * (b % 2) + HV * h
                    last = T.matmul(banks[:, b // 2, o:o + HV], attT[:, LH * b + h, :], val[:, b, HV * h:HV * h + HV],
                                    start=True, stop=True)
            last.then_inc(mixed_made, 1)
            pe.wait_ge(gated_made, 1)
            for a in range(2):
                for b in range(B):
                    last = T.transpose(banks[:, 2 + a, P * b:P * b + P], mixed[:, b, P * a:P * a + P], identf[:, :])
            last.then_inc(mixT_made, 1)
            pe.wait_ge(mixT_read, 1)
            for b in range(B):
                for a in range(2):
                    last = T.matmul(banks[:, 4, P * b:P * b + P], mixedT[:, a, P * b:P * b + P], wo_l[:, a, :],
                                    start=(a == 0), stop=(a == 1))
            last.then_inc(l_out, 1)

            to_features(2)
            pe.wait_ge(l_read_act, 6)
            for b in range(B):
                last = T.matmul(banks[:, 7, E * b:E * b + E], xhT[:, P * b:P * b + P], rw_s, start=True, stop=True)
            last.then_inc(logits_made, 1)
            pe.wait_ge(e_in, 48)

            def up(i):
                e, a = divmod(i, 2)
                if i >= 3:
                    pe.wait_ge(hid_made, i - 2)
                T.matmul(banks[:, 2 * (i % 3), :], eW_s[:, e, P * a:P * a + P], xhT[:, :], start=True, stop=True)
                T.matmul(banks[:, 2 * (i % 3) + 1, :], eV_s[:, e, P * a:P * a + P], xhT[:, :], start=True, stop=True).then_inc(up_made, 1)

            def down(e):
                pe.wait_ge(hid_made, 2 * e + 2)
                if e >= 2:
                    pe.wait_ge(expert_added, e - 1)
                if e == 1:
                    pe.wait_ge(l_read_dve, 5)
                for b in range(B):
                    for a in range(2):
                        last = T.matmul(banks[:, 6 + e % 2, P * b:P * b + P], hidT[(2 * e + a) % 4][:, P * b:P * b + P],
                                        eWo_s[:, e, a, :], start=(a == 0), stop=(a == 1))
                last.then_inc(down_made, 1)

            for i in range(2 * E):
                if i == 2:
                    pe.wait_ge(chosen_made, 1)
                    for b in range(B):
                        for c in range(b + 1):
                            last = T.matmul(banks[:, 7, E * b:E * b + E], upto if c == b else ones_sq[:, :], chosen[:, c, :],
                                            start=(c == 0), stop=(c == b))
                    last.then_inc(rank_made, 1)
                up(i)
                if i >= 3 and i % 2:
                    down(i // 2 - 1)
            down(E - 1)

        @block.scalar
        def _(act):
            A = nc.scalar
            chain = [0]

            def link(ins):
                chain[0] += 1
                ins.then_inc(act_chain, 1)
                act.wait_ge(act_chain, chain[0])

            def read_work(w):
                kind, a, c = w
                bank = bank_of(w)
                if kind == "q":
                    act.wait_ge(w_in, 112)
                    link(A.activation(bqs[:, :], bq_s[:, :], ACT.Copy, scale=SCALE))
                await_filled(act, w)
                if kind == "xhT":
                    A.copy(xhT[:, :], bank[:, :]).then_inc(work_read_act, 1)
                elif kind == "ctxT":
                    if a >= 1 and c == 0:
                        act.wait_ge(work_filled, slot[("v", a - 1, NC - 1)] + 1)
                    A.copy(ctxT[:, 512 * c:512 * c + 512], bank[:, :]).then_inc(work_read_act, 1)
                elif kind == "gT":
                    A.copy(gT[a % 2][:, 4 * c:4 * c + 4, :].rearrange("p t q -> p (t q)"), bank[:, :]).then_inc(work_read_act, 1)
                elif kind == "q":
                    A.activation(qf[:, :], bank[:, :], ACT.Identity, bias=bqs[:, :], scale=SCALE)
                    A.activation(qpart[0], bank[:, :], ACT.Identity, bias=bqs[:, :], scale=SCALE).then_inc(work_read_act, 1)
                elif kind == "k":
                    if a >= 1 and c == 0:
                        act.wait_ge(work_filled, slot[("gT", a - 1, NC - 1)] + 1)
                        act.wait_ge(k_stored, 16 * a)
                    o = 512 * c
                    A.activation(kf(a, slice(o, o + 512)), bank[:, :], ACT.Identity, bias=bk_s[:, :])
                    A.activation(kpart[0][:, o:o + 512], bank[:, :], ACT.Identity, bias=bk_s[:, :]).then_inc(work_read_act, 1)
                elif kind == "mrow":
                    b, g = divmod(a, GROUPS)
                    A.copy(qaug[ZROW:AUG, GH * g:GH * g + GH, b, :], bank[ZROW:AUG, :].rearrange(
                        "p (h q) -> p h q", h=GH)).then_inc(work_read_act, 1)

            def exps(t, half):
                act.wait_ge(score_made, 2 * t + half + 1)
                if half == 0 and t >= 2:
                    act.wait_ge(pv_done, t - 1)
                A.activation(prob[t % 2][:, 2 * half:2 * half + 2, :], score[half][:, :, :], ACT.Exp).then_inc(exp_made, 1)

            def denominators(u):
                act.wait_ge(pv_done, STEPS * (u + 1))
                if u >= 1:
                    act.wait_ge(work_filled, slot[("den", u - 1, 0)] + 1)
                A.copy(denom[:, :, :].rearrange("p h q -> p (h q)"), den_ps[:, :]).then_inc(denom_made, 1)

            for w in start_work:
                if w[0] in BY_ACT:
                    read_work(w)
            for t in range(TICKS):
                exps(t, 0)
                exps(t, 1)
                if t >= 1 and t % STEPS == 0:
                    denominators(t // STEPS - 1)
                for w in tick_work(t):
                    if w[0] in BY_ACT:
                        read_work(w)
            denominators(UNITS - 1)

            act.wait_ge(l_proj, 1)
            A.copy(xhT[:, :], banks[:, 0, :]).then_inc(l_read_act, 1)
            act.wait_ge(l_proj, 2)
            A.copy(lowT, banks[0:LR, 1, :]).then_inc(l_read_act, 1)
            act.wait_ge(l_proj, 3)
            A.activation(qT, banks[:, 2, :], ACT.Copy, scale=float(HK) ** -0.5)
            A.copy(kT, banks[:, 3, :]).then_inc(l_read_act, 1)
            act.wait_ge(l_proj, 4)
            link(A.activation(decay, banks[:, 0, :], ACT.Identity, bias=b_l))
            link(A.activation(lnexp, decay, ACT.Abs))
            link(A.activation(lnexp, lnexp, ACT.Exp, scale=-1.0))
            A.activation(lnexp, lnexp, ACT.Ln, bias=1.0).then_inc(l_read_act, 1)
            for l in range(NLEVEL):
                act.wait_ge(expo_made, l + 1)
                A.activation(expo[l % 2], expo[l % 2], ACT.Exp, scale=1.0 / 16.0).then_inc(decayed, 1)
                if l == 0:
                    act.wait_ge(l_proj, 5)
                    A.copy(val, banks[:, 4:8, 0:DV]).then_inc(l_read_act, 1)
            A.activation(zgate, banks[:, 4:8, DV:2 * DV], ACT.Tanh, scale=0.5).then_inc(squared, 1)
            for r in range(B // 2):
                act.wait_ge(pairs_made, r + 1)
                act.wait_ge(att_made, 1 + r)
                rows = slice(LH * 2 * r, LH * 2 * r + 8)
                A.copy(attT[0:64, rows, 64:128], banks[0:64, :, 192:256])
                A.copy(attT[0:32, rows, 32:64], banks[0:32, :, 256:288])
                A.copy(attT[64:96, rows, 96:128], banks[64:96, :, 256:288]).then_inc(off_read, 1)
            act.wait_ge(mixed_made, 1)
            A.activation(squares.rearrange("p (a b) v -> p a (b v)", a=2), banks[:, 0:2, :], ACT.Square).then_inc(squared, 1)
            act.wait_ge(mixT_made, 1)
            A.copy(mixedT, banks[:, 2:4, :]).then_inc(mixT_read, 1)
            act.wait_ge(l_proj, 6)
            A.copy(xhT[:, :], banks[:, 0, :]).then_inc(l_read_act, 1)
            for i in range(2 * E):
                if i == 1:
                    act.wait_ge(ratio_in, 1)
                    A.activation(ratio, ratio, ACT.Exp).then_inc(ratio_made, 1)
                act.wait_ge(up_made, i + 1)
                if i >= 2:
                    act.wait_ge(hid_made, i - 1)
                A.activation(tanhs[i % 2], banks[:, 2 * (i % 3) + 1, :], ACT.Tanh, scale=0.5).then_inc(tanh_made, 1)

        @block.vector
        def _(dve):
            V = nc.vector
            chain = [0]

            def link(ins):
                chain[0] += 1
                ins.then_inc(dve_chain, 1)
                dve.wait_ge(dve_chain, chain[0])

            def layer_norm(k):
                for b in range(B):
                    last = V.bn_stats(bnst[:, b, :], x1[:, b, :])
                link(last)
                for b in range(B):
                    last = V.bn_aggr(mv[:, b, :], bnst[:, b, :])
                last.then_inc(stats_made, 1)
                dve.wait_ge(rstd_made, k + 1)
                for b in range(B):
                    last = V.tensor_scalar(xh[:, b, :], x1[:, b, :], mv[:, b, 0:1], rstd[:, b:b + 1], ALU.subtract, ALU.mult)
                last.then_inc(xh_made, 1)

            def gate(t, half):
                u, s = divmod(t, STEPS)
                b = u // GROUPS
                dve.wait_ge(exp_made, 2 * t + half + 1)
                if half == 0:
                    if t >= 2:
                        dve.wait_ge(pv_done, t - 1)
                    if t % (GROUPS * STEPS) == 0:
                        dve.wait_ge(work_read_act, reads_before[("gT", b, NC - 1)][1])
                j = 2 * half + 1
                V.tensor_tensor(probg[t % 2][:, j, :].rearrange("p (h q) -> p h q", h=GH),
                                prob[t % 2][:, j, :].rearrange("p (h q) -> p h q", h=GH),
                                gT[b % 2][:, KT_TICK * s + j, :].unsqueeze(1).broadcast_to([P, GH, P]),
                                ALU.mult).then_inc(gated_dve, 1)

            def row_max(w):
                _, n, c = w
                u, h = divmod(n, GH)
                b = u // GROUPS
                if c == 0 and u % GROUPS == 0 and h == 0:
                    dve.wait_ge(neg_made, b + 1)
                await_filled(dve, w)
                if reads_before[w][1] > 2:
                    dve.wait_ge(work_read_dve, reads_before[w][1] - 2)
                V.tensor_tensor_reduce(out=junk[:, c % 2, :], in0=bank_of(w)[:, :], in1=neg[b % 2][:, 512 * c:512 * c + 512],
                                       scale=1.0, scalar=LOWEST, op0=ALU.add, op1=ALU.max,
                                       accum_out=mx[:, h, c:c + 1]).then_inc(work_read_dve, 1)

            def split_max(u):
                dve.wait_ge(work_read_dve, reads_before[("max", GH * u + GH - 1, NC - 1)][1])
                if u >= 1:
                    dve.wait_ge(work_filled, slot[("mrow", u - 1, 0)] + 1)
                link(V.reduce_max(mtop[:, :], mx[:, :, :], AX_X))
                link(V.tensor_scalar(mpart[:, :, 1], mtop[:, :], -1.0, None, ALU.mult))
                link(V.scalar_tensor_tensor(mres[:, :], mtop[:, :], -1.0, mpart[:, :, 1], ALU.mult, ALU.subtract))
                link(V.tensor_copy(mpart[:, :, 2], mres[:, :]))
                V.tensor_tensor(mpart[:, :, 3], mres[:, :], mpart[:, :, 2], ALU.subtract).then_inc(mpart_made, 1)

            def value_bias(w):
                _, b, c = w
                await_filled(dve, w)
                if c == 0 and b >= 2:
                    dve.wait_ge(pv_done, GROUPS * STEPS * (b - 1))
                V.tensor_tensor(v_s[b % 2][:, 4 * c:4 * c + 4, :], bank_of(w)[:, :].rearrange("p (t d) -> p t d", t=4),
                                bv_s[:, :].unsqueeze(1).broadcast_to([P, 4, D]), ALU.add).then_inc(work_read_dve, 1)

            def numerators(u):
                dve.wait_ge(pv_done, STEPS * (u + 1))
                if u >= 1:
                    dve.wait_ge(work_filled, slot[("wo", u - 1, 0)] + 1)
                V.tensor_tensor(numer[:, :, :], num_ps[:, :].rearrange("p (h q) -> p h q", h=GH),
                                headsel[:, :].unsqueeze(2).broadcast_to([P, GH, P]), ALU.mult).then_inc(numer_made, 1)

            def finish_den(w):
                await_filled(dve, w)
                ins = V.reciprocal(rden[:, :], bank_of(w)[:, 0:GH])
                ins.then_inc(work_read_dve, 1)

            def finish_wo(w):
                u = w[1]
                b = u // GROUPS
                await_filled(dve, w)
                dve.wait_ge(work_read_dve, reads_before[("den", u, 0)][1])
                for h in range(GH):
                    ins = V.scalar_tensor_tensor(x1[:, b, :], bank_of(w)[:, P * h:P * h + P], rden[:, h:h + 1], x1[:, b, :],
                                                 ALU.mult, ALU.add)
                    if h < GH - 1:
                        link(ins)
                ins.then_inc(work_read_dve, 1)
                dve.wait_ge(work_read_dve, reads_before[w][1])

            def read_work(w):
                {"max": row_max, "v": value_bias, "den": finish_den, "wo": finish_wo}[w[0]](w)

            V.memset(mpart[:, :, :], 0.0)
            V.memset(ones32[:, :], 1.0)
            V.memset(halfneg[:, :], -0.5)
            link(V.memset(ones_sq[:, :], 1.0))
            V.memset(qaug[32:64, :, :, :].rearrange("p a b c -> p (a b c)").bitcast(U32), 0).then_inc(kaug_set, 1)
            V.memset(qaug[64:AUG, :, :, :].rearrange("p a b c -> p (a b c)").bitcast(U32), 0).then_inc(kaug_set, 1)
            V.memset(kaug[0][32:64, :, :].rearrange("p a b -> p (a b)").bitcast(U32), 0).then_inc(kaug_set, 1)
            dve.wait_ge(x_in, 16)
            layer_norm(0)
            V.memset(kaug[1][32:64, :, :].rearrange("p a b -> p (a b)").bitcast(U32), 0).then_inc(kaug_set, 1)
            V.memset(kaug[2][32:64, :, :].rearrange("p a b -> p (a b)").bitcast(U32), 0).then_inc(kaug_set, 1)
            dve.wait_ge(work_read_act, reads_before[("q", 0, 0)][1])
            link(V.tensor_tensor(qf[:, :], qf[:, :], qpart[0], ALU.subtract))
            link(V.tensor_copy(qpart[1], qf[:, :]))
            V.tensor_tensor(qpart[2], qf[:, :], qpart[1], ALU.subtract).then_inc(q_parts_made, 1)
            dve.wait_ge(work_read_act, reads_before[("k", 0, NC - 1)][1])
            kf0 = kf(0, slice(0, S2))
            link(V.tensor_tensor(kf0, kf0, kpart[0], ALU.subtract))
            link(V.tensor_copy(kpart[1], kf0))
            V.tensor_tensor(kpart[2], kf0, kpart[1], ALU.subtract).then_inc(k_parts_made, 1)
            for b in range(B):
                ins = V.tensor_tensor(x1[:, b, :], x1[:, b, :], bo_s[:, :], ALU.add)
            link(ins)
            for w in start_work:
                if w[0] not in BY_ACT:
                    read_work(w)
                    if w == ("max", GH - 1, NC - 1):
                        split_max(0)
            for t in range(TICKS):
                u, s = divmod(t, STEPS)
                items = tick_work(t)
                gate(t, 0)
                for n in range(3):
                    for w in (items[0:2], items[2:4], items[4:])[n]:
                        if w[0] not in BY_ACT:
                            read_work(w)
                    if n == 0:
                        gate(t, 1)
                    if n == 1 and s == 0 and u >= 1:
                        numerators(u - 1)
                if s == STEPS - 2 and u + 1 < UNITS:
                    split_max(u + 1)
            numerators(UNITS - 1)
            read_work(("den", UNITS - 1, 0))
            read_work(("wo", UNITS - 1, 0))

            layer_norm(1)
            dve.wait_ge(l_read_act, 4)
            link(V.scalar_tensor_tensor(decay, decay, 0.0, lnexp, ALU.min, ALU.subtract))
            for b in range(B):
                last = V.tensor_tensor_scan(cum[:, P * b:P * b + P], ones_sq[:, :], decay[:, P * b:P * b + P], 0.0,
                                            ALU.mult, ALU.add)
            link(last)

            def parts_of(a, c):
                return a.rearrange("p (n two c) -> p n two c", two=2, c=c)

            def exponents(l):
                c = LEVELS[l]
                g, x_ = parts_of(cum, c), parts_of(expo[l % 2], c)
                border = g[:, :, 0, c - 1:c].broadcast_to([P, N // (2 * c), c])
                if l >= 2:
                    dve.wait_ge(scaled_made, l - 1)
                V.tensor_tensor(x_[:, :, 1, :], g[:, :, 1, :], border, ALU.subtract)
                V.tensor_tensor(x_[:, :, 0, :], border, g[:, :, 0, :], ALU.subtract).then_inc(expo_made, 1)

            def scale_parts(l):
                c = LEVELS[l]
                w_, o_ = parts_of(expo[l % 2], c), parts_of(scaled[l], c)
                dve.wait_ge(decayed, l + 1)
                V.tensor_tensor(o_[:, :, 0, :], w_[:, :, 0, :], parts_of(kT, c)[:, :, 0, :], ALU.mult)
                V.tensor_tensor(o_[:, :, 1, :], w_[:, :, 1, :], parts_of(qT, c)[:, :, 1, :], ALU.mult).then_inc(scaled_made, 1)

            exponents(0)
            for l in range(NLEVEL):
                if l + 1 < NLEVEL:
                    exponents(l + 1)
                scale_parts(l)
            dve.wait_ge(squared, 1)
            V.scalar_tensor_tensor(zgate, zgate, 1.0, banks[:, 4:8, DV:2 * DV], ALU.add, ALU.mult).then_inc(l_read_dve, 2)
            dve.wait_ge(cst_in, 16)
            for r in range(B // 2):
                dve.wait_ge(pairs_made, r + 1)
                rows = slice(8 * r, 8 * r + 8)
                V.tensor_tensor(picked[:, rows, :, :].rearrange("p c l t -> p c (l t)"), banks[:, :, 0:NDIAG * 32],
                                levelsel.rearrange("p l t -> p (l t)").unsqueeze(1).broadcast_to([P, 8, NDIAG * 32]),
                                ALU.mult).then_inc(picked_read, 1)
                dve.wait_ge(picked_read, r + 1)
                link(V.tensor_reduce(diag[:, rows, :], picked[:, rows, :, :].rearrange("p c l t -> p c t l"), AX_X, ALU.add))
                V.tensor_tensor(attT[:, rows, :].rearrange("p c (m t) -> p c m t", t=32),
                                diag[:, rows, :].unsqueeze(2).broadcast_to([P, 8, 4, 32]),
                                blocksel.unsqueeze(1).broadcast_to([P, 8, 4, 32]), ALU.mult).then_inc(att_made, 1)
            dve.wait_ge(squared, 2)
            V.tensor_reduce(rms_sum, squares.rearrange("p b (h v) -> p (b h) v", v=HV), AX_X, ALU.add).then_inc(sums_made, 1)
            dve.wait_ge(rms_made, 1)
            link(V.tensor_tensor(mixed.rearrange("p b (h v) -> p (b h) v", v=HV),
                                 banks[:, 0:2, :].rearrange("p a (c v) -> p (a c) v", v=HV),
                                 rms_inv.unsqueeze(2).broadcast_to([P, B * LH, HV]), ALU.mult))
            link(V.tensor_tensor(mixed.rearrange("p b (h v) -> p (b h) v", v=HV),
                                 mixed.rearrange("p b (h v) -> p (b h) v", v=HV),
                                 rms_l.unsqueeze(1).broadcast_to([P, B * LH, HV]), ALU.mult))
            V.scalar_tensor_tensor(mixed, mixed, 0.5, zgate, ALU.mult, ALU.mult).then_inc(gated_made, 1)
            dve.wait_ge(l_out, 1)
            link(V.tensor_tensor(x1[:, :, :].rearrange("p b d -> p (b d)"), x1[:, :, :].rearrange("p b d -> p (b d)"),
                                 banks[:, 4, :], ALU.add))
            layer_norm(2)
            dve.wait_ge(logits_made, 1)
            link(V.tensor_tensor(logit, banks[:, 7, 0:B * E].rearrange("p (b e) -> p b e", e=E),
                                 rb_s.unsqueeze(1).broadcast_to([P, B, E]), ALU.add))
            for b in range(B):
                last = V.max(top[:, b, :], logit[:, b, :])
            link(last)
            for b in range(B):
                last = V.max_index(topno[:, b, :].bitcast(U32), top[:, b, :], logit[:, b, :])
            V.tensor_tensor(ratio, top[:, :, 1], top[:, :, 0], ALU.subtract).then_inc(ratio_in, 1)
            link(last)
            link(V.tensor_copy(topnof, topno.bitcast(U32)))
            for i in range(2):
                last = V.tensor_tensor(pick[i], expert_no.unsqueeze(1).broadcast_to([P, B, E]),
                                       topnof[:, :, i:i + 1].broadcast_to([P, B, E]), ALU.is_equal)
            link(last)
            V.tensor_tensor(chosen, pick[0], pick[1], ALU.add).then_inc(chosen_made, 1)
            dve.wait_ge(ratio_made, 1)
            link(V.tensor_scalar(top_p[0], ratio, 1.0, None, ALU.add))
            link(V.reciprocal(top_p[0], top_p[0]))
            link(V.tensor_tensor(top_p[1], top_p[0], ratio, ALU.mult))
            for i in range(2):
                last = V.tensor_tensor(pick[i], pick[i], top_p[i].unsqueeze(2).broadcast_to([P, B, E]), ALU.mult)
            link(last)
            link(V.tensor_tensor(weight, pick[0], pick[1], ALU.add))

            def hidden(i):
                dve.wait_ge(tanh_made, i + 1)
                link(V.scalar_tensor_tensor(gated[i % 2], tanhs[i % 2], 1.0, banks[:, 2 * (i % 3) + 1, :], ALU.add, ALU.mult))
                if i >= 4:
                    dve.wait_ge(down_made, i // 2 - 1)
                V.tensor_tensor(hidT[i % 4], gated[i % 2], banks[:, 2 * (i % 3), :], ALU.mult).then_inc(hid_made, 1)

            def add_expert(e):
                dve.wait_ge(down_made, e + 1)
                if e >= 1:
                    dve.wait_ge(expert_added, e)
                for b in range(B):
                    last = V.scalar_tensor_tensor(x1[:, b, :], banks[:, 6 + e % 2, P * b:P * b + P], weight[:, b, e:e + 1],
                                                  x1[:, b, :], ALU.mult, ALU.add)
                last.then_inc(expert_added, 1)

            for i in range(2 * E):
                hidden(i)
                if i == 1:
                    dve.wait_ge(rank_made, 1)
                    V.tensor_scalar(chosen, banks[:, 7, 0:B * E].rearrange("p (b e) -> p b e", e=E), float(CAPACITY), 0.5,
                                    ALU.is_le, ALU.mult).then_inc(l_read_dve, 3)
                    dve.wait_ge(l_read_dve, 5)
                    link(V.tensor_tensor(weight, weight, chosen, ALU.mult))
                if i >= 3 and i % 2:
                    add_expert(i // 2 - 1)
            add_expert(E - 1)

        @block.gpsimd
        def _(pool):
            G = nc.gpsimd
            chain = [0]

            def link(ins):
                chain[0] += 1
                ins.then_inc(pool_chain, 1)
                pool.wait_ge(pool_chain, chain[0])

            def rsqrt(k):
                pool.wait_ge(stats_made, k + 1)
                link(G.tensor_scalar(rstd[:, :], mv[:, :, 1], EPS, None, ALU.add))
                G.tensor_tensor(rstd[:, :], rstd[:, :], halfneg[:, :], ALU.pow).then_inc(rstd_made, 1)

            def mask_offset(b):
                pool.wait_ge(mask_in, 16 * (b + 1))
                if b >= 2:
                    pool.wait_ge(score_made, 2 * STEPS * GROUPS * (b - 1))
                G.tensor_scalar(neg[b % 2][:, :], mask_s[:, :], -NEG, NEG, ALU.mult, ALU.add).then_inc(neg_made, 1)

            def gate(t, half):
                u, s = divmod(t, STEPS)
                b = u // GROUPS
                pool.wait_ge(exp_made, 2 * t + half + 1)
                if half == 0:
                    if t >= 2:
                        pool.wait_ge(pv_done, t - 1)
                    if t % (GROUPS * STEPS) == 0:
                        pool.wait_ge(work_read_act, reads_before[("gT", b, NC - 1)][1])
                j = 2 * half
                G.tensor_tensor(probg[t % 2][:, j, :].rearrange("p (h q) -> p h q", h=GH),
                                prob[t % 2][:, j, :].rearrange("p (h q) -> p h q", h=GH),
                                gT[b % 2][:, KT_TICK * s + j, :].unsqueeze(1).broadcast_to([P, GH, P]),
                                ALU.mult).then_inc(gated_pool, 1)

            def split_k(b, part):
                o = S2 // 4 * part
                sl = slice(o, o + S2 // 4)
                if part == 0:
                    pool.wait_ge(work_read_act, reads_before[("k", b, NC - 1)][1])
                link(G.tensor_tensor(kf(b, sl), kf(b, sl), kpart[0][:, sl], ALU.subtract))
                link(G.tensor_copy(kpart[1][:, sl], kf(b, sl)))
                last = G.tensor_tensor(kpart[2][:, sl], kf(b, sl), kpart[1][:, sl], ALU.subtract)
                if part == 3:
                    last.then_inc(k_parts_made, 1)

            link(G.memset(identf[:, :], 0.0))
            link(G.affine_select(out=identf[:, :], in_=identf[:, :], compare_op=ALU.not_equal, fill=1.0, base=0,
                                 pattern=[[-1, P]], channel_multiplier=1))
            link(G.memset(kaug[0][64:AUG, :, :].rearrange("p a b -> p (a b)").bitcast(U32), ONES_BF))
            pool.wait_ge(dve_chain, 1)
            rsqrt(0)
            for h in range(GH):
                link(G.tensor_copy(negident[:, h, :], identf[:, :]))
            link(G.memset(headsel[:, :], 1.0))
            link(G.memset(quadsel[:, :], 0.0))
            for j in range(4):
                v = headsel[32 * j:32 * j + 32, :]
                link(G.affine_select(out=v, in_=v, compare_op=ALU.is_ge, fill=0.0, base=0, pattern=[[-8, GH]], channel_multiplier=1))
                link(G.affine_select(out=v, in_=v, compare_op=ALU.is_ge, fill=0.0, base=7, pattern=[[8, GH]], channel_multiplier=-1))
                link(G.memset(quadsel[32 * j:32 * j + 1, :], 1.0))
            mask_offset(0)
            pool.wait_ge(neg_made, 1)
            link(G.memset(kaug[1][64:AUG, :, :].rearrange("p a b -> p (a b)").bitcast(U32), ONES_BF))
            link(G.memset(kaug[2][64:AUG, :, :].rearrange("p a b -> p (a b)").bitcast(U32), ONES_BF))
            for t in range(TICKS):
                b, i = divmod(t, GROUPS * STEPS)
                gate(t, 0)
                gate(t, 1)
                if b + 1 < B:
                    if i == 0:
                        mask_offset(b + 1)
                    if 7 <= i <= 8:
                        split_k(b + 1, 2 * (i - 7))
                        split_k(b + 1, 2 * (i - 7) + 1)
            rsqrt(1)
            link(G.memset(rms_half, -0.5))
            pool.wait_ge(sums_made, 1)
            link(G.tensor_scalar(rms_inv, rms_sum, 1.0 / HV, EPS, ALU.mult, ALU.add))
            G.tensor_tensor(rms_inv, rms_inv, rms_half, ALU.pow).then_inc(rms_made, 1)
            rsqrt(2)


_NAMES = ['x', 'ctx_1024', 'fside_BxSxS2_0', 'mask_BxSxS2_ik1', 'L0_xattn_wq_k', 'L0_xattn_wq_b', 'L0_xattn_wk_k',
          'L0_xattn_wk_b', 'L0_xattn_wv_k', 'L0_xattn_wv_b', 'L0_xattn_wo_k', 'L0_xattn_wo_b', 'L0_attn_Wq', 'L0_attn_Wk',
          'L0_attn_Wv', 'L0_attn_Wg', 'L0_attn_gk_w1', 'L0_attn_gk_w2', 'L0_attn_gk_b', 'L0_attn_Wo', 'L0_attn_rms_w',
          'L0_ffn_router_w', 'L0_ffn_router_b', 'L0_ffn_W', 'L0_ffn_V', 'L0_ffn_W_out']


def kernel(**inputs):
    import numpy as np
    import concourse.bacc as bacc
    from concourse.bass_utils import run_bass_kernel_spmd

    nc = bacc.Bacc("TRN2", target_bir_lowering=False, num_devices=1)
    arrays, args = {}, []
    for name in _NAMES:
        a = np.asarray(inputs[name])
        a = np.ascontiguousarray(a.T if name == "L0_ffn_router_w" else a)
        arrays["in_" + name] = a
        args.append(nc.dram_tensor("in_" + name, a.shape, mybir.dt.from_np(a.dtype), kind="ExternalInput").ap())
    s, t = np.arange(P)[:, None], np.arange(32)[None, :]
    differ = (s % 32) ^ t
    levels = [(differ >= c) & (differ < 2 * c) & (t > s % 32) for c in LEVELS[2:]] + [differ == 0]
    blocks = np.arange(P)[:, None] // 32 == np.arange(P)[None, :] // 32
    upto = s <= np.arange(P)[None, :]
    arrays["shape_consts"] = np.concatenate([*levels, blocks, upto, np.tile(np.arange(8), (P, 1))], axis=1).astype(np.float32)
    args.append(nc.dram_tensor("shape_consts", (P, CONSTS), F32, kind="ExternalInput").ap())
    out = nc.dram_tensor("out_x", inputs["x"].shape, F32, kind="ExternalOutput").ap()
    perceiver_kernel(nc, *args, out)
    r = run_bass_kernel_spmd(nc, [arrays], core_ids=[0])
    return r.results[0]["out_x"]
```

```python
from contextlib import ExitStack

import concourse.bass as bass
from concourse import mybir

F32 = mybir.dt.float32
BF16 = mybir.dt.bfloat16
I32 = mybir.dt.int32
U32 = mybir.dt.uint32
ALU = mybir.AluOpType
ACT = mybir.ActivationFunctionType
AX_X = mybir.AxisListType.X

P = 128
EPS = 1e-5
NEG = -998244352.0
LOWEST = -3.0e38


LEVELS = (64, 32, 16, 8, 4, 2, 1)
NLEVEL = len(LEVELS)
NDIAG = 6
CONSTS = NDIAG * 32 + 2 * P + 8

HEADS = 16
GH = 4
GROUPS = HEADS // GH
KT_TICK = 4
LEAD = GH + 2
PAIRS = [(0, 0), (0, 1), (1, 0), (1, 1), (0, 2), (2, 0)]
ZROW = 64
AUG = 68


def perceiver_kernel(nc, x, ctx, fside, mask, wq, bq, wk, bk, wv, bv, wo, bo,
                     gWq, gWk, gWv, gWg, gw1, gw2, gb, gWo, grms,
                     rw, rb, eW, eV, eWo, shape_consts, fill, out):
    B, S, D = x.shape
    S2 = ctx.shape[1]
    DH = D // HEADS
    NK = S2 // P
    NC = S2 // 512
    UNITS = B * GROUPS
    STEPS = NK // KT_TICK
    TICKS = UNITS * STEPS
    HEAD_SEQ = UNITS * GH
    SCALE = float(DH) ** -0.5

    es = ExitStack()
    with es:
        def sb(name, shape, dt=F32):
            return es.enter_context(nc.sbuf_tensor(name, shape, dt))

        def pb(name, shape, dt=F32):
            return es.enter_context(nc.psum_tensor(name, shape, dt))

        def sem(name):
            return es.enter_context(nc.semaphore(name))

        identf = sb("identf", [P, P])
        negident = sb("negident", [P, GH, P], BF16)
        identb = negident[:, 0, :]
        ones32 = sb("ones32", [P, 32])
        headsel = sb("headsel", [P, GH])
        quadsel = sb("quadsel", [P, 1])
        halfneg = sb("halfneg", [P, B])

        x1 = sb("x1", [P, B, D])
        xh = sb("xh", [P, B, D])
        xhT = sb("xhT", [P, B * P])
        bnst = sb("bnst", [P, B, 6])
        mv = sb("mv", [P, B, 2])
        rstd = sb("rstd", [P, B])

        wq_s, wk_s, wv_s = sb("wq_s", [P, D]), sb("wk_s", [P, D]), sb("wv_s", [P, D])
        wo_s = sb("wo_s", [P, GROUPS, D])
        bv_s, bo_s = sb("bv_s", [P, D]), sb("bo_s", [P, D])
        bq_s, bk_s, bqs = sb("bq_s", [P, 1]), sb("bk_s", [P, 1]), sb("bqs", [P, 1])

        qparts = sb("qparts", [P, 3, B * P], BF16)
        qpart = [qparts[:, i, :] for i in range(3)]
        kparts = sb("kparts", [P, 3, S2], BF16)
        kpart = [kparts[:, i, :] for i in range(3)]
        qaug = sb("qaug", [AUG, HEADS, B, P], BF16)
        kaug = [sb(f"kaug{i}", [AUG, GH, S2], BF16) for i in range(3)]

        ctx_s = sb("ctx_s", [P, NK, D])
        ctxT = sb("ctxT", [P, S2])
        v_s = [sb(f"v_s{i}", [P, NK, D]) for i in range(2)]
        f_s = sb("f_s", [P, S2])
        gT = [sb(f"gT{i}", [P, NK, P]) for i in range(2)]
        mask_s = sb("mask_s", [P, S2], I32)
        neg = [sb(f"neg{i}", [P, S2], BF16) for i in range(2)]
        junk = sb("junk", [P, 2, 512], BF16)

        prob = [sb(f"prob{i}", [P, KT_TICK, GH * P]) for i in range(2)]
        probg = [sb(f"probg{i}", [P, KT_TICK, GH * P]) for i in range(2)]
        def kf(b, cols):
            return (prob[0][:, :, :].rearrange("p t q -> p (t q)") if b == 0 else f_s)[:, cols]
        mx = sb("mx", [P, 2, GH, NC])
        mtop = sb("mtop", [P, GH])
        mres = sb("mres", [P, GH])
        mpart = sb("mpart", [P, GH, 4], BF16)
        numer = sb("numer", [P, GH, P])
        qf = numer[:, :, :].rearrange("p h q -> p (h q)")
        denom = sb("denom", [P, GH, P])
        rden = sb("rden", [P, GH])
        head_out = sb("head_out", [P, GH, P])

        banks = pb("banks", [P, 8, 512])
        score = [banks[:, 0:2, :], banks[:, 2:4, :]]
        work = [banks[:, 4, :], banks[:, 5, :]]
        num_ps, den_ps = banks[:, 6, :], banks[:, 7, :]

        LH, HK = 4, gWq.shape[1] // 4
        HV = gWv.shape[1] // LH
        DV, LR, E, HID = gWv.shape[1], gw1.shape[1], eW.shape[0], eW.shape[2]
        CAPACITY = 2 * B * S * 2 // E
        N = B * P
        cst = sb("cst", [P, CONSTS])
        levelsel = cst[:, 0:NDIAG * 32].rearrange("p (l t) -> p l t", t=32)
        blocksel = cst[:, NDIAG * 32:NDIAG * 32 + P].rearrange("p (m t) -> p m t", t=32)
        upto = cst[:, NDIAG * 32 + P:NDIAG * 32 + 2 * P]
        expert_no = cst[:, NDIAG * 32 + 2 * P:CONSTS]
        ones_sq = sb("ones_sq", [P, P])

        def flat(t):
            return t[:, :, :].rearrange("p a b -> p (a b)")

        small = flat(v_s[0])
        free = [0]

        def carve(n):
            free[0] += n
            return small[:, free[0] - n:free[0]]

        wqk_l, wvg_l, wo_l = carve(2 * P), carve(2 * DV), carve(2 * D).rearrange("p (a n) -> p a n", a=2)
        w1_l, w2_l, b_l, rms_l = carve(LR), carve(P)[0:LR, :], carve(1), carve(HV)
        rw_s, rb_s = carve(E), carve(E)
        logit = carve(B * E).rearrange("p (b e) -> p b e", e=E)
        top = carve(B * E).rearrange("p (b e) -> p b e", e=E)
        topno = carve(B * E).rearrange("p (b e) -> p b e", e=E)
        topnof = carve(B * E).rearrange("p (b e) -> p b e", e=E)
        pick = [carve(B * E).rearrange("p (b e) -> p b e", e=E) for _ in range(2)]
        chosen = carve(B * E).rearrange("p (b e) -> p b e", e=E)
        weight = carve(B * E).rearrange("p (b e) -> p b e", e=E)
        ratio, top_p = carve(B), [carve(B) for _ in range(2)]
        rms_sum, rms_inv, rms_half = carve(B * LH), carve(B * LH), carve(B * LH)
        qT, kT = flat(prob[0])[:, 0:N], flat(prob[0])[:, N:2 * N]
        decay, cum = flat(prob[0])[:, 2 * N:3 * N], flat(prob[0])[:, 3 * N:4 * N]
        val = flat(prob[1])[:, 0:B * DV].rearrange("p (b v) -> p b v", v=DV)
        zgate = flat(prob[1])[:, B * DV:2 * B * DV].rearrange("p (b v) -> p b v", v=DV)
        expo = [flat(probg[0])[:, N * i:N * i + N] for i in range(2)]
        lowT = flat(probg[0])[0:LR, 2 * N:3 * N]
        lnexp = flat(probg[0])[:, 3 * N:4 * N]
        scaled = [flat(gT[i // 4])[:, N * (i % 4):N * (i % 4) + N] for i in range(NLEVEL)]
        attT = flat(probg[1]).rearrange("p (c t) -> p c t", t=P)
        picked = kparts[:, :, :].rearrange("p a b -> p (a b)").bitcast(F32).rearrange(
            "p (c l t) -> p c l t", l=NDIAG, t=32)
        diag = flat(gT[1])[:, 3 * N:4 * N].rearrange("p (c t) -> p c t", t=32)
        mixed = flat(v_s[1])[:, 0:B * DV].rearrange("p (b v) -> p b v", v=DV)
        squares = flat(v_s[1])[:, B * DV:2 * B * DV].rearrange("p (b v) -> p b v", v=DV)
        mixedT = flat(probg[0])[:, 0:2 * N].rearrange("p (a n) -> p a n", a=2)
        eW_s = flat(ctx_s).rearrange("p (e f) -> p e f", e=E)
        eV_s = f_s[:, :].rearrange("p (e f) -> p e f", e=E)
        eWo_s = mask_s[:, :].bitcast(F32).rearrange("p (e a d) -> p e a d", e=E, a=2)
        tanhs = [flat(prob[0])[:, N * i:N * i + N] for i in range(2)]
        gated = [flat(prob[0])[:, N * (2 + i):N * (2 + i) + N] for i in range(2)]
        hidT = [flat(prob[1])[:, N * i:N * i + N] for i in range(4)]

        q_dram = nc.dram_tensor("q_dram", [3, P, B * P], BF16, kind="Internal").ap()
        k_dram = nc.dram_tensor("k_dram", [B, 3, P, S2], BF16, kind="Internal").ap()

        x_in, w_in, wv_in, wo_in, bo_in = sem("x_in"), sem("w_in"), sem("wv_in"), sem("wo_in"), sem("bo_in")
        ctx_in = [sem(f"ctx_in{c}") for c in range(NC)]
        f_in, mask_in, qfill_in = sem("f_in"), sem("mask_in"), sem("qfill_in")
        qaug_in = sem("qaug_in")
        q_stored, k_stored = sem("q_stored"), sem("k_stored")
        kaug_in = [sem(f"kaug_in{i}") for i in range(3)]
        pool_chain, dve_chain, act_chain = sem("pool_chain"), sem("dve_chain"), sem("act_chain")
        stats_made, rstd_made, xh_made = sem("stats_made"), sem("rstd_made"), sem("xh_made")
        work_filled, work_read_dve, work_read_act = sem("work_filled"), sem("work_read_dve"), sem("work_read_act")
        q_parts_made = sem("q_parts_made")
        k_half_made = sem("k_half_made")
        k_parts_made = sem("k_parts_made")
        neg_made = sem("neg_made")
        score_made, exp_made = sem("score_made"), sem("exp_made")
        gated_pool, gated_dve = sem("gated_pool"), sem("gated_dve")
        pv_done, weights_summed = sem("pv_done"), sem("weights_summed")
        unit_scaled = sem("unit_scaled")
        unit_added = sem("unit_added")
        mpart_made = sem("mpart_made")
        numer_made, denom_made = sem("numer_made"), sem("denom_made")
        cst_in, l_in, e_in = sem("cst_in"), sem("l_in"), sem("e_in")
        attention_done = sem("attention_done")
        l_proj, l_read_act, l_read_dve = sem("l_proj"), sem("l_read_act"), sem("l_read_dve")
        abs_made, expo_made, decayed, scaled_made = sem("abs_made"), sem("expo_made"), sem("decayed"), sem("scaled_made")
        pairs_made, picked_read, off_read, att_made = sem("pairs_made"), sem("picked_read"), sem("off_read"), sem("att_made")
        mixed_made, squared, sums_made, rms_made = sem("mixed_made"), sem("squared"), sem("sums_made"), sem("rms_made")
        gated_made, mixT_made, mixT_read, l_out = sem("gated_made"), sem("mixT_made"), sem("mixT_read"), sem("l_out")
        x_added = sem("x_added")
        logits_made, ratio_in, ratio_made, chosen_made, rank_made = (sem("logits_made"), sem("ratio_in"), sem("ratio_made"),
                                                                    sem("chosen_made"), sem("rank_made"))
        up_made, tanh_made, hid_made, down_made, expert_added = (sem("up_made"), sem("tanh_made"), sem("hid_made"),
                                                                 sem("down_made"), sem("expert_added"))
        out_done = sem("out_done")

        def prep(b, kind, c):
            return (kind, b, c)

        def tick_work(t):
            u, s = divmod(t, STEPS)
            b, i = divmod(t, GROUPS * STEPS)
            items = []
            if b + 1 < B:
                if 1 <= i <= 4:
                    items.append(("k", b + 1, i - 1))
                if i < 4:
                    items.append(("ctxT", b + 1, i))
                if 5 <= i <= 8:
                    items.append(("v", b + 1, i - 5))
                if 9 <= i <= 12:
                    items.append(("gT", b + 1, i - 9))
            if s == STEPS - 1 and u + 1 < UNITS:
                items.append(("mrow", u + 1, 0))
            if u >= 1 and s == 1:
                items.append(("den", u - 1, 0))
            if u >= 1 and s == 2:
                items.append(("wo", u - 1, 0))
            return items

        def tick_max(t, half):
            n = t + LEAD
            return [("max", n, c) for c in range(NC // 2 * half, NC // 2 * (half + 1))] if n < HEAD_SEQ else []

        start_work = [("xhT", 0, 0), ("ctxT", 0, 0), ("q", 0, 0), ("k", 0, 0)]
        for c in range(1, NC):
            start_work += [("ctxT", 0, c), ("k", 0, c)]
        start_work += [("v", 0, c) for c in range(NC)] + [("gT", 0, c) for c in range(NC)]
        start_work += [("max", n, c) for n in range(GH) for c in range(NC)] + [("mrow", 0, 0)]
        start_work += [("max", n, c) for n in range(GH, LEAD) for c in range(NC)]
        end_work = [("den", UNITS - 1, 0), ("wo", UNITS - 1, 0)]
        all_work = start_work + [w for t in range(TICKS) for w in tick_max(t, 0) + tick_work(t) + tick_max(t, 1)] + end_work
        slot = {w: n for n, w in enumerate(all_work)}
        BY_ACT = ("ctxT", "q", "k", "gT", "mrow", "xhT", "wo")
        reads_before = {}
        counts = {"act": 0, "dve": 0}
        for w in all_work:
            who = "act" if w[0] in BY_ACT else "dve"
            counts[who] += 1
            reads_before[w] = (who, counts[who])

        def bank_of(w):
            return work[slot[w] % 2]

        def await_bank(pe, w):
            if slot[w] >= 2:
                who, n = reads_before[all_work[slot[w] - 2]]
                pe.wait_ge(work_read_act if who == "act" else work_read_dve, n)

        def await_filled(eng, w):
            eng.wait_ge(work_filled, slot[w] + 1)

        block = es.enter_context(nc.Block())

        @block.sync
        def _(sp):
            def load_ctx(b):
                for c in range(NC):
                    sp.dma_start(ctx_s[:, 4 * c:4 * c + 4, :],
                                 ctx[b, 512 * c:512 * c + 512, :].rearrange("(t p) d -> p t d", p=P)).then_inc(ctx_in[c], 16)

            sp.dma_start(x1[:, :, :], x.rearrange("b s d -> s b d")).then_inc(x_in, 16)
            load_ctx(0)
            sp.dma_start(wk_s[:, :], wk).then_inc(w_in, 16)
            sp.dma_start(wq_s[:, :], wq).then_inc(w_in, 16)
            sp.dma_start(bk_s[:, :], bk.rearrange("(d a) -> d a", a=1)).then_inc(w_in, 16)
            sp.dma_start(bq_s[:, :], bq.rearrange("(d a) -> d a", a=1)).then_inc(w_in, 16)
            sp.dma_start(wv_s[:, :], wv).then_inc(wv_in, 16)
            sp.dma_start(bv_s[:, :], bv.partition_broadcast(P)).then_inc(wv_in, 16)
            zeros, ones = fill[0:1, :], fill[1:2, :]
            sp.dma_start(qaug[48:AUG, :, :, :].rearrange("p h b q -> p (h b q)"),
                         zeros.broadcast_to([AUG - 48, GH * S2])).then_inc(qfill_in, 16)

            def fill_k(i):
                sp.dma_start(kaug[i][48:64, :, :].rearrange("p h n -> p (h n)"),
                             zeros.broadcast_to([16, GH * S2])).then_inc(kaug_in[i], 16)
                sp.dma_start(kaug[i][64:AUG, :, :].rearrange("p h n -> p (h n)"),
                             ones.broadcast_to([AUG - 64, GH * S2])).then_inc(kaug_in[i], 16)

            fill_k(0)
            sp.dma_start(mask_s[:, :], mask[0]).then_inc(mask_in, 16)

            def stack_q():
                sp.dma_start(q_dram.rearrange("i p n -> p i n"), qparts[:, :, :]).then_inc(q_stored, 16)
                sp.wait_ge(q_stored, 16)
                for c, (qi, _) in enumerate(PAIRS):
                    sp.dma_start(qaug[8 * c:8 * c + 8, :, :, :].rearrange("d h b q -> d h (b q)"),
                                 q_dram[qi].rearrange("(h d) n -> d h n", d=DH)).then_inc(qaug_in, 16)

            def store_k(b):
                for c in range(NC):
                    cols = slice(512 * c, 512 * c + 512)
                    sp.wait_ge(k_parts_made, NC * b + c + 1)
                    sp.dma_start(k_dram[b].rearrange("i p n -> p i n")[:, :, cols], kparts[:, :, cols]).then_inc(k_stored, 16)
                sp.wait_ge(k_stored, 16 * NC * (b + 1))

            def stack_k(u):
                b, g = divmod(u, GROUPS)
                if g == 0:
                    store_k(b)
                if u >= 3:
                    sp.wait_ge(score_made, 2 * STEPS * (u - 2))
                for c, (_, ki) in enumerate(PAIRS):
                    sp.dma_start(kaug[u % 3][8 * c:8 * c + 8, :, :],
                                 k_dram[b, ki, 32 * g:32 * g + 32, :].rearrange("(h d) n -> d h n", d=DH)).then_inc(
                        kaug_in[u % 3], 16)

            sp.wait_ge(q_parts_made, 1)
            stack_q()
            stack_k(0)
            sp.dma_start(f_s[:, :], fside[0]).then_inc(f_in, 16)
            sp.dma_start(bo_s[:, :], bo.partition_broadcast(P)).then_inc(bo_in, 16)
            sp.dma_start(cst[:, :], shape_consts).then_inc(cst_in, 16)
            fill_k(1)
            fill_k(2)
            for g in range(GROUPS):
                sp.dma_start(wo_s[32 * g:32 * g + 32, :, :], wo.rearrange("(g r) n -> r g n", r=32)).then_inc(wo_in, 16)
            for u in range(1, UNITS):
                b, g = divmod(u, GROUPS)
                if g == 1 and b + 1 < B:
                    sp.wait_ge(work_filled, slot[("ctxT", b, NC - 1)] + 1)
                    load_ctx(b + 1)
                    sp.wait_ge(neg_made, b + 1)
                    sp.dma_start(mask_s[:, :], mask[b + 1]).then_inc(mask_in, 16)
                if g == 0:
                    sp.wait_ge(k_parts_made, NC * (b + 1))
                    sp.dma_start(f_s[:, :], fside[b]).then_inc(f_in, 16)
                stack_k(u)
            sp.wait_ge(pv_done, (B - 1) * GROUPS * STEPS)
            for dst, src in ((wqk_l[:, 0:P], gWq), (wqk_l[:, P:2 * P], gWk), (wvg_l[:, 0:DV], gWv), (wvg_l[:, DV:], gWg),
                             (wo_l, gWo.rearrange("(a p) n -> p a n", p=P)), (w1_l, gw1), (w2_l, gw2),
                             (b_l, gb.rearrange("(d a) -> d a", a=1)), (rms_l, grms.partition_broadcast(P)),
                             (rw_s, rw), (rb_s, rb.partition_broadcast(P))):
                sp.dma_start(dst, src).then_inc(l_in, 16)
            sp.wait_ge(neg_made, B)
            sp.dma_start(eWo_s, eWo.rearrange("e (a p) d -> p e a d", p=P)).then_inc(e_in, 16)
            sp.wait_ge(work_filled, slot[("gT", B - 1, NC - 1)] + 1)
            sp.dma_start(eW_s, eW.rearrange("e d f -> d e f")).then_inc(e_in, 16)
            sp.dma_start(eV_s, eV.rearrange("e d f -> d e f")).then_inc(e_in, 16)
            sp.wait_ge(expert_added, E)
            sp.dma_start(out.rearrange("b s d -> s b d"), x1[:, :, :]).then_inc(out_done, 16)
            sp.wait_ge(out_done, 16)

        @block.tensor
        def _(pe):
            T = nc.tensor

            def transposes(w, src):
                await_bank(pe, w)
                for j in range(4):
                    last = T.transpose(bank_of(w)[:, P * j:P * j + P], src(j), identf[:, :])
                last.then_inc(work_filled, 1)

            def do_work(w):
                kind, a, c = w
                bank = bank_of(w)
                if kind == "xhT":
                    pe.wait_ge(pool_chain, 2)
                    pe.wait_ge(xh_made, 1)
                    transposes(w, lambda j: xh[:, j, :])
                elif kind == "ctxT":
                    pe.wait_ge(ctx_in[c], 16 * (a + 1))
                    transposes(w, lambda j: ctx_s[:, 4 * c + j, :])
                elif kind == "gT":
                    pe.wait_ge(f_in, 16 * (a + 1))
                    transposes(w, lambda j: f_s[:, 512 * c + P * j:512 * c + P * j + P])
                elif kind == "q":
                    pe.wait_ge(w_in, 64)
                    await_bank(pe, w)
                    pe.wait_ge(work_read_act, reads_before[("xhT", 0, 0)][1])
                    T.matmul(bank[:, :], wq_s[:, :], xhT[:, :], start=True, stop=True).then_inc(work_filled, 1)
                elif kind == "k":
                    await_bank(pe, w)
                    pe.wait_ge(work_read_act, reads_before[("ctxT", a, c)][1])
                    T.matmul(bank[:, :], wk_s[:, :], ctxT[:, 512 * c:512 * c + 512], start=True, stop=True).then_inc(work_filled, 1)
                elif kind == "v":
                    if a == 0 and c == 0:
                        pe.wait_ge(wv_in, 32)
                    await_bank(pe, w)
                    for j in range(4):
                        o = 512 * c + P * j
                        last = T.matmul(bank[:, P * j:P * j + P], ctxT[:, o:o + P], wv_s[:, :], start=True, stop=True)
                    last.then_inc(work_filled, 1)
                elif kind == "max":
                    u, h = divmod(a, GH)
                    b, g = divmod(u, GROUPS)
                    if c == 0:
                        pe.wait_ge(qaug_in, 16 * len(PAIRS))
                        pe.wait_ge(qfill_in, 16)
                        pe.wait_ge(kaug_in[u % 3], 16 * (2 + len(PAIRS) * (u // 3 + 1)))
                    await_bank(pe, w)
                    T.matmul(bank[:, :], qaug[0:ZROW + 1, GH * g + h, b, :],
                             kaug[u % 3][0:ZROW + 1, h, 512 * c:512 * c + 512], start=True, stop=True).then_inc(work_filled, 1)
                elif kind == "mrow":
                    await_bank(pe, w)
                    pe.wait_ge(mpart_made, a + 1)
                    for h in range(GH):
                        last = T.matmul(bank[ZROW:AUG, P * h:P * h + P], mpart[:, h, :], identb, start=True, stop=True,
                                        tile_position=(0, ZROW))
                    last.then_inc(work_filled, 1)
                elif kind == "den":
                    await_bank(pe, w)
                    pe.wait_ge(denom_made, a + 1)
                    for h in range(GH):
                        last = T.matmul(bank[:, h:h + 1], denom[:, h, :], quadsel[:, :], start=True, stop=True)
                    last.then_inc(work_filled, 1)
                elif kind == "wo":
                    g = a % GROUPS
                    if a == 0:
                        pe.wait_ge(wo_in, 64)
                    await_bank(pe, w)
                    pe.wait_ge(numer_made, a + 1)
                    for h in range(GH):
                        last = T.matmul(bank[:, P * h:P * h + P], numer[:, h, :], wo_s[:, g, :], start=True, stop=True)
                    last.then_inc(work_filled, 1)

            def scores(t, half):
                u, s = divmod(t, STEPS)
                b, g = divmod(u, GROUPS)
                e = 2 * t + half
                maxima = tick_max(t, half)
                for w in maxima[:1]:
                    do_work(w)
                if e >= 2:
                    pe.wait_ge(exp_made, e - 1)
                if s == 0 and half == 0:
                    pe.wait_ge(work_read_act, reads_before[("mrow", u, 0)][1])
                    pe.wait_ge(neg_made, b + 1)
                for j in range(2):
                    kt = KT_TICK * s + 2 * half + j
                    T.matmul(score[half][:, j, :], neg[b % 2][:, P * kt:P * kt + P],
                             negident[:, :, :].rearrange("p h q -> p (h q)"), start=True, stop=False)
                    for h in range(GH):
                        last = T.matmul(score[half][:, j, P * h:P * h + P], kaug[u % 3][:, h, P * kt:P * kt + P],
                                        qaug[:, GH * g + h, b, :], start=False, stop=(h == GH - 1))
                    if j == 0:
                        for w in maxima[1:]:
                            do_work(w)
                last.then_inc(score_made, 1)

            def weights_sum(t):
                u, s = divmod(t, STEPS)
                b, g = divmod(u, GROUPS)
                pe.wait_ge(exp_made, 2 * t + 2)
                if s == 0 and u >= 1:
                    pe.wait_ge(denom_made, u)
                for j in range(KT_TICK):
                    last = T.matmul(den_ps[32 * j:32 * j + 32, :], ones32[:, :], prob[t % 2][:, j, :],
                                    start=(s == 0), stop=(s == STEPS - 1), tile_position=(0, 32 * j))
                last.then_inc(weights_summed, 1)

            def values(t):
                u, s = divmod(t, STEPS)
                b, g = divmod(u, GROUPS)
                pe.wait_ge(gated_pool, 2 * t + 2)
                pe.wait_ge(gated_dve, 2 * t + 2)
                if s == 0:
                    pe.wait_ge(work_read_dve, reads_before[("v", b, NC - 1)][1])
                    if u >= 1:
                        pe.wait_ge(numer_made, u)
                for j in range(KT_TICK):
                    last = T.matmul(num_ps[32 * j:32 * j + 32, :], v_s[b % 2][:, KT_TICK * s + j, 32 * g:32 * g + 32],
                                    probg[t % 2][:, j, :], start=(s == 0), stop=(s == STEPS - 1), tile_position=(0, 32 * j))
                last.then_inc(pv_done, 1)

            for w in start_work:
                do_work(w)
            for t in range(TICKS):
                scores(t, 0)
                if t >= 1:
                    weights_sum(t - 1)
                for w in tick_work(t):
                    do_work(w)
                scores(t, 1)
                if t >= 1:
                    values(t - 1)
            weights_sum(TICKS - 1)
            values(TICKS - 1)
            for w in end_work:
                do_work(w)

            def to_features(n):
                pe.wait_ge(xh_made, n + 1)
                for b in range(B):
                    last = T.transpose(banks[:, 0, P * b:P * b + P], xh[:, b, :], identf[:, :])
                last.then_inc(l_proj, 1)

            to_features(1)
            pe.wait_ge(l_in, 16 * 11)
            pe.wait_ge(l_read_act, 1)
            T.matmul(banks[0:LR, 1, :], w1_l, xhT[:, :], start=True, stop=True).then_inc(l_proj, 1)
            T.matmul(banks[:, 2, :], wqk_l[:, 0:P], xhT[:, :], start=True, stop=True)
            T.matmul(banks[:, 3, :], wqk_l[:, P:2 * P], xhT[:, :], start=True, stop=True).then_inc(l_proj, 1)
            pe.wait_ge(l_read_act, 2)
            T.matmul(banks[:, 0, :], w2_l, lowT, start=True, stop=True).then_inc(l_proj, 1)
            for b in range(B):
                last = T.matmul(banks[:, 4 + b, :], xhT[:, P * b:P * b + P], wvg_l, start=True, stop=True)
            last.then_inc(l_proj, 1)
            pe.wait_ge(l_read_act, 5)
            pe.wait_ge(l_read_dve, 2)
            for r in range(B // 2):
                if r == 1:
                    pe.wait_ge(picked_read, 1)
                    pe.wait_ge(off_read, 1)
                for b in (2 * r, 2 * r + 1):
                    for l in range(NDIAG):
                        if r == 0 and b == 0:
                            pe.wait_ge(scaled_made, NLEVEL if l == NDIAG - 1 else l + 3)
                        for m in range(4):
                            for h in range(LH):
                                kd = slice(HK * h, HK * h + HK)
                                o = P * b + 32 * m
                                left, right = (kT, qT) if l == NDIAG - 1 else (scaled[l + 2], scaled[l + 2])
                                T.matmul(banks[32 * m:32 * m + 32, LH * (b % 2) + h, 32 * l:32 * l + 32],
                                         left[kd, o:o + 32], right[kd, o:o + 32], start=True, stop=True,
                                         tile_position=(HK * h, 32 * m))
                    for h in range(LH):
                        kd = slice(HK * h, HK * h + HK)
                        bank = banks[:, LH * (b % 2) + h, :]
                        for m in (0, 64):
                            T.matmul(bank[m:m + 32, 256:288], scaled[1][kd, P * b + m:P * b + m + 32],
                                     scaled[1][kd, P * b + m + 32:P * b + m + 64], start=True, stop=True,
                                     tile_position=(HK * h, m))
                    for h in range(LH):
                        kd = slice(HK * h, HK * h + HK)
                        last = T.matmul(banks[0:64, LH * (b % 2) + h, 192:256], scaled[0][kd, P * b:P * b + 64],
                                        scaled[0][kd, P * b + 64:P * b + P], start=True, stop=True,
                                        tile_position=(HK * h, 0))
                last.then_inc(pairs_made, 1)
            pe.wait_ge(off_read, 2)
            for b in range(B):
                for h in range(LH):
                    o = DV * (b % 2) + HV * h
                    last = T.matmul(banks[:, b // 2, o:o + HV], attT[:, LH * b + h, :], val[:, b, HV * h:HV * h + HV],
                                    start=True, stop=True)
            last.then_inc(mixed_made, 1)
            pe.wait_ge(gated_made, 1)
            for a in range(2):
                for b in range(B):
                    last = T.transpose(banks[:, 2 + a, P * b:P * b + P], mixed[:, b, P * a:P * a + P], identf[:, :])
            last.then_inc(mixT_made, 1)
            pe.wait_ge(mixT_read, 1)
            for b in range(B):
                for a in range(2):
                    last = T.matmul(banks[:, 4, P * b:P * b + P], mixedT[:, a, P * b:P * b + P], wo_l[:, a, :],
                                    start=(a == 0), stop=(a == 1))
            last.then_inc(l_out, 1)

            to_features(2)
            pe.wait_ge(l_read_act, 6)
            for b in range(B):
                last = T.matmul(banks[:, 7, E * b:E * b + E], xhT[:, P * b:P * b + P], rw_s, start=True, stop=True)
            last.then_inc(logits_made, 1)
            pe.wait_ge(e_in, 48)

            def up(i):
                e, a = divmod(i, 2)
                if i >= 3:
                    pe.wait_ge(hid_made, i - 2)
                T.matmul(banks[:, 2 * (i % 3), :], eW_s[:, e, P * a:P * a + P], xhT[:, :], start=True, stop=True)
                T.matmul(banks[:, 2 * (i % 3) + 1, :], eV_s[:, e, P * a:P * a + P], xhT[:, :], start=True, stop=True).then_inc(up_made, 1)

            def down(e):
                pe.wait_ge(hid_made, 2 * e + 2)
                if e >= 2:
                    pe.wait_ge(expert_added, e - 1)
                if e == 1:
                    pe.wait_ge(l_read_dve, 5)
                for b in range(B):
                    for a in range(2):
                        last = T.matmul(banks[:, 6 + e % 2, P * b:P * b + P], hidT[(2 * e + a) % 4][:, P * b:P * b + P],
                                        eWo_s[:, e, a, :], start=(a == 0), stop=(a == 1))
                last.then_inc(down_made, 1)

            for i in range(2 * E):
                if i == 2:
                    pe.wait_ge(chosen_made, 1)
                    for b in range(B):
                        for c in range(b + 1):
                            last = T.matmul(banks[:, 7, E * b:E * b + E], upto if c == b else ones_sq[:, :], chosen[:, c, :],
                                            start=(c == 0), stop=(c == b))
                    last.then_inc(rank_made, 1)
                up(i)
                if i >= 3 and i % 2:
                    down(i // 2 - 1)
            down(E - 1)

        @block.scalar
        def _(act):
            A = nc.scalar
            chain = [0]

            def link(ins):
                chain[0] += 1
                ins.then_inc(act_chain, 1)
                act.wait_ge(act_chain, chain[0])

            def read_work(w):
                kind, a, c = w
                bank = bank_of(w)
                if kind == "q":
                    act.wait_ge(w_in, 64)
                    link(A.activation(bqs[:, :], bq_s[:, :], ACT.Copy, scale=SCALE))
                await_filled(act, w)
                if kind == "xhT":
                    A.copy(xhT[:, :], bank[:, :]).then_inc(work_read_act, 1)
                elif kind == "ctxT":
                    if a >= 1 and c == 0:
                        act.wait_ge(work_filled, slot[("v", a - 1, NC - 1)] + 1)
                    A.copy(ctxT[:, 512 * c:512 * c + 512], bank[:, :]).then_inc(work_read_act, 1)
                elif kind == "gT":
                    A.copy(gT[a % 2][:, 4 * c:4 * c + 4, :].rearrange("p t q -> p (t q)"), bank[:, :]).then_inc(work_read_act, 1)
                elif kind == "q":
                    A.activation(qf, bank[:, :], ACT.Identity, bias=bqs[:, :], scale=SCALE)
                    A.activation(qpart[0], bank[:, :], ACT.Identity, bias=bqs[:, :], scale=SCALE).then_inc(work_read_act, 1)
                elif kind == "k":
                    if a >= 1 and c == 0:
                        act.wait_ge(work_filled, slot[("gT", a - 1, NC - 1)] + 1)
                        act.wait_ge(k_stored, 16 * NC * a)
                    o = 512 * c
                    A.activation(kf(a, slice(o, o + 512)), bank[:, :], ACT.Identity, bias=bk_s[:, :])
                    A.activation(kpart[0][:, o:o + 512], bank[:, :], ACT.Identity, bias=bk_s[:, :]).then_inc(work_read_act, 1)
                elif kind == "wo":
                    act.wait_ge(work_read_dve, reads_before[("den", a, 0)][1])
                    if a >= 1:
                        act.wait_ge(unit_added, a)
                    for h in range(GH):
                        last = A.activation(head_out[:, h, :], bank[:, P * h:P * h + P], ACT.Copy, scale=rden[:, h:h + 1])
                    last.then_inc(work_read_act, 1)
                elif kind == "mrow":
                    b, g = divmod(a, GROUPS)
                    A.copy(qaug[ZROW:AUG, GH * g:GH * g + GH, b, :], bank[ZROW:AUG, :].rearrange(
                        "p (h q) -> p h q", h=GH)).then_inc(work_read_act, 1)

            def exps(t, half):
                act.wait_ge(score_made, 2 * t + half + 1)
                if half == 0 and t >= 2:
                    act.wait_ge(pv_done, t - 1)
                A.activation(prob[t % 2][:, 2 * half:2 * half + 2, :], score[half][:, :, :], ACT.Exp).then_inc(exp_made, 1)

            def denominators(u):
                act.wait_ge(weights_summed, STEPS * (u + 1))
                if u >= 1:
                    act.wait_ge(work_filled, slot[("den", u - 1, 0)] + 1)
                A.copy(denom[:, :, :].rearrange("p h q -> p (h q)"), den_ps[:, :]).then_inc(denom_made, 1)

            for w in start_work:
                if w[0] in BY_ACT:
                    read_work(w)
            for t in range(TICKS):
                exps(t, 0)
                for w in tick_work(t):
                    if w[0] in BY_ACT:
                        read_work(w)
                exps(t, 1)
                if t >= 1 and t % STEPS == 0:
                    denominators(t // STEPS - 1)
            denominators(UNITS - 1)
            read_work(("wo", UNITS - 1, 0))

            act.wait_ge(l_proj, 1)
            A.copy(xhT[:, :], banks[:, 0, :]).then_inc(l_read_act, 1)
            act.wait_ge(l_proj, 2)
            A.copy(lowT, banks[0:LR, 1, :]).then_inc(l_read_act, 1)
            act.wait_ge(l_proj, 3)
            A.activation(qT, banks[:, 2, :], ACT.Copy, scale=float(HK) ** -0.5)
            A.copy(kT, banks[:, 3, :]).then_inc(l_read_act, 1)
            act.wait_ge(l_proj, 4)
            link(A.activation(decay, banks[:, 0, :], ACT.Identity, bias=b_l))
            link(A.activation(lnexp, decay, ACT.Abs))
            link(A.activation(lnexp, lnexp, ACT.Exp, scale=-1.0))
            A.activation(lnexp, lnexp, ACT.Ln, bias=1.0).then_inc(l_read_act, 1)
            for l in range(NLEVEL):
                act.wait_ge(expo_made, l + 1)
                A.activation(expo[l % 2], expo[l % 2], ACT.Exp, scale=1.0 / 16.0).then_inc(decayed, 1)
                if l == 0:
                    act.wait_ge(l_proj, 5)
                    A.copy(val, banks[:, 4:8, 0:DV]).then_inc(l_read_act, 1)
            A.activation(zgate, banks[:, 4:8, DV:2 * DV], ACT.Tanh, scale=0.5).then_inc(squared, 1)
            for r in range(B // 2):
                act.wait_ge(pairs_made, r + 1)
                act.wait_ge(att_made, 1 + r)
                rows = slice(LH * 2 * r, LH * 2 * r + 8)
                A.copy(attT[0:64, rows, 64:128], banks[0:64, :, 192:256])
                A.copy(attT[0:32, rows, 32:64], banks[0:32, :, 256:288])
                A.copy(attT[64:96, rows, 96:128], banks[64:96, :, 256:288]).then_inc(off_read, 1)
            act.wait_ge(mixed_made, 1)
            A.activation(squares.rearrange("p (a b) v -> p a (b v)", a=2), banks[:, 0:2, :], ACT.Square).then_inc(squared, 1)
            act.wait_ge(mixT_made, 1)
            A.copy(mixedT, banks[:, 2:4, :]).then_inc(mixT_read, 1)
            act.wait_ge(l_proj, 6)
            A.copy(xhT[:, :], banks[:, 0, :]).then_inc(l_read_act, 1)
            for i in range(2 * E):
                if i == 1:
                    act.wait_ge(ratio_in, 1)
                    A.activation(ratio, ratio, ACT.Exp).then_inc(ratio_made, 1)
                act.wait_ge(up_made, i + 1)
                if i >= 2:
                    act.wait_ge(hid_made, i - 1)
                A.activation(tanhs[i % 2], banks[:, 2 * (i % 3) + 1, :], ACT.Tanh, scale=0.5).then_inc(tanh_made, 1)

        @block.vector
        def _(dve):
            V = nc.vector
            chain = [0]

            def link(ins):
                chain[0] += 1
                ins.then_inc(dve_chain, 1)
                dve.wait_ge(dve_chain, chain[0])

            def layer_norm(k):
                for b in range(B):
                    last = V.bn_stats(bnst[:, b, :], x1[:, b, :])
                link(last)
                for b in range(B):
                    last = V.bn_aggr(mv[:, b, :], bnst[:, b, :])
                last.then_inc(stats_made, 1)
                dve.wait_ge(rstd_made, k + 1)
                for b in range(B):
                    last = V.tensor_scalar(xh[:, b, :], x1[:, b, :], mv[:, b, 0:1], rstd[:, b:b + 1], ALU.subtract, ALU.mult)
                last.then_inc(xh_made, 1)

            def gate(t, half):
                u, s = divmod(t, STEPS)
                b = u // GROUPS
                dve.wait_ge(exp_made, 2 * t + half + 1)
                if half == 0:
                    if t >= 2:
                        dve.wait_ge(pv_done, t - 1)
                    if t % (GROUPS * STEPS) == 0:
                        dve.wait_ge(work_read_act, reads_before[("gT", b, NC - 1)][1])
                j = 2 * half + 1
                V.tensor_tensor(probg[t % 2][:, j, :].rearrange("p (h q) -> p h q", h=GH),
                                prob[t % 2][:, j, :].rearrange("p (h q) -> p h q", h=GH),
                                gT[b % 2][:, KT_TICK * s + j, :].unsqueeze(1).broadcast_to([P, GH, P]),
                                ALU.mult).then_inc(gated_dve, 1)

            def row_max(w):
                _, n, c = w
                u, h = divmod(n, GH)
                b = u // GROUPS
                if c == 0 and u % GROUPS == 0 and h == 0:
                    dve.wait_ge(neg_made, b + 1)
                await_filled(dve, w)
                if reads_before[w][1] > 2:
                    dve.wait_ge(work_read_dve, reads_before[w][1] - 2)
                V.tensor_tensor_reduce(out=junk[:, c % 2, :], in0=bank_of(w)[:, :], in1=neg[b % 2][:, 512 * c:512 * c + 512],
                                       scale=1.0, scalar=LOWEST, op0=ALU.add, op1=ALU.max,
                                       accum_out=mx[:, u % 2, h, c:c + 1]).then_inc(work_read_dve, 1)

            def split_max(u):
                dve.wait_ge(work_read_dve, reads_before[("max", GH * u + GH - 1, NC - 1)][1])
                if u >= 1:
                    dve.wait_ge(work_filled, slot[("mrow", u - 1, 0)] + 1)
                link(V.reduce_max(mtop[:, :], mx[:, u % 2, :, :], AX_X))
                link(V.tensor_scalar(mpart[:, :, 1], mtop[:, :], -1.0, None, ALU.mult))
                link(V.scalar_tensor_tensor(mres[:, :], mtop[:, :], -1.0, mpart[:, :, 1], ALU.mult, ALU.subtract))
                link(V.tensor_copy(mpart[:, :, 2], mres[:, :]))
                V.tensor_tensor(mpart[:, :, 3], mres[:, :], mpart[:, :, 2], ALU.subtract).then_inc(mpart_made, 1)

            def value_bias(w):
                _, b, c = w
                await_filled(dve, w)
                if c == 0 and b >= 2:
                    dve.wait_ge(pv_done, GROUPS * STEPS * (b - 1))
                V.tensor_tensor(v_s[b % 2][:, 4 * c:4 * c + 4, :], bank_of(w)[:, :].rearrange("p (t d) -> p t d", t=4),
                                bv_s[:, :].unsqueeze(1).broadcast_to([P, 4, D]), ALU.add).then_inc(work_read_dve, 1)

            def numerators(u):
                dve.wait_ge(pv_done, STEPS * (u + 1))
                if u >= 1:
                    dve.wait_ge(work_filled, slot[("wo", u - 1, 0)] + 1)
                V.tensor_tensor(numer[:, :, :], num_ps[:, :].rearrange("p (h q) -> p h q", h=GH),
                                headsel[:, :].unsqueeze(2).broadcast_to([P, GH, P]), ALU.mult).then_inc(numer_made, 1)

            def finish_den(w):
                await_filled(dve, w)
                if w[1] >= 1:
                    dve.wait_ge(work_read_act, reads_before[("wo", w[1] - 1, 0)][1])
                ins = V.reciprocal(rden[:, :], bank_of(w)[:, 0:GH])
                ins.then_inc(work_read_dve, 1)

            def read_work(w):
                {"max": row_max, "v": value_bias, "den": finish_den}[w[0]](w)

            V.memset(mpart[:, :, :], 0.0)
            V.memset(ones32[:, :], 1.0)
            V.memset(halfneg[:, :], -0.5)
            link(V.memset(ones_sq[:, :], 1.0))
            dve.wait_ge(x_in, 16)
            layer_norm(0)
            dve.wait_ge(work_read_act, reads_before[("q", 0, 0)][1])
            link(V.tensor_tensor(qf, qf, qpart[0], ALU.subtract))
            link(V.tensor_copy(qpart[1], qf))
            V.tensor_tensor(qpart[2], qf, qpart[1], ALU.subtract).then_inc(q_parts_made, 1)
            for c in range(NC):
                cols = slice(512 * c, 512 * c + 512)
                dve.wait_ge(work_read_act, reads_before[("k", 0, c)][1])
                link(V.tensor_tensor(kf(0, cols), kf(0, cols), kpart[0][:, cols], ALU.subtract))
                link(V.tensor_copy(kpart[1][:, cols], kf(0, cols)))
                V.tensor_tensor(kpart[2][:, cols], kf(0, cols), kpart[1][:, cols], ALU.subtract).then_inc(k_parts_made, 1)
            for w in start_work:
                if w[0] not in BY_ACT:
                    read_work(w)
                    if w == ("max", GH - 1, NC - 1):
                        split_max(0)
            for t in range(TICKS):
                u, s = divmod(t, STEPS)
                for w in tick_max(t, 0):
                    read_work(w)
                if t >= 1:
                    gate(t - 1, 1)
                if s == 1 and u >= 1:
                    numerators(u - 1)
                for w in tick_work(t):
                    if w[0] not in BY_ACT:
                        read_work(w)
                if s == STEPS - 2 and u + 1 < UNITS:
                    split_max(u + 1)
                for w in tick_max(t, 1):
                    read_work(w)
                gate(t, 0)
            gate(TICKS - 1, 1)
            numerators(UNITS - 1)
            read_work(("den", UNITS - 1, 0))

            dve.wait_ge(unit_added, UNITS)
            layer_norm(1)
            dve.wait_ge(l_read_act, 4)
            link(V.scalar_tensor_tensor(decay, decay, 0.0, lnexp, ALU.min, ALU.subtract))
            for b in range(B):
                last = V.tensor_tensor_scan(cum[:, P * b:P * b + P], ones_sq[:, :], decay[:, P * b:P * b + P], 0.0,
                                            ALU.mult, ALU.add)
            link(last)

            def parts_of(a, c):
                return a.rearrange("p (n two c) -> p n two c", two=2, c=c)

            def exponents(l):
                c = LEVELS[l]
                g, x_ = parts_of(cum, c), parts_of(expo[l % 2], c)
                border = g[:, :, 0, c - 1:c].broadcast_to([P, N // (2 * c), c])
                if l >= 2:
                    dve.wait_ge(scaled_made, l - 1)
                V.tensor_tensor(x_[:, :, 1, :], g[:, :, 1, :], border, ALU.subtract)
                V.tensor_tensor(x_[:, :, 0, :], border, g[:, :, 0, :], ALU.subtract).then_inc(expo_made, 1)

            def scale_parts(l):
                c = LEVELS[l]
                w_, o_ = parts_of(expo[l % 2], c), parts_of(scaled[l], c)
                dve.wait_ge(decayed, l + 1)
                V.tensor_tensor(o_[:, :, 0, :], w_[:, :, 0, :], parts_of(kT, c)[:, :, 0, :], ALU.mult)
                V.tensor_tensor(o_[:, :, 1, :], w_[:, :, 1, :], parts_of(qT, c)[:, :, 1, :], ALU.mult).then_inc(scaled_made, 1)

            exponents(0)
            for l in range(NLEVEL):
                if l + 1 < NLEVEL:
                    exponents(l + 1)
                scale_parts(l)
            dve.wait_ge(squared, 1)
            V.scalar_tensor_tensor(zgate, zgate, 1.0, banks[:, 4:8, DV:2 * DV], ALU.add, ALU.mult).then_inc(l_read_dve, 2)
            dve.wait_ge(cst_in, 16)
            for r in range(B // 2):
                dve.wait_ge(pairs_made, r + 1)
                rows = slice(8 * r, 8 * r + 8)
                V.tensor_tensor(picked[:, rows, :, :].rearrange("p c l t -> p c (l t)"), banks[:, :, 0:NDIAG * 32],
                                levelsel.rearrange("p l t -> p (l t)").unsqueeze(1).broadcast_to([P, 8, NDIAG * 32]),
                                ALU.mult).then_inc(picked_read, 1)
                dve.wait_ge(picked_read, r + 1)
                link(V.tensor_reduce(diag[:, rows, :], picked[:, rows, :, :].rearrange("p c l t -> p c t l"), AX_X, ALU.add))
                V.tensor_tensor(attT[:, rows, :].rearrange("p c (m t) -> p c m t", t=32),
                                diag[:, rows, :].unsqueeze(2).broadcast_to([P, 8, 4, 32]),
                                blocksel.unsqueeze(1).broadcast_to([P, 8, 4, 32]), ALU.mult).then_inc(att_made, 1)
            dve.wait_ge(squared, 2)
            V.tensor_reduce(rms_sum, squares.rearrange("p b (h v) -> p (b h) v", v=HV), AX_X, ALU.add).then_inc(sums_made, 1)
            dve.wait_ge(rms_made, 1)
            link(V.tensor_tensor(mixed.rearrange("p b (h v) -> p (b h) v", v=HV),
                                 banks[:, 0:2, :].rearrange("p a (c v) -> p (a c) v", v=HV),
                                 rms_inv.unsqueeze(2).broadcast_to([P, B * LH, HV]), ALU.mult))
            link(V.tensor_tensor(mixed.rearrange("p b (h v) -> p (b h) v", v=HV),
                                 mixed.rearrange("p b (h v) -> p (b h) v", v=HV),
                                 rms_l.unsqueeze(1).broadcast_to([P, B * LH, HV]), ALU.mult))
            V.scalar_tensor_tensor(mixed, mixed, 0.5, zgate, ALU.mult, ALU.mult).then_inc(gated_made, 1)
            dve.wait_ge(l_out, 1)
            link(V.tensor_tensor(x1[:, :, :].rearrange("p b d -> p (b d)"), x1[:, :, :].rearrange("p b d -> p (b d)"),
                                 banks[:, 4, :], ALU.add))
            layer_norm(2)
            dve.wait_ge(logits_made, 1)
            link(V.tensor_tensor(logit, banks[:, 7, 0:B * E].rearrange("p (b e) -> p b e", e=E),
                                 rb_s.unsqueeze(1).broadcast_to([P, B, E]), ALU.add))
            for b in range(B):
                last = V.max(top[:, b, :], logit[:, b, :])
            link(last)
            for b in range(B):
                last = V.max_index(topno[:, b, :].bitcast(U32), top[:, b, :], logit[:, b, :])
            V.tensor_tensor(ratio, top[:, :, 1], top[:, :, 0], ALU.subtract).then_inc(ratio_in, 1)
            link(last)
            link(V.tensor_copy(topnof, topno.bitcast(U32)))
            for i in range(2):
                last = V.tensor_tensor(pick[i], expert_no.unsqueeze(1).broadcast_to([P, B, E]),
                                       topnof[:, :, i:i + 1].broadcast_to([P, B, E]), ALU.is_equal)
            link(last)
            V.tensor_tensor(chosen, pick[0], pick[1], ALU.add).then_inc(chosen_made, 1)
            dve.wait_ge(ratio_made, 1)
            link(V.tensor_scalar(top_p[0], ratio, 1.0, None, ALU.add))
            link(V.reciprocal(top_p[0], top_p[0]))
            link(V.tensor_tensor(top_p[1], top_p[0], ratio, ALU.mult))
            for i in range(2):
                last = V.tensor_tensor(pick[i], pick[i], top_p[i].unsqueeze(2).broadcast_to([P, B, E]), ALU.mult)
            link(last)
            link(V.tensor_tensor(weight, pick[0], pick[1], ALU.add))

            def hidden(i):
                dve.wait_ge(tanh_made, i + 1)
                link(V.scalar_tensor_tensor(gated[i % 2], tanhs[i % 2], 1.0, banks[:, 2 * (i % 3) + 1, :], ALU.add, ALU.mult))
                if i >= 4:
                    dve.wait_ge(down_made, i // 2 - 1)
                V.tensor_tensor(hidT[i % 4], gated[i % 2], banks[:, 2 * (i % 3), :], ALU.mult).then_inc(hid_made, 1)

            def add_expert(e):
                dve.wait_ge(down_made, e + 1)
                if e >= 1:
                    dve.wait_ge(expert_added, e)
                for b in range(B):
                    last = V.scalar_tensor_tensor(x1[:, b, :], banks[:, 6 + e % 2, P * b:P * b + P], weight[:, b, e:e + 1],
                                                  x1[:, b, :], ALU.mult, ALU.add)
                last.then_inc(expert_added, 1)

            for i in range(2 * E):
                hidden(i)
                if i == 1:
                    dve.wait_ge(rank_made, 1)
                    V.tensor_scalar(chosen, banks[:, 7, 0:B * E].rearrange("p (b e) -> p b e", e=E), float(CAPACITY), 0.5,
                                    ALU.is_le, ALU.mult).then_inc(l_read_dve, 3)
                    dve.wait_ge(l_read_dve, 5)
                    link(V.tensor_tensor(weight, weight, chosen, ALU.mult))
                if i >= 3 and i % 2:
                    add_expert(i // 2 - 1)
            add_expert(E - 1)

        @block.gpsimd
        def _(pool):
            G = nc.gpsimd
            chain = [0]

            def link(ins):
                chain[0] += 1
                ins.then_inc(pool_chain, 1)
                pool.wait_ge(pool_chain, chain[0])

            def rsqrt(k):
                pool.wait_ge(stats_made, k + 1)
                link(G.tensor_scalar(rstd[:, :], mv[:, :, 1], EPS, None, ALU.add))
                G.tensor_tensor(rstd[:, :], rstd[:, :], halfneg[:, :], ALU.pow).then_inc(rstd_made, 1)

            def mask_offset(b):
                pool.wait_ge(mask_in, 16 * (b + 1))
                if b >= 2:
                    pool.wait_ge(score_made, 2 * STEPS * GROUPS * (b - 1))
                G.tensor_scalar(neg[b % 2][:, :], mask_s[:, :], -NEG, NEG, ALU.mult, ALU.add).then_inc(neg_made, 1)

            def gate(t, half):
                u, s = divmod(t, STEPS)
                b = u // GROUPS
                pool.wait_ge(exp_made, 2 * t + half + 1)
                if half == 0:
                    if t >= 2:
                        pool.wait_ge(pv_done, t - 1)
                    if t % (GROUPS * STEPS) == 0:
                        pool.wait_ge(work_read_act, reads_before[("gT", b, NC - 1)][1])
                j = 2 * half
                G.tensor_tensor(probg[t % 2][:, j, :].rearrange("p (h q) -> p h q", h=GH),
                                prob[t % 2][:, j, :].rearrange("p (h q) -> p h q", h=GH),
                                gT[b % 2][:, KT_TICK * s + j, :].unsqueeze(1).broadcast_to([P, GH, P]),
                                ALU.mult).then_inc(gated_pool, 1)

            def split_k(b, c):
                cols = slice(512 * c, 512 * c + 512)
                pool.wait_ge(work_read_act, reads_before[("k", b, c)][1])
                link(G.tensor_tensor(kf(b, cols), kf(b, cols), kpart[0][:, cols], ALU.subtract))
                link(G.tensor_copy(kpart[1][:, cols], kf(b, cols)))
                G.tensor_tensor(kpart[2][:, cols], kf(b, cols), kpart[1][:, cols], ALU.subtract).then_inc(k_parts_made, 1)

            def add_unit(u):
                pool.wait_ge(work_read_act, reads_before[("wo", u, 0)][1])
                link(G.tensor_tensor(head_out[:, 0:2, :], head_out[:, 0:2, :], head_out[:, 2:4, :], ALU.add))
                link(G.tensor_tensor(head_out[:, 0, :], head_out[:, 0, :], head_out[:, 1, :], ALU.add))
                b = u // GROUPS
                if u >= 1:
                    pool.wait_ge(unit_added, u)
                G.tensor_tensor(x1[:, b, :], x1[:, b, :], head_out[:, 0, :], ALU.add).then_inc(unit_added, 1)

            link(G.memset(identf[:, :], 0.0))
            link(G.affine_select(out=identf[:, :], in_=identf[:, :], compare_op=ALU.not_equal, fill=1.0, base=0,
                                 pattern=[[-1, P]], channel_multiplier=1))
            pool.wait_ge(dve_chain, 1)
            rsqrt(0)
            for h in range(GH):
                link(G.tensor_copy(negident[:, h, :], identf[:, :]))
            link(G.memset(headsel[:, :], 1.0))
            link(G.memset(quadsel[:, :], 0.0))
            for j in range(4):
                v = headsel[32 * j:32 * j + 32, :]
                link(G.affine_select(out=v, in_=v, compare_op=ALU.is_ge, fill=0.0, base=0, pattern=[[-8, GH]], channel_multiplier=1))
                link(G.affine_select(out=v, in_=v, compare_op=ALU.is_ge, fill=0.0, base=7, pattern=[[8, GH]], channel_multiplier=-1))
                link(G.memset(quadsel[32 * j:32 * j + 1, :], 1.0))
            mask_offset(0)
            pool.wait_ge(bo_in, 16)
            pool.wait_ge(xh_made, 1)
            link(G.tensor_tensor(x1[:, :, :], x1[:, :, :], bo_s[:, :].unsqueeze(1).broadcast_to([P, B, D]), ALU.add))
            for t in range(TICKS):
                b, i = divmod(t, GROUPS * STEPS)
                gate(t, 0)
                gate(t, 1)
                if b + 1 < B:
                    if i == 0:
                        mask_offset(b + 1)
                    if 2 <= i <= 5:
                        split_k(b + 1, i - 2)
                u, s = divmod(t, STEPS)
                if s == STEPS - 1 and u >= 1:
                    add_unit(u - 1)
            add_unit(UNITS - 1)
            rsqrt(1)
            link(G.memset(rms_half, -0.5))
            pool.wait_ge(sums_made, 1)
            link(G.tensor_scalar(rms_inv, rms_sum, 1.0 / HV, EPS, ALU.mult, ALU.add))
            G.tensor_tensor(rms_inv, rms_inv, rms_half, ALU.pow).then_inc(rms_made, 1)
            rsqrt(2)


_NAMES = ['x', 'ctx_1024', 'fside_BxSxS2_0', 'mask_BxSxS2_ik1', 'L0_xattn_wq_k', 'L0_xattn_wq_b', 'L0_xattn_wk_k',
          'L0_xattn_wk_b', 'L0_xattn_wv_k', 'L0_xattn_wv_b', 'L0_xattn_wo_k', 'L0_xattn_wo_b', 'L0_attn_Wq', 'L0_attn_Wk',
          'L0_attn_Wv', 'L0_attn_Wg', 'L0_attn_gk_w1', 'L0_attn_gk_w2', 'L0_attn_gk_b', 'L0_attn_Wo', 'L0_attn_rms_w',
          'L0_ffn_router_w', 'L0_ffn_router_b', 'L0_ffn_W', 'L0_ffn_V', 'L0_ffn_W_out']


def kernel(**inputs):
    import numpy as np
    import concourse.bacc as bacc
    from concourse.bass_utils import run_bass_kernel_spmd

    nc = bacc.Bacc("TRN2", target_bir_lowering=False, num_devices=1)
    arrays, args = {}, []
    for name in _NAMES:
        a = np.asarray(inputs[name])
        a = np.ascontiguousarray(a.T if name == "L0_ffn_router_w" else a)
        arrays["in_" + name] = a
        args.append(nc.dram_tensor("in_" + name, a.shape, mybir.dt.from_np(a.dtype), kind="ExternalInput").ap())
    s, t = np.arange(P)[:, None], np.arange(32)[None, :]
    differ = (s % 32) ^ t
    levels = [(differ >= c) & (differ < 2 * c) & (t > s % 32) for c in LEVELS[2:]] + [differ == 0]
    blocks = np.arange(P)[:, None] // 32 == np.arange(P)[None, :] // 32
    upto = s <= np.arange(P)[None, :]
    arrays["shape_consts"] = np.concatenate([*levels, blocks, upto, np.tile(np.arange(8), (P, 1))], axis=1).astype(np.float32)
    args.append(nc.dram_tensor("shape_consts", (P, CONSTS), F32, kind="ExternalInput").ap())
    fill_rows = np.concatenate([np.zeros((1, GH * 2048)), np.ones((1, GH * 2048))]).astype(mybir.dt.np(BF16))
    arrays["fill_rows"] = fill_rows
    args.append(nc.dram_tensor("fill_rows", fill_rows.shape, BF16, kind="ExternalInput").ap())
    out = nc.dram_tensor("out_x", inputs["x"].shape, F32, kind="ExternalOutput").ap()
    perceiver_kernel(nc, *args, out)
    r = run_bass_kernel_spmd(nc, [arrays], core_ids=[0])
    return r.results[0]["out_x"]
```

```python
from contextlib import ExitStack

import concourse.bass as bass
from concourse import mybir

F32 = mybir.dt.float32
BF16 = mybir.dt.bfloat16
I32 = mybir.dt.int32
U32 = mybir.dt.uint32
ALU = mybir.AluOpType
ACT = mybir.ActivationFunctionType
AX_X = mybir.AxisListType.X

P = 128
EPS = 1e-5
NEG = -998244352.0
LOWEST = -3.0e38


LEVELS = (64, 32, 16, 8, 4, 2, 1)
NLEVEL = len(LEVELS)
INNER = 5
PICKS = INNER * 16 + 32
LEVEL_ORDER = (2, 3, 4, 5, 6, 0, 1)
CONSTS = PICKS + 2 * P + 8

HEADS = 16
GH = 4
GROUPS = HEADS // GH
KT_TICK = 4
LEAD = GH + 2
PAIRS = [(0, 0), (0, 1), (1, 0), (1, 1), (0, 2), (2, 0)]
ZROW = 64
AUG = 68


def perceiver_kernel(nc, x, ctx, fside, mask, wq, bq, wk, bk, wv, bv, wo, bo,
                     gWq, gWk, gWv, gWg, gw1, gw2, gb, gWo, grms,
                     rw, rb, eW, eV, eWo, shape_consts, fill, out):
    B, S, D = x.shape
    S2 = ctx.shape[1]
    DH = D // HEADS
    NK = S2 // P
    NC = S2 // 512
    UNITS = B * GROUPS
    STEPS = NK // KT_TICK
    TICKS = UNITS * STEPS
    HEAD_SEQ = UNITS * GH
    SCALE = float(DH) ** -0.5

    es = ExitStack()
    with es:
        def sb(name, shape, dt=F32):
            return es.enter_context(nc.sbuf_tensor(name, shape, dt))

        def pb(name, shape, dt=F32):
            return es.enter_context(nc.psum_tensor(name, shape, dt))

        def sem(name):
            return es.enter_context(nc.semaphore(name))

        identf = sb("identf", [P, P])
        negident = sb("negident", [P, GH, P], BF16)
        identb = negident[:, 0, :]
        ones32 = sb("ones32", [P, 32])
        headsel = sb("headsel", [P, GH])
        quadsel = sb("quadsel", [P, 1])
        halfneg = sb("halfneg", [P, B])

        x1 = sb("x1", [P, B, D])
        xh = sb("xh", [P, B, D])
        xhT = sb("xhT", [P, B * P])
        bnst = sb("bnst", [P, B, 6])
        mv = sb("mv", [P, B, 2])
        rstd = sb("rstd", [P, B])

        wq_s, wk_s, wv_s = sb("wq_s", [P, D]), sb("wk_s", [P, D]), sb("wv_s", [P, D])
        wo_s = sb("wo_s", [P, GROUPS, D])
        bv_s, bo_s = sb("bv_s", [P, D]), sb("bo_s", [P, D])
        bq_s, bk_s, bqs = sb("bq_s", [P, 1]), sb("bk_s", [P, 1]), sb("bqs", [P, 1])

        qparts = sb("qparts", [P, 3, B * P], BF16)
        qpart = [qparts[:, i, :] for i in range(3)]
        kparts = sb("kparts", [P, 3, S2], BF16)
        kpart = [kparts[:, i, :] for i in range(3)]
        qaug = sb("qaug", [AUG, HEADS, B, P], BF16)
        kaug = [sb(f"kaug{i}", [AUG, GH, S2], BF16) for i in range(3)]

        ctx_s = sb("ctx_s", [P, NK, D])
        ctxT = sb("ctxT", [P, S2])
        v_s = [sb(f"v_s{i}", [P, NK, D]) for i in range(2)]
        f_s = sb("f_s", [P, S2])
        gT = [sb(f"gT{i}", [P, NK, P]) for i in range(2)]
        mask_s = sb("mask_s", [P, S2], I32)
        neg = [sb(f"neg{i}", [P, S2], BF16) for i in range(2)]
        junk = sb("junk", [P, 2, 512], BF16)

        prob = [sb(f"prob{i}", [P, KT_TICK, GH * P]) for i in range(2)]
        probg = [sb(f"probg{i}", [P, KT_TICK, GH * P]) for i in range(2)]
        def kf(b, cols):
            return (prob[0][:, :, :].rearrange("p t q -> p (t q)") if b == 0 else f_s)[:, cols]
        mx = sb("mx", [P, 2, GH, NC])
        mtop = sb("mtop", [P, GH])
        mres = sb("mres", [P, GH])
        mpart = sb("mpart", [P, GH, 4], BF16)
        numer = sb("numer", [P, GH, P])
        qf = numer[:, :, :].rearrange("p h q -> p (h q)")
        denom = sb("denom", [P, GH, P])
        rden = sb("rden", [P, GH])
        head_out = sb("head_out", [P, GH, P])

        banks = pb("banks", [P, 8, 512])
        score = [banks[:, 0:2, :], banks[:, 2:4, :]]
        num_ps, den_ps = banks[:, 6, :], banks[:, 7, :]

        LH, HK = 4, gWq.shape[1] // 4
        HV = gWv.shape[1] // LH
        DV, LR, E, HID = gWv.shape[1], gw1.shape[1], eW.shape[0], eW.shape[2]
        CAPACITY = 2 * B * S * 2 // E
        N = B * P
        cst = sb("cst", [P, CONSTS])
        levelsel = cst[:, 0:PICKS]
        blocksel = cst[:, PICKS:PICKS + P].rearrange("p (m t) -> p m t", t=32)
        upto = cst[:, PICKS + P:PICKS + 2 * P]
        expert_no = cst[:, PICKS + 2 * P:CONSTS]
        ones_sq = sb("ones_sq", [P, P])

        def flat(t):
            return t[:, :, :].rearrange("p a b -> p (a b)")

        small = flat(v_s[0])
        free = [0]

        def carve(n):
            free[0] += n
            return small[:, free[0] - n:free[0]]

        wqk_l, wvg_l, wo_l = carve(2 * P), carve(2 * DV), carve(2 * D).rearrange("p (a n) -> p a n", a=2)
        w1_l, w2_l, b_l, rms_l = carve(LR), carve(P)[0:LR, :], carve(1), carve(HV)
        rw_s, rb_s = carve(E), carve(E)
        logit = carve(B * E).rearrange("p (b e) -> p b e", e=E)
        top = carve(B * E).rearrange("p (b e) -> p b e", e=E)
        topno = carve(B * E).rearrange("p (b e) -> p b e", e=E)
        topnof = carve(B * E).rearrange("p (b e) -> p b e", e=E)
        pick = [carve(B * E).rearrange("p (b e) -> p b e", e=E) for _ in range(2)]
        chosen, chosen_before = [carve(B * E).rearrange("p (b e) -> p b e", e=E) for _ in range(2)]
        weight = carve(B * E).rearrange("p (b e) -> p b e", e=E)
        ratio, top_p = carve(B), [carve(B) for _ in range(2)]
        rms_sum, rms_inv, rms_half = carve(B * LH), carve(B * LH), carve(B * LH)
        LGROUPS = ((0, B - 1), (B - 1, B))
        kT, cum, qT, decay = (ctxT[:, N * i:N * i + N] for i in range(4))
        kparts_f = kparts[:, :, :].rearrange("p a b -> p (a b)").bitcast(F32)
        expo = [kparts_f[:, N * i:N * i + N] for i in range(NLEVEL - 1)] + [flat(gT[0])[:, 0:N]]
        lnexp = flat(gT[0])[:, N:2 * N]
        zgate = flat(gT[0])[:, 2 * N:4 * N].rearrange("p (b v) -> p b v", v=DV)
        val = neg[0][:, :].bitcast(F32).rearrange("p (b v) -> p b v", v=DV)
        lowT = carve((B - 1) * P)[0:LR, :]
        qheads = flat(probg[0]).rearrange("p (h n) -> p h n", h=LH)
        later_homes = (prob[0], prob[0], prob[1], prob[1], v_s[1], v_s[1], probg[1])

        def later_of(g, l):
            home, side = flat(later_homes[l]), l % 2
            n = (B - 1) * 2 * P
            at = n * side if g == 0 else (n + 2 * P * side if l == NLEVEL - 1 else 2 * n + 2 * P * side)
            return home[:, at:at + (n if g == 0 else 2 * P)].rearrange("p (h n) -> p h n", h=LH)

        later = [[later_of(g, l) for l in range(NLEVEL)] for g in range(2)]
        attT = flat(gT[1]).rearrange("p (c t) -> p c t", t=P)
        picked = [flat(prob[0])[:, 0:(B - 1) * LH * PICKS].rearrange("p (c j) -> p c j", j=PICKS),
                  denom[:, :, :].rearrange("p h q -> p (h q)")[:, 0:LH * PICKS].rearrange("p (c j) -> p c j", j=PICKS)]
        mixed = [flat(prob[1])[:, 0:(B - 1) * DV].rearrange("p (b v) -> p b v", v=DV), qf[:, 0:DV].unsqueeze(1)]
        squares = [flat(prob[1])[:, (B - 1) * DV:2 * (B - 1) * DV].rearrange("p (b v) -> p b v", v=DV),
                   qf[:, DV:2 * DV].unsqueeze(1)]
        ztanh = flat(probg[1])[:, 2 * N:4 * N].rearrange("p (b v) -> p b v", v=DV)
        mixedT = neg[1][:, :].bitcast(F32).rearrange("p (a n) -> p a n", a=2)
        inner_bank, outer_bank = (0, 1, 2, 4), (3, 6, 7, 5)
        eW_s = flat(ctx_s).rearrange("p (e f) -> p e f", e=E)
        eV_s = f_s[:, :].rearrange("p (e f) -> p e f", e=E)
        eWo_s = mask_s[:, :].bitcast(F32).rearrange("p (e a d) -> p e a d", e=E, a=2)
        tanhs = [flat(prob[0])[:, N * i:N * i + N] for i in range(2)]
        gated = [flat(prob[0])[:, N * (2 + i):N * (2 + i) + N] for i in range(2)]
        hidT = [flat(prob[1])[:, N * i:N * i + N] for i in range(4)]

        q_dram = nc.dram_tensor("q_dram", [3, P, B * P], BF16, kind="Internal").ap()
        k_dram = nc.dram_tensor("k_dram", [B, 3, P, S2], BF16, kind="Internal").ap()

        x_in, w_in, wv_in, wo_in, bo_in = sem("x_in"), sem("w_in"), sem("wv_in"), sem("wo_in"), sem("bo_in")
        ctx_in = [sem(f"ctx_in{c}") for c in range(NC)]
        f_in, mask_in, qfill_in = sem("f_in"), sem("mask_in"), sem("qfill_in")
        qaug_in = sem("qaug_in")
        q_stored, k_stored, kfirst_stored = sem("q_stored"), sem("k_stored"), sem("kfirst_stored")
        kaug_in = [sem(f"kaug_in{i}") for i in range(3)]
        kfill_in = [sem(f"kfill_in{i}") for i in range(3)]
        kfirst_in = sem("kfirst_in")
        pool_chain, dve_chain, act_chain = sem("pool_chain"), sem("dve_chain"), sem("act_chain")
        stats_made, rstd_made, xh_made = sem("stats_made"), sem("rstd_made"), sem("xh_made")
        work_filled, work_read_dve, work_read_act = sem("work_filled"), sem("work_read_dve"), sem("work_read_act")
        q_parts_made = sem("q_parts_made")
        k_parts_made, k_parts_made_pool = sem("k_parts_made"), sem("k_parts_made_pool")
        k_rest_made, k_middle_made = sem("k_rest_made"), sem("k_middle_made")
        neg_made = sem("neg_made")
        score_made, exp_made = sem("score_made"), sem("exp_made")
        gated_pool, gated_dve = sem("gated_pool"), sem("gated_dve")
        pv_done, weights_summed = sem("pv_done"), sem("weights_summed")
        unit_added = sem("unit_added")
        mpart_made = sem("mpart_made")
        numer_made, denom_made = sem("numer_made"), sem("denom_made")
        cst_in, l_in, e_in = sem("cst_in"), sem("l_in"), sem("e_in")
        rank_read, features_made, features_read = sem("rank_read"), sem("features_made"), sem("features_read")
        picks_made = sem("picks_made")
        soft_made = sem("soft_made")
        zgate_made, zgate_scaled, ztanh_made = sem("zgate_made"), sem("zgate_scaled"), sem("ztanh_made")
        expo_made, decayed, scaled_made = sem("expo_made"), sem("decayed"), sem("scaled_made")
        pairs_made, off_read, qheads_made = sem("pairs_made"), sem("off_read"), sem("qheads_made")
        att_made = [sem(f"att_made{g}") for g in range(2)]
        mixed_made, squared, sums_made, rms_made = sem("mixed_made"), sem("squared"), sem("sums_made"), sem("rms_made")
        gated_made, mixT_made, mixT_read, l_out = sem("gated_made"), sem("mixT_made"), sem("mixT_read"), sem("l_out")
        logits_made, ratio_in, ratio_made, chosen_made, rank_made = (sem("logits_made"), sem("ratio_in"), sem("ratio_made"),
                                                                    sem("chosen_made"), sem("rank_made"))
        up_made, tanh_made, hid_made, down_made, expert_added = (sem("up_made"), sem("tanh_made"), sem("hid_made"),
                                                                 sem("down_made"), sem("expert_added"))
        gate_up_made = sem("gate_up_made")
        batch_done, out_done = sem("batch_done"), sem("out_done")

        LINEAR_WORK = {(6, 0): [("lT", 0, 0)], (7, 0): [("l1", 0, 0)], (7, 1): [("lq", 0, 0)], (8, 0): [("l2", 0, 0)],
                       (9, 0): [("lk", 0, 0)], (10, 1): [("lv", 0, 0)], (11, 1): [("lv", 0, 1)], (12, 1): [("lv", 0, 2)]}

        k_tick = {GROUPS * STEPS * (b - 1) + c + (b == 1): (b, c) for b in range(1, B) for c in range(NC)}

        def tick_work(t, half):
            u, s = divmod(t, STEPS)
            b, i = divmod(t, GROUPS * STEPS)
            items = []
            if t == 0:
                items += [("gT", 0, 2 * half), ("gT", 0, 2 * half + 1)]
            if half == 0 and t in k_tick:
                items.append(("k", *k_tick[t]))
            if b + 1 < B and half == 0:
                if 5 <= i <= 8:
                    items.append(("v", b + 1, i - 5))
                if 9 <= i <= 12:
                    items.append(("gT", b + 1, i - 9))
            if half == 1 and t + 1 in k_tick:
                items.append(("ctxT", *k_tick[t + 1]))
            if b + 1 == B:
                items += LINEAR_WORK.get((i, half), [])
            if s == STEPS - 1 and u + 1 < UNITS and half == 0:
                items.append(("mrow", u + 1, 0))
            if u >= 1 and s == 1 and half == 1:
                items.append(("den", u - 1, 0))
            if u >= 1 and s == 3 and half == 1:
                items.append(("wo", u - 1, 0))
            return items

        def tick_max(t, half):
            heads = {(0, 0): [], (0, 1): [4], (1, 0): [5], (1, 1): [6], (2, 0): [7], (2, 1): [8]}.get((t, half))
            if heads is not None:
                return [("max", n, c) for n in heads for c in range(NC)]
            n = t + LEAD
            return [("max", n, c) for c in range(NC // 2 * half, NC // 2 * (half + 1))] if n < HEAD_SEQ else []

        start_work = [("xhT", 0, 0), ("ctxT", 0, 0), ("q", 0, 0), ("ctxT", 0, 1), ("k", 0, 0)]
        for c in range(1, NC):
            start_work += [("ctxT", 0, c + 1)] * (c + 1 < NC) + [("k", 0, c)]
        start_work += [("v", 0, c) for c in range(NC)]
        start_work += [("max", n, c) for half in range(2) for n in range(GH) for c in (2 * half, 2 * half + 1)]
        start_work += [("mrow", 0, 0)]
        end_work = [("den", UNITS - 1, 0), ("wo", UNITS - 1, 0), ("lT", 1, 0), ("l1", 1, 0), ("lq", 1, 0), ("lk", 1, 0),
                    ("l2", 1, 0), ("lv", 1, B - 1)]
        tick_steps = [w for t in range(TICKS) for half in range(2) for w in tick_max(t, half) + tick_work(t, half)]
        all_work = start_work + tick_steps + end_work
        slot = {w: n for n, w in enumerate(all_work)}
        BY_ACT = ("ctxT", "q", "k", "gT", "mrow", "xhT", "wo", "lT", "l1", "l2", "lq", "lk", "lv")
        reads_before = {}
        counts = {"act": 0, "dve": 0}
        for w in all_work:
            who = "act" if w[0] in BY_ACT else "dve"
            counts[who] += 1
            reads_before[w] = (who, counts[who])

        ring = [4 + n % 2 if n >= len(start_work) else (4, 5, 0, 1, 2, 3)[n % 6] for n in range(len(all_work))]
        before, holder = {}, {}
        for w, bank_no in zip(all_work, ring):
            if w == (tick_max(0, 0) + tick_work(0, 0))[0]:
                start_holders = dict(holder)
            before[w] = holder.get(bank_no)
            holder[bank_no] = w

        def bank_of(w):
            return banks[:, ring[slot[w]], :]

        def await_read(pe, w):
            who, n = reads_before[w]
            pe.wait_ge(work_read_act if who == "act" else work_read_dve, n)

        def await_bank(pe, w):
            if before[w] is not None:
                await_read(pe, before[w])

        def await_act(eng, w):
            eng.wait_ge(work_read_act, reads_before[w][1])

        def columns(g):
            return slice(P * LGROUPS[g][0], P * LGROUPS[g][1])

        def spread_blocks(engine, b):
            g = 0 if b < LGROUPS[1][0] else 1
            at = LH * (b - LGROUPS[g][0])
            engine.tensor_tensor(attT[:, LH * b:LH * b + LH, :].rearrange("p c (m t) -> p c m t", t=32),
                                 picked[g][:, at:at + LH, PICKS - 32:PICKS].unsqueeze(2).broadcast_to([P, LH, 4, 32]),
                                 blocksel.unsqueeze(1).broadcast_to([P, LH, 4, 32]), ALU.mult).then_inc(att_made[g], 1)

        def await_filled(eng, w):
            eng.wait_ge(work_filled, slot[w] + 1)

        block = es.enter_context(nc.Block())

        @block.sync
        def _(sp):
            def load_ctx(b, c):
                sp.dma_start(ctx_s[:, 4 * c:4 * c + 4, :],
                             ctx[b, 512 * c:512 * c + 512, :].rearrange("(t p) d -> p t d", p=P)).then_inc(ctx_in[c], 16)

            sp.dma_start(x1[:, :, :], x.rearrange("b s d -> s b d")).then_inc(x_in, 16)
            load_ctx(0, 0)
            sp.dma_start(wk_s[:, :], wk).then_inc(w_in, 16)
            sp.dma_start(wq_s[:, :], wq).then_inc(w_in, 16)
            sp.dma_start(bk_s[:, :], bk.rearrange("(d a) -> d a", a=1)).then_inc(w_in, 16)
            sp.dma_start(bq_s[:, :], bq.rearrange("(d a) -> d a", a=1)).then_inc(w_in, 16)
            for c in range(1, NC):
                load_ctx(0, c)
            sp.dma_start(wv_s[:, :], wv).then_inc(wv_in, 16)
            sp.dma_start(bv_s[:, :], bv.partition_broadcast(P)).then_inc(wv_in, 16)
            zeros, ones = fill[0:1, :], fill[1:2, :]
            sp.dma_start(qaug[48:AUG, :, :, :].rearrange("p h b q -> p (h b q)"),
                         zeros.broadcast_to([AUG - 48, GH * S2])).then_inc(qfill_in, 16)

            def fill_k(i):
                sp.dma_start(kaug[i][48:64, :, :].rearrange("p h n -> p (h n)"),
                             zeros.broadcast_to([16, GH * S2])).then_inc(kfill_in[i], 16)
                sp.dma_start(kaug[i][64:AUG, :, :].rearrange("p h n -> p (h n)"),
                             ones.broadcast_to([AUG - 64, GH * S2])).then_inc(kfill_in[i], 16)

            fill_k(0)
            sp.dma_start(mask_s[:, :], mask[0]).then_inc(mask_in, 16)

            def stack_q():
                for c, (qi, _) in enumerate(PAIRS):
                    sp.dma_start(qaug[8 * c:8 * c + 8, :, :, :].rearrange("d h b q -> d h (b q)"),
                                 q_dram[qi].rearrange("(h d) n -> d h n", d=DH)).then_inc(qaug_in, 16)

            def store_k(b, c):
                cols = slice(512 * c, 512 * c + 512)
                if b == 0 and c == 2:
                    sp.wait_ge(k_parts_made_pool, 1)
                else:
                    sp.wait_ge(k_parts_made, NC * b + c + (0 if b or c > 2 else 1))
                sp.dma_start(k_dram[b].rearrange("i p n -> p i n")[:, :, cols], kparts[:, :, cols]).then_inc(
                    kfirst_stored if b == 0 and c < 2 else k_stored, 16)

            def stack_keys(u, cols, signal):
                b, g = divmod(u, GROUPS)
                for c, (_, ki) in enumerate(PAIRS):
                    sp.dma_start(kaug[u % 3][8 * c:8 * c + 8, :, cols],
                                 k_dram[b, ki, 32 * g:32 * g + 32, cols].rearrange("(h d) n -> d h n", d=DH)).then_inc(signal, 16)

            def stack_k(u):
                b, g = divmod(u, GROUPS)
                if g == 0:
                    for c in range(NC):
                        store_k(b, c)
                    sp.wait_ge(k_stored, 16 * (NC * (b + 1) - 2))
                if u >= 3:
                    sp.wait_ge(score_made, 2 * STEPS * (u - 2))
                stack_keys(u, slice(0, S2), kaug_in[u % 3])

            def load_weights():
                sp.wait_ge(pv_done, (B - 1) * GROUPS * STEPS)
                for dst, src in ((wqk_l[:, 0:P], gWq), (wqk_l[:, P:2 * P], gWk), (wvg_l[:, 0:DV], gWv), (wvg_l[:, DV:], gWg),
                                 (wo_l, gWo.rearrange("(a p) n -> p a n", p=P)), (w1_l, gw1), (w2_l, gw2),
                                 (b_l, gb.rearrange("(d a) -> d a", a=1)), (rms_l, grms.partition_broadcast(P)),
                                 (rw_s, rw), (rb_s, rb.partition_broadcast(P))):
                    sp.dma_start(dst, src).then_inc(l_in, 16)

            sp.wait_ge(q_parts_made, 1)
            sp.dma_start(q_dram.rearrange("i p n -> p i n"), qparts[:, :, :]).then_inc(q_stored, 16)
            store_k(0, 0)
            store_k(0, 1)
            sp.wait_ge(q_stored, 16)
            stack_q()
            store_k(0, 3)
            store_k(0, 2)
            sp.wait_ge(kfirst_stored, 32)
            stack_keys(0, slice(0, S2 // 2), kfirst_in)
            sp.dma_start(f_s[:, :], fside[0]).then_inc(f_in, 16)
            sp.wait_ge(k_stored, 32)
            stack_keys(0, slice(S2 // 2, S2), kaug_in[0])
            sp.dma_start(bo_s[:, :], bo.partition_broadcast(P)).then_inc(bo_in, 16)
            fill_k(1)
            stack_k(1)
            for g in range(GROUPS):
                sp.dma_start(wo_s[32 * g:32 * g + 32, :, :], wo.rearrange("(g r) n -> r g n", r=32)).then_inc(wo_in, 16)
            fill_k(2)
            sp.dma_start(cst[:, :], shape_consts).then_inc(cst_in, 16)
            for u in range(1, UNITS):
                b, g = divmod(u, GROUPS)
                if g == 1 and b + 1 < B:
                    sp.wait_ge(work_filled, slot[("ctxT", b, NC - 1)] + 1)
                    for c in range(NC):
                        load_ctx(b + 1, c)
                    sp.wait_ge(neg_made, b + 1)
                    sp.dma_start(mask_s[:, :], mask[b + 1]).then_inc(mask_in, 16)
                if g == 0:
                    sp.wait_ge(k_parts_made, NC * (b + 1) - 1)
                    sp.dma_start(f_s[:, :], fside[b]).then_inc(f_in, 16)
                if u == UNITS - 1:
                    load_weights()
                if u > 1:
                    stack_k(u)
            sp.wait_ge(neg_made, B)
            sp.dma_start(eWo_s, eWo.rearrange("e (a p) d -> p e a d", p=P)).then_inc(e_in, 16)
            sp.wait_ge(work_filled, slot[("gT", B - 1, NC - 1)] + 1)
            sp.dma_start(eW_s, eW.rearrange("e d f -> d e f")).then_inc(e_in, 16)
            sp.dma_start(eV_s, eV.rearrange("e d f -> d e f")).then_inc(e_in, 16)
            for b in range(B):
                sp.wait_ge(batch_done, b + 1)
                sp.dma_start(out[b], x1[:, b, :]).then_inc(out_done, 16)
            sp.wait_ge(out_done, 16 * B)

        @block.tensor
        def _(pe):
            T = nc.tensor

            def transposes(w, src):
                await_bank(pe, w)
                for j in range(4):
                    last = T.transpose(bank_of(w)[:, P * j:P * j + P], src(j), identf[:, :])
                last.then_inc(work_filled, 1)

            def do_work(w):
                kind, a, c = w
                bank = bank_of(w)
                if kind == "xhT":
                    pe.wait_ge(pool_chain, 2)
                    pe.wait_ge(xh_made, 1)
                    transposes(w, lambda j: xh[:, j, :])
                elif kind == "ctxT":
                    pe.wait_ge(ctx_in[c], 16 * (a + 1))
                    transposes(w, lambda j: ctx_s[:, 4 * c + j, :])
                elif kind == "gT":
                    pe.wait_ge(f_in, 16 * (a + 1))
                    transposes(w, lambda j: f_s[:, 512 * c + P * j:512 * c + P * j + P])
                elif kind == "q":
                    pe.wait_ge(w_in, 64)
                    await_bank(pe, w)
                    pe.wait_ge(work_read_act, reads_before[("xhT", 0, 0)][1])
                    T.matmul(bank[:, :], wq_s[:, :], xhT[:, :], start=True, stop=True).then_inc(work_filled, 1)
                elif kind == "k":
                    await_bank(pe, w)
                    pe.wait_ge(work_read_act, reads_before[("ctxT", a, c)][1])
                    T.matmul(bank[:, :], wk_s[:, :], ctxT[:, 512 * c:512 * c + 512], start=True, stop=True).then_inc(work_filled, 1)
                elif kind == "v":
                    if a == 0 and c == 0:
                        pe.wait_ge(wv_in, 32)
                    await_bank(pe, w)
                    for j in range(4):
                        o = 512 * c + P * j
                        last = T.matmul(bank[:, P * j:P * j + P], ctxT[:, o:o + P], wv_s[:, :], start=True, stop=True)
                    last.then_inc(work_filled, 1)
                elif kind == "max":
                    u, h = divmod(a, GH)
                    b, g = divmod(u, GROUPS)
                    if c == 0 and a == 0:
                        pe.wait_ge(qaug_in, 16 * len(PAIRS))
                        pe.wait_ge(qfill_in, 16)
                        pe.wait_ge(kfirst_in, 16 * len(PAIRS))
                    if h == 0 and c == 0:
                        pe.wait_ge(kfill_in[u % 3], 32)
                    if h == 0 and c == (2 if u == 0 else 0):
                        pe.wait_ge(kaug_in[u % 3], 16 * len(PAIRS) * (u // 3 + 1))
                    await_bank(pe, w)
                    T.matmul(bank[:, :], qaug[0:ZROW + 1, GH * g + h, b, :],
                             kaug[u % 3][0:ZROW + 1, h, 512 * c:512 * c + 512], start=True, stop=True).then_inc(work_filled, 1)
                elif kind == "mrow":
                    await_bank(pe, w)
                    pe.wait_ge(mpart_made, a + 1)
                    for h in range(GH):
                        last = T.matmul(bank[ZROW:AUG, P * h:P * h + P], mpart[:, h, :], identb, start=True, stop=True,
                                        tile_position=(0, ZROW))
                    last.then_inc(work_filled, 1)
                elif kind == "den":
                    await_bank(pe, w)
                    pe.wait_ge(denom_made, a + 1)
                    for h in range(GH):
                        last = T.matmul(bank[:, h:h + 1], denom[:, h, :], quadsel[:, :], start=True, stop=True)
                    last.then_inc(work_filled, 1)
                elif kind == "lT":
                    pe.wait_ge(xh_made, a + 2)
                    await_bank(pe, w)
                    for b in range(*LGROUPS[a]):
                        o = P * (b - LGROUPS[a][0])
                        last = T.transpose(bank[:, o:o + P], xh[:, b, :], identf[:, :])
                    last.then_inc(work_filled, 1)
                elif kind in ("l1", "l2", "lq", "lk"):
                    pe.wait_ge(l_in, 16 * 11)
                    await_bank(pe, w)
                    await_act(pe, ("l1" if kind == "l2" else "lT", a, 0))
                    n = P * (LGROUPS[a][1] - LGROUPS[a][0])
                    left = {"l1": w1_l, "l2": w2_l, "lq": wqk_l[:, 0:P], "lk": wqk_l[:, P:2 * P]}[kind]
                    T.matmul(bank[0:LR, 0:n] if kind == "l1" else bank[:, 0:n], left,
                             lowT[:, 0:n] if kind == "l2" else xhT[:, columns(a)], start=True, stop=True).then_inc(work_filled, 1)
                elif kind == "lv":
                    await_bank(pe, w)
                    T.matmul(bank[:, :], xhT[:, P * c:P * c + P], wvg_l, start=True, stop=True).then_inc(work_filled, 1)
                elif kind == "wo":
                    g = a % GROUPS
                    if a == 0:
                        pe.wait_ge(wo_in, 64)
                    await_bank(pe, w)
                    pe.wait_ge(numer_made, a + 1)
                    for h in range(GH):
                        last = T.matmul(bank[:, P * h:P * h + P], numer[:, h, :], wo_s[:, g, :], start=True, stop=True)
                    last.then_inc(work_filled, 1)

            def scores(t, half):
                u, s = divmod(t, STEPS)
                b, g = divmod(u, GROUPS)
                e = 2 * t + half
                maxima = tick_max(t, half)
                for w in maxima[:1]:
                    do_work(w)
                if e >= 2:
                    pe.wait_ge(exp_made, e - 1)
                if t == 0 and half == 0:
                    for bank_no in range(4):
                        await_read(pe, start_holders[bank_no])
                if s == 0 and half == 0:
                    pe.wait_ge(work_read_act, reads_before[("mrow", u, 0)][1])
                    pe.wait_ge(neg_made, b + 1)
                for j in range(2):
                    kt = KT_TICK * s + 2 * half + j
                    T.matmul(score[half][:, j, :], neg[b % 2][:, P * kt:P * kt + P],
                             negident[:, :, :].rearrange("p h q -> p (h q)"), start=True, stop=False)
                    for h in range(GH):
                        last = T.matmul(score[half][:, j, P * h:P * h + P], kaug[u % 3][:, h, P * kt:P * kt + P],
                                        qaug[:, GH * g + h, b, :], start=False, stop=(h == GH - 1))
                    if j == 0:
                        for w in maxima[1:]:
                            do_work(w)
                last.then_inc(score_made, 1)

            def weights_sum(t):
                u, s = divmod(t, STEPS)
                b, g = divmod(u, GROUPS)
                pe.wait_ge(exp_made, 2 * t + 2)
                if s == 0 and u >= 1:
                    pe.wait_ge(denom_made, u)
                for j in range(KT_TICK):
                    last = T.matmul(den_ps[32 * j:32 * j + 32, :], ones32[:, :], prob[t % 2][:, j, :],
                                    start=(s == 0), stop=(s == STEPS - 1), tile_position=(0, 32 * j))
                last.then_inc(weights_summed, 1)

            def values(t):
                u, s = divmod(t, STEPS)
                b, g = divmod(u, GROUPS)
                pe.wait_ge(gated_pool, 2 * t + 2)
                pe.wait_ge(gated_dve, 2 * t + 2)
                if s == 0:
                    pe.wait_ge(work_read_dve, reads_before[("v", b, NC - 1)][1])
                    if u >= 1:
                        pe.wait_ge(numer_made, u)
                for j in range(KT_TICK):
                    last = T.matmul(num_ps[32 * j:32 * j + 32, :], v_s[b % 2][:, KT_TICK * s + j, 32 * g:32 * g + 32],
                                    probg[t % 2][:, j, :], start=(s == 0), stop=(s == STEPS - 1), tile_position=(0, 32 * j))
                last.then_inc(pv_done, 1)

            for w in start_work:
                do_work(w)
            for t in range(TICKS):
                scores(t, 0)
                for w in tick_work(t, 0):
                    do_work(w)
                if t >= 1:
                    weights_sum(t - 1)
                scores(t, 1)
                for w in tick_work(t, 1):
                    do_work(w)
                if t >= 1:
                    values(t - 1)
            weights_sum(TICKS - 1)
            values(TICKS - 1)
            do_work(("den", UNITS - 1, 0))
            do_work(("wo", UNITS - 1, 0))

            def inner(b, left, right, at, j, n):
                for m in range(4):
                    out_ = banks[32 * m:32 * m + 32, inner_bank[b], 0:LH * PICKS].rearrange(
                        "p (h j) -> p h j", j=PICKS)[:, :, j:j + n]
                    last = T.matmul(out_, left[:, P * b + 32 * m:P * b + 32 * m + 32],
                                    right[:, :, n * (4 * at + m):n * (4 * at + m) + n], start=True, stop=True,
                                    tile_position=(0, 32 * m))
                return last

            def diagonal(g):
                pe.wait_ge(qheads_made, g + 1)
                await_act(pe, ("lk", g, 0))
                for b in range(*LGROUPS[g]):
                    inner(b, kT, qheads, b, PICKS - 32, 32)

            def level_products(g, k):
                l = LEVEL_ORDER[k]
                pe.wait_ge(scaled_made, NLEVEL * g + k + 1)
                for b in range(*LGROUPS[g]):
                    o, at = P * b, b - LGROUPS[g][0]
                    if l >= 2:
                        last = inner(b, expo[l], later[g][l], at, 16 * (l - 2), 16)
                    elif l == 1:
                        for m in (0, 1):
                            last = T.matmul(banks[64 * m:64 * m + 32, outer_bank[b], 0:P],
                                            expo[1][:, o + 64 * m:o + 64 * m + 32],
                                            later[g][1][:, :, 64 * at + 32 * m:64 * at + 32 * m + 32],
                                            start=True, stop=True, tile_position=(0, 64 * m))
                    else:
                        last = T.matmul(banks[0:64, outer_bank[b], P:3 * P], expo[0][:, o:o + 64],
                                        later[g][0][:, :, 64 * at:64 * at + 64], start=True, stop=True, tile_position=(0, 0))
                last.then_inc(pairs_made, 1)

            def mix(g):
                for b in range(*LGROUPS[g]):
                    pe.wait_ge(off_read, b + 1)
                    for h in range(LH):
                        last = T.matmul(banks[:, outer_bank[b], HV * h:HV * h + HV], attT[:, LH * b + h, :],
                                        val[:, b, HV * h:HV * h + HV], start=True, stop=True)
                    last.then_inc(mixed_made, 1)

            def transpose_mixed(b):
                g = 0 if b < LGROUPS[1][0] else 1
                pe.wait_ge(gated_made, b + 1)
                for a in range(2):
                    last = T.transpose(banks[:, outer_bank[b], DV + P * a:DV + P * a + P],
                                       mixed[g][:, b - LGROUPS[g][0], P * a:P * a + P], identf[:, :])
                last.then_inc(mixT_made, 1)

            def linear_out(b):
                pe.wait_ge(mixT_read, b + 1)
                for a in range(2):
                    last = T.matmul(banks[:, inner_bank[b], 0:P], mixedT[:, a, P * b:P * b + P], wo_l[:, a, :],
                                    start=(a == 0), stop=(a == 1))
                last.then_inc(l_out, 1)

            pe.wait_ge(exp_made, 2 * TICKS)
            diagonal(0)
            for k in range(4):
                level_products(0, k)
            for w in end_work[2:7]:
                do_work(w)
            for k in range(4, NLEVEL):
                level_products(0, k)
            do_work(("lv", 1, B - 1))
            await_act(pe, ("lv", 1, B - 1))
            diagonal(1)
            for k in range(NLEVEL):
                level_products(1, k)
            mix(0)
            mix(1)
            transpose_mixed(0)
            for b in range(1, B):
                transpose_mixed(b)
                linear_out(b - 1)
            linear_out(B - 1)

            for g in range(2):
                pe.wait_ge(xh_made, 4 + g)
                for b in range(*LGROUPS[g]):
                    last = T.transpose(banks[:, g, P * b:P * b + P], xh[:, b, :], identf[:, :])
                last.then_inc(features_made, 1)
            pe.wait_ge(features_read, 2)
            for b in range(B):
                last = T.matmul(banks[:, 7, E * b:E * b + E], xhT[:, P * b:P * b + P], rw_s, start=True, stop=True)
            last.then_inc(logits_made, 1)
            pe.wait_ge(e_in, 48)

            def up(i):
                e, a = divmod(i, 2)
                if i >= 3:
                    pe.wait_ge(hid_made, i - 2)
                T.matmul(banks[:, 2 * (i % 3) + 1, :], eV_s[:, e, P * a:P * a + P], xhT[:, :], start=True, stop=True).then_inc(gate_up_made, 1)
                T.matmul(banks[:, 2 * (i % 3), :], eW_s[:, e, P * a:P * a + P], xhT[:, :], start=True, stop=True).then_inc(up_made, 1)

            def down(e):
                pe.wait_ge(hid_made, 2 * e + 2)
                if e >= 2:
                    pe.wait_ge(expert_added, e - 1)
                if e == 1:
                    pe.wait_ge(rank_read, 1)
                for b in range(B):
                    for a in range(2):
                        last = T.matmul(banks[:, 6 + e % 2, P * b:P * b + P], hidT[(2 * e + a) % 4][:, P * b:P * b + P],
                                        eWo_s[:, e, a, :], start=(a == 0), stop=(a == 1))
                last.then_inc(down_made, 1)

            for i in range(2 * E):
                if i == 2:
                    pe.wait_ge(chosen_made, 1)
                    counts = banks[:, 7, 0:B * E]
                    T.matmul(counts, upto, chosen.rearrange("p b e -> p (b e)"), start=True, stop=False)
                    T.matmul(counts, ones_sq[:, :], chosen_before.rearrange("p b e -> p (b e)"),
                             start=False, stop=True).then_inc(rank_made, 1)
                up(i)
                if i >= 3 and i % 2:
                    down(i // 2 - 1)
            down(E - 1)

        @block.scalar
        def _(act):
            A = nc.scalar
            chain = [0]

            def link(ins):
                chain[0] += 1
                ins.then_inc(act_chain, 1)
                act.wait_ge(act_chain, chain[0])

            def read_work(w):
                kind, a, c = w
                bank = bank_of(w)
                if kind == "q":
                    act.wait_ge(w_in, 64)
                    link(A.activation(bqs[:, :], bq_s[:, :], ACT.Copy, scale=SCALE))
                await_filled(act, w)
                if kind == "xhT":
                    A.copy(xhT[:, :], bank[:, :]).then_inc(work_read_act, 1)
                elif kind == "ctxT":
                    if a >= 1 and c == 0:
                        act.wait_ge(work_filled, slot[("v", a - 1, NC - 1)] + 1)
                    A.copy(ctxT[:, 512 * c:512 * c + 512], bank[:, :]).then_inc(work_read_act, 1)
                elif kind == "gT":
                    A.copy(gT[a % 2][:, 4 * c:4 * c + 4, :].rearrange("p t q -> p (t q)"), bank[:, :]).then_inc(work_read_act, 1)
                elif kind == "q":
                    A.activation(qf, bank[:, :], ACT.Identity, bias=bqs[:, :], scale=SCALE)
                    A.activation(qpart[0], bank[:, :], ACT.Identity, bias=bqs[:, :], scale=SCALE).then_inc(work_read_act, 1)
                elif kind == "k":
                    if a >= 1 and c == 0:
                        act.wait_ge(work_filled, slot[("gT", a - 1, NC - 1)] + 1)
                        act.wait_ge(kfirst_stored, 32)
                        act.wait_ge(k_stored, 16 * (NC * a - 2))
                    o = 512 * c
                    A.activation(kf(a, slice(o, o + 512)), bank[:, :], ACT.Identity, bias=bk_s[:, :])
                    A.activation(kpart[0][:, o:o + 512], bank[:, :], ACT.Identity, bias=bk_s[:, :]).then_inc(work_read_act, 1)
                elif kind == "wo":
                    act.wait_ge(work_read_dve, reads_before[("den", a, 0)][1])
                    if a >= 1:
                        act.wait_ge(unit_added, a)
                    for h in range(GH):
                        last = A.activation(head_out[:, h, :], bank[:, P * h:P * h + P], ACT.Copy, scale=rden[:, h:h + 1])
                    last.then_inc(work_read_act, 1)
                elif kind in ("lT", "l1", "lq", "lk", "l2"):
                    cols = columns(a)
                    n = cols.stop - cols.start
                    if kind == "lT":
                        last = A.copy(xhT[:, cols], bank[:, 0:n])
                    elif kind == "l1":
                        last = A.copy(lowT[:, 0:n], bank[0:LR, 0:n])
                    elif kind == "lq":
                        last = A.activation(qT[:, cols], bank[:, 0:n], ACT.Copy, scale=float(HK) ** -0.5)
                    elif kind == "lk":
                        last = A.copy(kT[:, cols], bank[:, 0:n])
                    else:
                        last = A.activation(decay[:, cols], bank[:, 0:n], ACT.Identity, bias=b_l)
                    last.then_inc(work_read_act, 1)
                elif kind == "lv":
                    A.copy(val[:, c, :], bank[:, 0:DV])
                    A.copy(zgate[:, c, :], bank[:, DV:2 * DV]).then_inc(work_read_act, 1)
                elif kind == "mrow":
                    b, g = divmod(a, GROUPS)
                    A.copy(qaug[ZROW:AUG, GH * g:GH * g + GH, b, :], bank[ZROW:AUG, :].rearrange(
                        "p (h q) -> p h q", h=GH)).then_inc(work_read_act, 1)

            def exps(t, half):
                act.wait_ge(score_made, 2 * t + half + 1)
                if half == 0 and t >= 2:
                    act.wait_ge(pv_done, t - 1)
                A.activation(prob[t % 2][:, 2 * half:2 * half + 2, :], score[half][:, :, :], ACT.Exp).then_inc(exp_made, 1)

            def denominators(u):
                act.wait_ge(weights_summed, STEPS * (u + 1))
                if u >= 1:
                    act.wait_ge(work_filled, slot[("den", u - 1, 0)] + 1)
                A.copy(denom[:, :, :].rearrange("p h q -> p (h q)"), den_ps[:, :]).then_inc(denom_made, 1)

            def soft_part(g):
                cols = columns(g)
                await_act(act, ("l2", g, 0))
                link(A.activation(lnexp[:, cols], decay[:, cols], ACT.Abs))
                link(A.activation(lnexp[:, cols], lnexp[:, cols], ACT.Exp, scale=-1.0))
                A.activation(lnexp[:, cols], lnexp[:, cols], ACT.Ln, bias=1.0).then_inc(soft_made, 1)

            def level_weights(g, k):
                act.wait_ge(expo_made, NLEVEL * g + k + 1)
                x_ = expo[LEVEL_ORDER[k]][:, columns(g)]
                A.activation(x_, x_, ACT.Exp, scale=1.0 / 16.0).then_inc(decayed, 1)

            def spread_heads(g):
                act.wait_ge(cst_in, 16)
                await_act(act, ("lq", g, 0))
                for h in range(LH):
                    last = A.activation(qheads[:, h, columns(g)], qT[:, columns(g)], ACT.Copy, scale=blocksel[:, h, 0:1])
                last.then_inc(qheads_made, 1)

            def gate_tanh(g):
                await_act(act, ("lv", g, LGROUPS[g][1] - 1))
                bs = slice(*LGROUPS[g])
                A.activation(ztanh[:, bs, :], zgate[:, bs, :], ACT.Tanh, scale=0.5).then_inc(ztanh_made, 1)

            def outer_levels(g):
                act.wait_ge(pairs_made, NLEVEL * (g + 1))
                for b in range(*LGROUPS[g]):
                    act.wait_ge(att_made[g], b - LGROUPS[g][0] + 1)
                    rows, bank = slice(LH * b, LH * b + LH), banks[:, outer_bank[b], :]
                    A.copy(attT[0:64, rows, 64:128], bank[0:64, P:3 * P].rearrange("p (h t) -> p h t", h=LH))
                    A.copy(attT[0:32, rows, 32:64], bank[0:32, 0:P].rearrange("p (h t) -> p h t", h=LH))
                    A.copy(attT[64:96, rows, 96:128], bank[64:96, 0:P].rearrange("p (h t) -> p h t", h=LH)).then_inc(off_read, 1)

            def square(g):
                for b in range(*LGROUPS[g]):
                    act.wait_ge(mixed_made, b + 1)
                    last = A.activation(squares[g][:, b - LGROUPS[g][0], :], banks[:, outer_bank[b], 0:DV], ACT.Square)
                last.then_inc(squared, 1)

            def take_mixT(b):
                act.wait_ge(mixT_made, b + 1)
                A.copy(mixedT[:, :, P * b:P * b + P], banks[:, outer_bank[b], DV:2 * DV].rearrange(
                    "p (a n) -> p a n", a=2)).then_inc(mixT_read, 1)

            for w in start_work:
                if w[0] in BY_ACT:
                    read_work(w)
            for t in range(TICKS):
                exps(t, 0)
                for w in tick_work(t, 0):
                    if w[0] in BY_ACT:
                        read_work(w)
                if t - 2 in k_tick:
                    b, c = k_tick[t - 2]
                    act.wait_ge(k_rest_made, NC * (b - 1) + c + 1)
                    A.copy(kpart[1][:, 512 * c:512 * c + 512], kf(b, slice(512 * c, 512 * c + 512))).then_inc(k_middle_made, 1)
                exps(t, 1)
                for w in tick_work(t, 1):
                    if w[0] in BY_ACT:
                        read_work(w)
                if t >= 1 and t % STEPS == 0:
                    denominators(t // STEPS - 1)
                i = t - (B - 1) * GROUPS * STEPS
                if i == 9:
                    soft_part(0)
                if 12 <= i <= 15:
                    for k in range(2 * (i - 12), min(2 * (i - 11), NLEVEL)):
                        level_weights(0, k)
            act.wait_ge(pv_done, TICKS - 1)
            spread_heads(0)
            denominators(UNITS - 1)
            read_work(("wo", UNITS - 1, 0))

            act.wait_ge(pv_done, TICKS)
            gate_tanh(0)
            for w in end_work[2:7]:
                read_work(w)
            soft_part(1)
            spread_heads(1)
            for k in range(NLEVEL):
                level_weights(1, k)
            read_work(("lv", 1, B - 1))
            gate_tanh(1)
            outer_levels(0)
            square(0)
            outer_levels(1)
            square(1)
            for b in range(B):
                take_mixT(b)
            for g in range(2):
                act.wait_ge(features_made, g + 1)
                A.copy(xhT[:, columns(g)], banks[:, g, columns(g)]).then_inc(features_read, 1)
            for i in range(2 * E):
                if i == 1:
                    act.wait_ge(ratio_in, 1)
                    A.activation(ratio, ratio, ACT.Exp).then_inc(ratio_made, 1)
                act.wait_ge(gate_up_made, i + 1)
                if i >= 2:
                    act.wait_ge(hid_made, i - 1)
                A.activation(tanhs[i % 2], banks[:, 2 * (i % 3) + 1, :], ACT.Tanh, scale=0.5).then_inc(tanh_made, 1)

        @block.vector
        def _(dve):
            V = nc.vector
            chain = [0]

            def link(ins):
                chain[0] += 1
                ins.then_inc(dve_chain, 1)
                dve.wait_ge(dve_chain, chain[0])

            def norm_stats(bs):
                for b in range(*bs):
                    last = V.bn_stats(bnst[:, b, :], x1[:, b, :])
                link(last)
                for b in range(*bs):
                    last = V.bn_aggr(mv[:, b, :], bnst[:, b, :])
                last.then_inc(stats_made, 1)

            def norm_apply(k, bs):
                dve.wait_ge(rstd_made, k + 1)
                for b in range(*bs):
                    last = V.tensor_scalar(xh[:, b, :], x1[:, b, :], mv[:, b, 0:1], rstd[:, b:b + 1], ALU.subtract, ALU.mult)
                last.then_inc(xh_made, 1)

            def gate(t, half):
                u, s = divmod(t, STEPS)
                b = u // GROUPS
                dve.wait_ge(exp_made, 2 * t + half + 1)
                if half == 0:
                    if t >= 2:
                        dve.wait_ge(pv_done, t - 1)
                    if t % (GROUPS * STEPS) == 0:
                        dve.wait_ge(work_read_act, reads_before[("gT", b, NC - 1)][1])
                j = 2 * half + 1
                V.tensor_tensor(probg[t % 2][:, j, :].rearrange("p (h q) -> p h q", h=GH),
                                prob[t % 2][:, j, :].rearrange("p (h q) -> p h q", h=GH),
                                gT[b % 2][:, KT_TICK * s + j, :].unsqueeze(1).broadcast_to([P, GH, P]),
                                ALU.mult).then_inc(gated_dve, 1)

            def row_max(w):
                _, n, c = w
                u, h = divmod(n, GH)
                b = u // GROUPS
                if c == 0 and u % GROUPS == 0 and h == 0:
                    dve.wait_ge(neg_made, b + 1)
                await_filled(dve, w)
                if reads_before[w][1] > 2:
                    dve.wait_ge(work_read_dve, reads_before[w][1] - 2)
                V.tensor_tensor_reduce(out=junk[:, c % 2, :], in0=bank_of(w)[:, :], in1=neg[b % 2][:, 512 * c:512 * c + 512],
                                       scale=1.0, scalar=LOWEST, op0=ALU.add, op1=ALU.max,
                                       accum_out=mx[:, u % 2, h, c:c + 1]).then_inc(work_read_dve, 1)

            def split_max(u):
                dve.wait_ge(work_read_dve, reads_before[("max", GH * u + GH - 1, NC - 1)][1])
                if u >= 1:
                    dve.wait_ge(work_filled, slot[("mrow", u - 1, 0)] + 1)
                link(V.reduce_max(mtop[:, :], mx[:, u % 2, :, :], AX_X))
                link(V.tensor_scalar(mpart[:, :, 1], mtop[:, :], -1.0, None, ALU.mult))
                link(V.scalar_tensor_tensor(mres[:, :], mtop[:, :], -1.0, mpart[:, :, 1], ALU.mult, ALU.subtract))
                link(V.tensor_copy(mpart[:, :, 2], mres[:, :]))
                V.tensor_tensor(mpart[:, :, 3], mres[:, :], mpart[:, :, 2], ALU.subtract).then_inc(mpart_made, 1)

            def value_bias(w):
                _, b, c = w
                await_filled(dve, w)
                if c == 0 and b >= 2:
                    dve.wait_ge(pv_done, GROUPS * STEPS * (b - 1))
                V.tensor_tensor(v_s[b % 2][:, 4 * c:4 * c + 4, :], bank_of(w)[:, :].rearrange("p (t d) -> p t d", t=4),
                                bv_s[:, :].unsqueeze(1).broadcast_to([P, 4, D]), ALU.add).then_inc(work_read_dve, 1)

            def numerators(u):
                dve.wait_ge(pv_done, STEPS * (u + 1))
                if u >= 1:
                    dve.wait_ge(work_filled, slot[("wo", u - 1, 0)] + 1)
                V.tensor_tensor(numer[:, :, :], num_ps[:, :].rearrange("p (h q) -> p h q", h=GH),
                                headsel[:, :].unsqueeze(2).broadcast_to([P, GH, P]), ALU.mult).then_inc(numer_made, 1)

            def finish_den(w):
                await_filled(dve, w)
                if w[1] >= 1:
                    dve.wait_ge(work_read_act, reads_before[("wo", w[1] - 1, 0)][1])
                ins = V.reciprocal(rden[:, :], bank_of(w)[:, 0:GH])
                ins.then_inc(work_read_dve, 1)

            def read_work(w):
                {"max": row_max, "v": value_bias, "den": finish_den}[w[0]](w)

            V.memset(mpart[:, :, :], 0.0)
            V.memset(ones32[:, :], 1.0)
            V.memset(halfneg[:, :], -0.5)
            link(V.memset(ones_sq[:, :], 1.0))
            dve.wait_ge(x_in, 16)
            norm_stats((0, B))
            norm_apply(0, (0, B))
            dve.wait_ge(work_read_act, reads_before[("q", 0, 0)][1])
            link(V.tensor_tensor(qf, qf, qpart[0], ALU.subtract))
            link(V.tensor_copy(qpart[1], qf))
            V.tensor_tensor(qpart[2], qf, qpart[1], ALU.subtract).then_inc(q_parts_made, 1)
            for c in (0, 1, 3):
                cols = slice(512 * c, 512 * c + 512)
                dve.wait_ge(work_read_act, reads_before[("k", 0, c)][1])
                link(V.tensor_tensor(kf(0, cols), kf(0, cols), kpart[0][:, cols], ALU.subtract))
                link(V.tensor_copy(kpart[1][:, cols], kf(0, cols)))
                V.tensor_tensor(kpart[2][:, cols], kf(0, cols), kpart[1][:, cols], ALU.subtract).then_inc(k_parts_made, 1)
            for w in start_work:
                if w[0] not in BY_ACT:
                    read_work(w)
                    if w == ("max", GH - 1, NC - 1):
                        split_max(0)
            def parts_of(a, c):
                return a.rearrange("p (n two c) -> p n two c", two=2, c=c)

            def decay_sums(g):
                cols = columns(g)
                dve.wait_ge(soft_made, g + 1)
                link(V.scalar_tensor_tensor(decay[:, cols], decay[:, cols], 0.0, lnexp[:, cols], ALU.min, ALU.subtract))
                for b in range(*LGROUPS[g]):
                    last = V.tensor_tensor_scan(cum[:, P * b:P * b + P], ones_sq[:, :], decay[:, P * b:P * b + P], 0.0,
                                                ALU.mult, ALU.add)
                link(last)

            def exponents(g, k):
                l = LEVEL_ORDER[k]
                c = LEVELS[l]
                p_, x_ = parts_of(cum[:, columns(g)], c), parts_of(expo[l][:, columns(g)], c)
                border = p_[:, :, 0, c - 1:c].broadcast_to([P, p_.shape[1], c])
                V.tensor_tensor(x_[:, :, 1, :], p_[:, :, 1, :], border, ALU.subtract)
                V.tensor_tensor(x_[:, :, 0, :], border, p_[:, :, 0, :], ALU.subtract).then_inc(expo_made, 1)

            def scale_parts(g, k):
                l = LEVEL_ORDER[k]
                c = LEVELS[l]
                w_ = parts_of(expo[l][:, columns(g)], c)
                dve.wait_ge(decayed, NLEVEL * g + k + 1)
                if k == 0:
                    await_act(dve, ("lk", g, 0))
                    dve.wait_ge(qheads_made, g + 1)
                V.tensor_tensor(w_[:, :, 0, :], w_[:, :, 0, :], parts_of(kT[:, columns(g)], c)[:, :, 0, :], ALU.mult)
                V.tensor_tensor(later[g][l].rearrange("p h (n c) -> p h n c", c=c),
                                w_[:, :, 1, :].unsqueeze(1).broadcast_to([P, LH, w_.shape[1], c]),
                                qheads[:, :, columns(g)].rearrange("p h (n two c) -> p h n two c", two=2, c=c)[:, :, :, 1, :],
                                ALU.mult).then_inc(scaled_made, 1)

            def output_gate(g):
                bs = slice(*LGROUPS[g])
                dve.wait_ge(ztanh_made, g + 1)
                V.scalar_tensor_tensor(zgate[:, bs, :], ztanh[:, bs, :], 1.0, zgate[:, bs, :], ALU.add, ALU.mult).then_inc(zgate_made, 1)

            def pick_pairs(g):
                b0, b1 = LGROUPS[g]
                dve.wait_ge(cst_in, 16)
                dve.wait_ge(pairs_made, NLEVEL * (g + 1))
                for b in range(b0, b1):
                    last = V.tensor_tensor(picked[g][:, LH * (b - b0):LH * (b - b0) + LH, :],
                                           banks[:, inner_bank[b], 0:LH * PICKS].rearrange("p (h j) -> p h j", j=PICKS),
                                           levelsel.unsqueeze(1).broadcast_to([P, LH, PICKS]), ALU.mult)
                link(last)
                base = picked[g][:, :, PICKS - 32:PICKS]
                for l in range(2, NLEVEL):
                    c = LEVELS[l]
                    at = base.rearrange("p c (n two t) -> p c n two t", two=2, t=c)[:, :, :, 1, :]
                    V.tensor_tensor(at, at, picked[g][:, :, 16 * (l - 2):16 * (l - 1)].rearrange(
                        "p c (n t) -> p c n t", t=c), ALU.add).then_inc(picks_made, 1)
                    dve.wait_ge(picks_made, (NLEVEL - 2) * g + l - 1)

            def square_sums(g):
                cs = slice(LH * LGROUPS[g][0], LH * LGROUPS[g][1])
                dve.wait_ge(squared, g + 1)
                V.tensor_reduce(rms_sum[:, cs], squares[g].rearrange("p b (h v) -> p (b h) v", v=HV), AX_X, ALU.add).then_inc(sums_made, 1)

            def norm_and_gate(g):
                b0, b1 = LGROUPS[g]
                dve.wait_ge(rms_made, g + 1)
                for b in range(b0, b1):
                    last = V.tensor_tensor(mixed[g][:, b - b0, :].rearrange("p (h v) -> p h v", v=HV),
                                           banks[:, outer_bank[b], 0:DV].rearrange("p (h v) -> p h v", v=HV),
                                           rms_inv[:, LH * b:LH * b + LH].unsqueeze(2).broadcast_to([P, LH, HV]), ALU.mult)
                link(last)
                dve.wait_ge(zgate_scaled, g + 1)
                for b in range(b0, b1):
                    V.scalar_tensor_tensor(mixed[g][:, b - b0, :], mixed[g][:, b - b0, :], 0.5, zgate[:, b, :],
                                           ALU.mult, ALU.mult).then_inc(gated_made, 1)

            def add_linear(g):
                for b in range(*LGROUPS[g]):
                    dve.wait_ge(l_out, b + 1)
                    last = V.tensor_tensor(x1[:, b, :], x1[:, b, :], banks[:, inner_bank[b], 0:P], ALU.add)
                link(last)

            for t in range(TICKS):
                u, s = divmod(t, STEPS)
                for w in tick_max(t, 0):
                    read_work(w)
                if t >= 1:
                    gate(t - 1, 1)
                if s == 1 and u >= 1:
                    numerators(u - 1)
                for w in tick_work(t, 0):
                    if w[0] not in BY_ACT:
                        read_work(w)
                if s == STEPS - 2 and u + 1 < UNITS:
                    split_max(u + 1)
                for w in tick_max(t, 1):
                    read_work(w)
                gate(t, 0)
                for w in tick_work(t, 1):
                    if w[0] not in BY_ACT:
                        read_work(w)
                i = t - (B - 1) * GROUPS * STEPS
                if i == 4:
                    dve.wait_ge(unit_added, (B - 1) * GROUPS)
                    norm_stats(LGROUPS[0])
                if i == 5:
                    norm_apply(1, LGROUPS[0])
                if i == 10:
                    decay_sums(0)
                if 11 <= i <= 14:
                    for k in range(2 * (i - 11), min(2 * (i - 10), NLEVEL)):
                        exponents(0, k)
            gate(TICKS - 1, 1)
            numerators(UNITS - 1)
            scale_parts(0, 0)
            scale_parts(0, 1)
            read_work(("den", UNITS - 1, 0))

            scale_parts(0, 2)
            scale_parts(0, 3)
            dve.wait_ge(unit_added, UNITS)
            norm_stats(LGROUPS[1])
            scale_parts(0, 4)
            norm_apply(2, LGROUPS[1])
            scale_parts(0, 5)
            scale_parts(0, 6)
            output_gate(0)
            decay_sums(1)
            for k in range(NLEVEL):
                exponents(1, k)
            pick_pairs(0)
            for k in range(NLEVEL):
                scale_parts(1, k)
            output_gate(1)
            pick_pairs(1)
            spread_blocks(V, B - 1)
            square_sums(0)
            square_sums(1)
            norm_and_gate(0)
            norm_and_gate(1)
            add_linear(0)
            norm_stats(LGROUPS[0])
            add_linear(1)
            norm_stats(LGROUPS[1])
            for g in range(2):
                norm_apply(3 + g, LGROUPS[g])
            dve.wait_ge(logits_made, 1)
            link(V.tensor_tensor(logit, banks[:, 7, 0:B * E].rearrange("p (b e) -> p b e", e=E),
                                 rb_s.unsqueeze(1).broadcast_to([P, B, E]), ALU.add))
            for b in range(B):
                last = V.max(top[:, b, :], logit[:, b, :])
            link(last)
            for b in range(B):
                last = V.max_index(topno[:, b, :].bitcast(U32), top[:, b, :], logit[:, b, :])
            V.tensor_tensor(ratio, top[:, :, 1], top[:, :, 0], ALU.subtract).then_inc(ratio_in, 1)
            link(last)
            link(V.tensor_copy(topnof, topno.bitcast(U32)))
            for i in range(2):
                last = V.tensor_tensor(pick[i], expert_no.unsqueeze(1).broadcast_to([P, B, E]),
                                       topnof[:, :, i:i + 1].broadcast_to([P, B, E]), ALU.is_equal)
            link(last)
            link(V.tensor_tensor(chosen, pick[0], pick[1], ALU.add))
            V.memset(chosen_before[:, 0, :], 0.0)
            last = V.tensor_copy(chosen_before[:, 1, :], chosen[:, 0, :])
            for b in range(2, B):
                link(last)
                last = V.tensor_tensor(chosen_before[:, b, :], chosen_before[:, b - 1, :], chosen[:, b - 1, :], ALU.add)
            last.then_inc(chosen_made, 1)
            dve.wait_ge(ratio_made, 1)
            link(V.tensor_scalar(top_p[0], ratio, 1.0, None, ALU.add))
            link(V.reciprocal(top_p[0], top_p[0]))
            link(V.tensor_tensor(top_p[1], top_p[0], ratio, ALU.mult))
            for i in range(2):
                last = V.tensor_tensor(pick[i], pick[i], top_p[i].unsqueeze(2).broadcast_to([P, B, E]), ALU.mult)
            link(last)
            link(V.tensor_tensor(weight, pick[0], pick[1], ALU.add))

            def hidden(i):
                dve.wait_ge(tanh_made, i + 1)
                link(V.scalar_tensor_tensor(gated[i % 2], tanhs[i % 2], 1.0, banks[:, 2 * (i % 3) + 1, :], ALU.add, ALU.mult))
                if i >= 4:
                    dve.wait_ge(down_made, i // 2 - 1)
                dve.wait_ge(up_made, i + 1)
                V.tensor_tensor(hidT[i % 4], gated[i % 2], banks[:, 2 * (i % 3), :], ALU.mult).then_inc(hid_made, 1)

            def add_expert(e):
                dve.wait_ge(down_made, e + 1)
                if e >= 1:
                    dve.wait_ge(expert_added, e)
                for b in range(B):
                    last = V.scalar_tensor_tensor(x1[:, b, :], banks[:, 6 + e % 2, P * b:P * b + P], weight[:, b, e:e + 1],
                                                  x1[:, b, :], ALU.mult, ALU.add)
                    if e == E - 1:
                        last.then_inc(batch_done, 1)
                if e < E - 1:
                    last.then_inc(expert_added, 1)

            for i in range(2 * E):
                hidden(i)
                if i == 1:
                    dve.wait_ge(rank_made, 1)
                    V.tensor_scalar(chosen, banks[:, 7, 0:B * E].rearrange("p (b e) -> p b e", e=E), float(CAPACITY), 0.5,
                                    ALU.is_le, ALU.mult).then_inc(rank_read, 1)
                    dve.wait_ge(rank_read, 1)
                    link(V.tensor_tensor(weight, weight, chosen, ALU.mult))
                if i >= 3 and i % 2:
                    add_expert(i // 2 - 1)
            add_expert(E - 1)

        @block.gpsimd
        def _(pool):
            G = nc.gpsimd
            chain = [0]

            def link(ins):
                chain[0] += 1
                ins.then_inc(pool_chain, 1)
                pool.wait_ge(pool_chain, chain[0])

            def rsqrt(k, bs):
                r = rstd[:, bs[0]:bs[1]]
                pool.wait_ge(stats_made, k + 1)
                link(G.tensor_scalar(r, mv[:, bs[0]:bs[1], 1], EPS, None, ALU.add))
                G.tensor_tensor(r, r, halfneg[:, bs[0]:bs[1]], ALU.pow).then_inc(rstd_made, 1)

            def scale_gate(g):
                n = LH * (LGROUPS[g][1] - LGROUPS[g][0])
                z = zgate[:, slice(*LGROUPS[g]), :].rearrange("p b (h v) -> p (b h) v", v=HV)
                pool.wait_ge(zgate_made, g + 1)
                G.tensor_tensor(z, z, rms_l.unsqueeze(1).broadcast_to([P, n, HV]), ALU.mult).then_inc(zgate_scaled, 1)

            def head_rsqrt(g):
                cs = slice(LH * LGROUPS[g][0], LH * LGROUPS[g][1])
                pool.wait_ge(sums_made, g + 1)
                link(G.tensor_scalar(rms_inv[:, cs], rms_sum[:, cs], 1.0 / HV, EPS, ALU.mult, ALU.add))
                G.tensor_tensor(rms_inv[:, cs], rms_inv[:, cs], rms_half[:, cs], ALU.pow).then_inc(rms_made, 1)

            def mask_offset(b):
                pool.wait_ge(mask_in, 16 * (b + 1))
                if b >= 2:
                    pool.wait_ge(score_made, 2 * STEPS * GROUPS * (b - 1))
                G.tensor_scalar(neg[b % 2][:, :], mask_s[:, :], -NEG, NEG, ALU.mult, ALU.add).then_inc(neg_made, 1)

            def gate(t, half):
                u, s = divmod(t, STEPS)
                b = u // GROUPS
                pool.wait_ge(exp_made, 2 * t + half + 1)
                if half == 0:
                    if t >= 2:
                        pool.wait_ge(pv_done, t - 1)
                    if t % (GROUPS * STEPS) == 0:
                        pool.wait_ge(work_read_act, reads_before[("gT", b, NC - 1)][1])
                j = 2 * half
                G.tensor_tensor(probg[t % 2][:, j, :].rearrange("p (h q) -> p h q", h=GH),
                                prob[t % 2][:, j, :].rearrange("p (h q) -> p h q", h=GH),
                                gT[b % 2][:, KT_TICK * s + j, :].unsqueeze(1).broadcast_to([P, GH, P]),
                                ALU.mult).then_inc(gated_pool, 1)

            def split_k(b, c, step, signal=k_parts_made):
                cols = slice(512 * c, 512 * c + 512)
                if step == 0:
                    pool.wait_ge(work_read_act, reads_before[("k", b, c)][1])
                    rest = G.tensor_tensor(kf(b, cols), kf(b, cols), kpart[0][:, cols], ALU.subtract)
                    if b > 0:
                        rest.then_inc(k_rest_made, 1)
                    else:
                        link(rest)
                elif step == 1:
                    link(G.tensor_copy(kpart[1][:, cols], kf(b, cols)))
                else:
                    if b > 0:
                        pool.wait_ge(k_middle_made, NC * (b - 1) + c + 1)
                    G.tensor_tensor(kpart[2][:, cols], kf(b, cols), kpart[1][:, cols], ALU.subtract).then_inc(signal, 1)

            def add_unit(u):
                pool.wait_ge(work_read_act, reads_before[("wo", u, 0)][1])
                link(G.tensor_tensor(head_out[:, 0:2, :], head_out[:, 0:2, :], head_out[:, 2:4, :], ALU.add))
                link(G.tensor_tensor(head_out[:, 0, :], head_out[:, 0, :], head_out[:, 1, :], ALU.add))
                b = u // GROUPS
                if u >= 1:
                    pool.wait_ge(unit_added, u)
                G.tensor_tensor(x1[:, b, :], x1[:, b, :], head_out[:, 0, :], ALU.add).then_inc(unit_added, 1)

            link(G.memset(identf[:, :], 0.0))
            link(G.affine_select(out=identf[:, :], in_=identf[:, :], compare_op=ALU.not_equal, fill=1.0, base=0,
                                 pattern=[[-1, P]], channel_multiplier=1))
            pool.wait_ge(dve_chain, 1)
            rsqrt(0, (0, B))
            for h in range(GH):
                link(G.tensor_copy(negident[:, h, :], identf[:, :]))
            link(G.memset(headsel[:, :], 1.0))
            link(G.memset(quadsel[:, :], 0.0))
            for j in range(4):
                v = headsel[32 * j:32 * j + 32, :]
                link(G.affine_select(out=v, in_=v, compare_op=ALU.is_ge, fill=0.0, base=0, pattern=[[-8, GH]], channel_multiplier=1))
                link(G.affine_select(out=v, in_=v, compare_op=ALU.is_ge, fill=0.0, base=7, pattern=[[8, GH]], channel_multiplier=-1))
                link(G.memset(quadsel[32 * j:32 * j + 1, :], 1.0))
            for step in range(3):
                split_k(0, 2, step, k_parts_made_pool)
            mask_offset(0)
            pool.wait_ge(bo_in, 16)
            pool.wait_ge(xh_made, 1)
            link(G.tensor_tensor(x1[:, :, :], x1[:, :, :], bo_s[:, :].unsqueeze(1).broadcast_to([P, B, D]), ALU.add))
            for t in range(TICKS):
                b, i = divmod(t, GROUPS * STEPS)
                gate(t, 0)
                gate(t, 1)
                if b + 1 < B:
                    if i == 7:
                        mask_offset(b + 1)
                    if t - 1 in k_tick:
                        split_k(*k_tick[t - 1], 0)
                    if t - 2 in k_tick:
                        split_k(*k_tick[t - 2], 2)
                u, s = divmod(t, STEPS)
                if s == STEPS - 1 and u >= 1:
                    add_unit(u - 1)
                if t == (B - 1) * GROUPS * STEPS + 4:
                    rsqrt(1, LGROUPS[0])
            add_unit(UNITS - 1)
            rsqrt(2, LGROUPS[1])
            link(G.memset(rms_half, -0.5))
            scale_gate(0)
            pool.wait_ge(picks_made, NLEVEL - 2)
            for b in range(*LGROUPS[0]):
                spread_blocks(G, b)
            scale_gate(1)
            for g in range(2):
                head_rsqrt(g)
            for g in range(2):
                rsqrt(3 + g, LGROUPS[g])


_NAMES = ['x', 'ctx_1024', 'fside_BxSxS2_0', 'mask_BxSxS2_ik1', 'L0_xattn_wq_k', 'L0_xattn_wq_b', 'L0_xattn_wk_k',
          'L0_xattn_wk_b', 'L0_xattn_wv_k', 'L0_xattn_wv_b', 'L0_xattn_wo_k', 'L0_xattn_wo_b', 'L0_attn_Wq', 'L0_attn_Wk',
          'L0_attn_Wv', 'L0_attn_Wg', 'L0_attn_gk_w1', 'L0_attn_gk_w2', 'L0_attn_gk_b', 'L0_attn_Wo', 'L0_attn_rms_w',
          'L0_ffn_router_w', 'L0_ffn_router_b', 'L0_ffn_W', 'L0_ffn_V', 'L0_ffn_W_out']


def kernel(**inputs):
    import numpy as np
    import concourse.bacc as bacc
    from concourse.bass_utils import run_bass_kernel_spmd

    nc = bacc.Bacc("TRN2", target_bir_lowering=False, num_devices=1)
    arrays, args = {}, []
    for name in _NAMES:
        a = np.asarray(inputs[name])
        a = np.ascontiguousarray(a.T if name == "L0_ffn_router_w" else a)
        arrays["in_" + name] = a
        args.append(nc.dram_tensor("in_" + name, a.shape, mybir.dt.from_np(a.dtype), kind="ExternalInput").ap())
    s, t = np.arange(P)[:, None], np.arange(32)[None, :]
    def level(c):
        j = np.arange(16)[None, :]
        return s % 32 // c == 2 * (j // c)
    levels = [level(c) for c in LEVELS[2:]] + [s % 32 == t]
    blocks = np.arange(P)[:, None] // 32 == np.arange(P)[None, :] // 32
    upto = s <= np.arange(P)[None, :]
    arrays["shape_consts"] = np.concatenate([*levels, blocks, upto, np.tile(np.arange(8), (P, 1))], axis=1).astype(np.float32)
    args.append(nc.dram_tensor("shape_consts", (P, CONSTS), F32, kind="ExternalInput").ap())
    fill_rows = np.concatenate([np.zeros((1, GH * 2048)), np.ones((1, GH * 2048))]).astype(mybir.dt.np(BF16))
    arrays["fill_rows"] = fill_rows
    args.append(nc.dram_tensor("fill_rows", fill_rows.shape, BF16, kind="ExternalInput").ap())
    out = nc.dram_tensor("out_x", inputs["x"].shape, F32, kind="ExternalOutput").ap()
    perceiver_kernel(nc, *args, out)
    r = run_bass_kernel_spmd(nc, [arrays], core_ids=[0])
    return r.results[0]["out_x"]
```
